# Optimizing a Trainium2 kernel written in Bass

```python
import numpy as np
import jax
import jax.numpy as jnp

def _softmax(x, axis=-1):
    return jax.nn.softmax(x, axis=axis)

def _gelu(x):
    return jax.nn.gelu(x, approximate=True)

def _silu(x):
    return jax.nn.silu(x)

def _sigmoid(x):
    return jax.nn.sigmoid(x)

def _layernorm(x, axis=-1, eps=1e-05):
    m = jnp.mean(x, axis=axis, keepdims=True)
    v = jnp.var(x, axis=axis, keepdims=True)
    return (x - m) / jnp.sqrt(v + eps)

def _scatter_add(tgt, idx, src, axis=0):
    return tgt.at[idx].add(src)

def _segment_sum(src, seg, n):
    return jax.ops.segment_sum(src, seg, n)
kernel_name = 'mk_vit_tower_cls_d4_tok_img1024_r4_8cb123'

def setup_inputs(seed: int=0):
    np.random.seed(seed)
    _w = jnp.asarray

    def _rec_inputs():
        import jax
        import jax.numpy as jnp
        _rk = jax.random.key(seed)
        x = -0.00040386 + 0.999972 * jax.random.normal(jax.random.fold_in(_rk, 1), (32, 3, 64, 64), jnp.float32)
        cls_tok = 0.02 * jax.random.normal(jax.random.fold_in(_rk, 5), (1, 1, 256), jnp.float32)
        return (x, cls_tok)
    x, cls_tok = _rec_inputs()

    def _L0_tok_setup():
        import math
        import jax, jax.numpy as jnp
        import numpy as np
        PATCH = 16
        HIDDEN = 256
        IMG = 64
        GRID = IMG // PATCH
        N_TOK = GRID * GRID
        PDIM = 3 * PATCH * PATCH

        def make_pos_emb(n: int, d: int) -> jnp.ndarray:
            pos = jnp.arange(n, dtype=jnp.float32)[:, None]
            div = jnp.exp(jnp.arange(0, d, 2, dtype=jnp.float32) * (-math.log(10000.0) / d))
            pe = jnp.zeros((n, d), dtype=jnp.float32)
            pe = pe.at[:, 0::2].set(jnp.sin(pos * div))
            pe = pe.at[:, 1::2].set(jnp.cos(pos * div[:d // 2]))
            return pe
        key = jax.random.key(seed)
        k_img, k_w, k_b = jax.random.split(key, 3)
        img = jax.random.normal(k_img, (64, 3, IMG, IMG), dtype=jnp.float32)
        bound = 1.0 / math.sqrt(PDIM)
        W = jax.random.uniform(k_w, (HIDDEN, PDIM), minval=-bound, maxval=bound, dtype=jnp.float32)
        b = jax.random.uniform(k_b, (HIDDEN,), minval=-bound, maxval=bound, dtype=jnp.float32)
        pos_emb = make_pos_emb(N_TOK, HIDDEN)
        return {'img': img, 'W': W, 'b': b, 'pos_emb': pos_emb}
    _L0_tok_all = _L0_tok_setup()
    _L0_tok_in = {k: v for k, v in _L0_tok_all.items() if k in ('W', 'b', 'pos_emb')}
    del _L0_tok_all

    def _L0_attn_setup():
        import jax, jax.numpy as jnp
        import numpy as np
        D_IN = 256
        D_OUT = 256
        CTX_LEN = 512
        BATCH = 4
        SEQ = 512
        key = jax.random.key(seed)
        kx, kq, kk, kv = jax.random.split(key, 4)
        x = jax.random.normal(kx, (BATCH, SEQ, D_IN), dtype=jnp.float32)
        s = 1.0 / np.sqrt(D_IN)
        W_q = jax.random.uniform(kq, (D_IN, D_OUT), dtype=jnp.float32, minval=-s, maxval=s)
        W_k = jax.random.uniform(kk, (D_IN, D_OUT), dtype=jnp.float32, minval=-s, maxval=s)
        W_v = jax.random.uniform(kv, (D_IN, D_OUT), dtype=jnp.float32, minval=-s, maxval=s)
        return {'x': x, 'W_q': W_q, 'W_k': W_k, 'W_v': W_v}
    _L0_attn_all = _L0_attn_setup()
    _L0_attn_in = {k: v for k, v in _L0_attn_all.items() if k in ('W_q', 'W_k', 'W_v')}
    del _L0_attn_all

    def _L0_ffn_setup():
        import math
        import jax, jax.numpy as jnp
        import numpy as np
        E = 8
        H = 256
        HP = 128
        SPARSITY = 8
        N_ROTATE = 64
        ROPE_BASE = 10000.0

        def _rope(x, pos):
            half = N_ROTATE // 2
            inv_freq = 1.0 / ROPE_BASE ** (jnp.arange(half, dtype=jnp.float32) * 2.0 / N_ROTATE)
            ang = pos.astype(jnp.float32)[..., None] * inv_freq
            sin, cos = (jnp.sin(ang), jnp.cos(ang))
            x1, x2 = (x[..., :half], x[..., half:])
            return jnp.concatenate([x1 * cos - x2 * sin, x2 * cos + x1 * sin], axis=-1)
        key = jax.random.key(seed)
        k1, k2, k3, k4 = jax.random.split(key, 4)
        B, T = (4, 2048)
        X = jax.random.normal(k1, (B, T, H), dtype=jnp.float32)
        Wr = jax.random.uniform(k2, (E, H), minval=-1 / math.sqrt(H), maxval=1 / math.sqrt(H), dtype=jnp.float32)
        bq = 1 / math.sqrt(3 * HP)
        Wqkv = jax.random.uniform(k3, (E, H, 3 * HP), minval=-bq, maxval=bq, dtype=jnp.float32)
        bo = 1 / math.sqrt(H * E)
        Wo = jax.random.uniform(k4, (E, HP, H), minval=-bo, maxval=bo, dtype=jnp.float32)
        return {'X': X, 'Wr': Wr, 'Wqkv': Wqkv, 'Wo': Wo}
    _L0_ffn_all = _L0_ffn_setup()
    _L0_ffn_in = {k: v for k, v in _L0_ffn_all.items() if k in ('Wr', 'Wqkv', 'Wo')}
    del _L0_ffn_all

    def _L1_attn_setup():
        import jax, jax.numpy as jnp
        from jax import lax
        import numpy as np
        INPUT_DIM, STATE_DIM, CONV_K, EXPAND = (256, 16, 4, 2)
        INNER = INPUT_DIM * EXPAND
        BATCH, SEQ = (2, 512)
        key = jax.random.key(seed)
        ks = jax.random.split(key, 6)
        x = jax.random.normal(ks[0], (BATCH, SEQ, INPUT_DIM), jnp.float32)
        W_in = jax.random.normal(ks[1], (2 * INNER, INPUT_DIM), jnp.float32) * 0.02
        conv_w = jax.random.normal(ks[2], (INNER, 1, CONV_K), jnp.float32) * 0.1
        conv_b = jnp.zeros((INNER,), jnp.float32)
        A_log = jax.random.normal(ks[3], (INNER, STATE_DIM), jnp.float32)
        D = jnp.ones((INNER,), jnp.float32)
        W_out = jax.random.normal(ks[4], (INPUT_DIM, INNER), jnp.float32) * 0.02
        return {'x': x, 'W_in': W_in, 'conv_w': conv_w, 'conv_b': conv_b, 'A_log': A_log, 'D': D, 'W_out': W_out}
    _L1_attn_all = _L1_attn_setup()
    _L1_attn_in = {k: v for k, v in _L1_attn_all.items() if k in ('W_in', 'conv_w', 'conv_b', 'A_log', 'D', 'W_out')}
    del _L1_attn_all

    def _L1_ffn_setup():
        import jax, jax.numpy as jnp
        import numpy as np
        EMBED_DIM = 256
        NUM_EXPERTS = 8
        ACTIVE_EXPERTS = 2
        B, S = (2, 512)
        key = jax.random.key(seed)
        ks = jax.random.split(key, 8)
        D, E, H = (EMBED_DIM, NUM_EXPERTS, 4 * EMBED_DIM)
        sd = 1.0 / np.sqrt(D)
        sh = 1.0 / np.sqrt(H)
        x = jax.random.normal(ks[0], (B, S, D), dtype=jnp.float32)
        W1 = jax.random.uniform(ks[1], (E, D, H), jnp.float32, -sd, sd)
        b1 = jax.random.uniform(ks[2], (E, H), jnp.float32, -sd, sd)
        W2 = jax.random.uniform(ks[3], (E, H, D), jnp.float32, -sh, sh)
        b2 = jax.random.uniform(ks[4], (E, D), jnp.float32, -sh, sh)
        Wr = jax.random.uniform(ks[5], (D, E), jnp.float32, -sd, sd)
        br = jax.random.uniform(ks[6], (E,), jnp.float32, -sd, sd)
        return {'x': x, 'W1': W1, 'b1': b1, 'W2': W2, 'b2': b2, 'Wr': Wr, 'br': br}
    _L1_ffn_all = _L1_ffn_setup()
    _L1_ffn_in = {k: v for k, v in _L1_ffn_all.items() if k in ('W1', 'b1', 'W2', 'b2', 'Wr', 'br')}
    del _L1_ffn_all

    def _L2_attn_setup():
        import jax, jax.numpy as jnp
        import numpy as np
        B, S, D = (2, 512, 256)
        H, DH = (16, 64)
        DQL, DKVL = (128, 128)
        DR = 64
        TOPK = 64
        LN_EPS = 1e-05
        ROPE_BASE = 10000.0

        def _rope_tables(seq_len, dim):
            inv_freq = 1.0 / ROPE_BASE ** (np.arange(0, dim, 2, dtype=np.float32) / dim)
            t = np.arange(seq_len, dtype=np.float32)
            freqs = np.outer(t, inv_freq)
            cos = np.concatenate([np.cos(freqs), np.cos(freqs)], -1)[:, ::2]
            sin = np.concatenate([np.sin(freqs), np.sin(freqs)], -1)[:, ::2]
            return (jnp.asarray(cos), jnp.asarray(sin))

        def _apply_rope_subspace(x, d_rope):
            s = x.shape[-2]
            cos, sin = _rope_tables(s, d_rope)
            xr, xp = (x[..., :d_rope], x[..., d_rope:])
            e, o = (xr[..., 0::2], xr[..., 1::2])
            rot = jnp.stack([e * cos - o * sin, e * sin + o * cos], axis=-1).reshape(xr.shape)
            return jnp.concatenate([rot, xp], axis=-1)

        def _reference_tuple_inner(x, w_down_q, w_down_kv, w_up_q, w_up_k, w_up_v, w_out, ln_scale, ln_bias):
            b, s, d = x.shape
            residual = x
            mu = jnp.mean(x, axis=-1, keepdims=True)
            var = jnp.mean((x - mu) ** 2, axis=-1, keepdims=True)
            h = (x - mu) * jax.lax.rsqrt(var + LN_EPS) * ln_scale + ln_bias
            c_q = h @ w_down_q.T
            c_kv = h @ w_down_kv.T
            q = (c_q @ w_up_q.T).reshape(b, s, H, DH).transpose(0, 2, 1, 3)
            k = (c_kv @ w_up_k.T).reshape(b, s, H, DH).transpose(0, 2, 1, 3)
            v = (c_kv @ w_up_v.T).reshape(b, s, H, DH).transpose(0, 2, 1, 3)
            q = _apply_rope_subspace(q, DR)
            k = _apply_rope_subspace(k, DR)
            scale = 1.0 / np.sqrt(DH).astype(np.float32)
            scores = jnp.einsum('bhqd,bhkd->bhqk', q, k) * scale
            _, indices = jax.lax.top_k(scores, min(TOPK, s))
            attn = jax.nn.softmax(scores, axis=-1)
            out = jnp.einsum('bhqk,bhkd->bhqd', attn, v)
            out = out.transpose(0, 2, 1, 3).reshape(b, s, H * DH)
            out = out @ w_out.T + residual
            return (out, indices.astype(jnp.int64))
        key = jax.random.key(seed)
        ks = jax.random.split(key, 7)
        init = lambda k, shape: jax.random.normal(k, shape, jnp.float32) * 0.02
        return {'x': jax.random.normal(ks[0], (B, S, D), jnp.float32), 'w_down_q': init(ks[1], (DQL, D)), 'w_down_kv': init(ks[2], (DKVL, D)), 'w_up_q': init(ks[3], (H * DH, DQL)), 'w_up_k': init(ks[4], (H * DH, DKVL)), 'w_up_v': init(ks[5], (H * DH, DKVL)), 'w_out': init(ks[6], (D, H * DH)), 'ln_scale': jnp.ones((D,), jnp.float32), 'ln_bias': jnp.zeros((D,), jnp.float32)}
    _L2_attn_all = _L2_attn_setup()
    _L2_attn_in = {k: v for k, v in _L2_attn_all.items() if k in ('w_down_q', 'w_down_kv', 'w_up_q', 'w_up_k', 'w_up_v', 'w_out', 'ln_scale', 'ln_bias')}
    del _L2_attn_all

    def _L2_ffn_setup():
        import jax, jax.numpy as jnp
        import numpy as np
        B, S, D = (2, 512, 256)
        E, H, K = (8, 1408, 2)
        N_RESERVED = 4
        key = jax.random.key(seed)
        ks = jax.random.split(key, 5)
        scale = 0.02
        x = jax.random.normal(ks[0], (B, S, D), dtype=jnp.float32)
        gate_w = jax.random.normal(ks[1], (E, D), dtype=jnp.float32) * scale
        w1 = jax.random.normal(ks[2], (E, D, H), dtype=jnp.float32) * scale
        w3 = jax.random.normal(ks[3], (E, D, H), dtype=jnp.float32) * scale
        w2 = jax.random.normal(ks[4], (E, H, D), dtype=jnp.float32) * scale
        return {'x': x, 'gate_w': gate_w, 'w1': w1, 'w2': w2, 'w3': w3}
    _L2_ffn_all = _L2_ffn_setup()
    _L2_ffn_in = {k: v for k, v in _L2_ffn_all.items() if k in ('gate_w', 'w1', 'w2', 'w3')}
    del _L2_ffn_all

    def _L3_attn_setup():
        import math
        import jax, jax.numpy as jnp
        import numpy as np
        E = 256
        H = 16
        KVH = 8
        N_REP = H // KVH
        HD = E // H // 2
        DEPTH = 12
        LAMBDA_INIT = 0.8 - 0.6 * math.exp(-0.3 * DEPTH)
        EPS = 1e-06
        ROPE_BASE = 10000.0

        def rope_tables(T):
            inv_freq = 1.0 / ROPE_BASE ** (np.arange(0, HD, 2, dtype=np.float32) / HD)
            t = np.arange(T, dtype=np.float32)
            freqs = np.outer(t, inv_freq)
            return (jnp.asarray(np.cos(freqs)), jnp.asarray(np.sin(freqs)))

        def apply_rope(x, cos, sin):
            d = x.shape[-1] // 2
            c = cos[None, :, None, :]
            s = sin[None, :, None, :]
            x1, x2 = (x[..., :d], x[..., d:])
            return jnp.concatenate([x1 * c + x2 * s, -x1 * s + x2 * c], axis=-1)

        def causal_attn(q, k, v, scale):
            T = q.shape[1]
            mask = jnp.tril(jnp.ones((T, T), dtype=bool))
            s = jnp.einsum('bthd,bshd->bhts', q, k) * scale
            s = jnp.where(mask[None, None], s, jnp.finfo(s.dtype).min)
            p = jax.nn.softmax(s, axis=-1)
            return jnp.einsum('bhts,bshd->bthd', p, v)
        key = jax.random.key(seed)
        ks = jax.random.split(key, 10)
        s = 0.02
        return {'x': jax.random.normal(ks[0], (4, 256, E), jnp.float32), 'Wq': jax.random.normal(ks[1], (E, E), jnp.float32) * s, 'Wk': jax.random.normal(ks[2], (E, E // N_REP), jnp.float32) * s, 'Wv': jax.random.normal(ks[3], (E, E // N_REP), jnp.float32) * s, 'Wo': jax.random.normal(ks[4], (E, E), jnp.float32) * s, 'lambda_q1': jax.random.normal(ks[5], (HD,), jnp.float32) * 0.1, 'lambda_k1': jax.random.normal(ks[6], (HD,), jnp.float32) * 0.1, 'lambda_q2': jax.random.normal(ks[7], (HD,), jnp.float32) * 0.1, 'lambda_k2': jax.random.normal(ks[8], (HD,), jnp.float32) * 0.1, 'rms_w': jnp.ones((2 * HD,), jnp.float32)}
    _L3_attn_all = _L3_attn_setup()
    _L3_attn_in = {k: v for k, v in _L3_attn_all.items() if k in ('Wq', 'Wk', 'Wv', 'Wo', 'lambda_q1', 'lambda_k1', 'lambda_q2', 'lambda_k2', 'rms_w')}
    del _L3_attn_all

    def _L3_ffn_setup():
        import jax, jax.numpy as jnp
        import numpy as np
        key = jax.random.key(seed)
        k_x, k_W, k_b, k_ids, k_w = jax.random.split(key, 5)
        N_ADAPTERS, D_OUT, D_IN = (32, 256, 256)
        B, S = (2, 512)
        K = 8
        x = jax.random.normal(k_x, (B, S, D_IN), dtype=jnp.float32)
        W = jax.random.normal(k_W, (N_ADAPTERS, D_OUT, D_IN), dtype=jnp.float32)
        b = jax.random.normal(k_b, (N_ADAPTERS, D_OUT), dtype=jnp.float32)
        ids = jax.random.randint(k_ids, (K,), 0, N_ADAPTERS, dtype=jnp.int64)
        weights = jax.random.uniform(k_w, (K,), dtype=jnp.float32)
        return {'x': x, 'W': W, 'b': b, 'ids': ids, 'weights': weights}
    _L3_ffn_all = _L3_ffn_setup()
    _L3_ffn_in = {k: v for k, v in _L3_ffn_all.items() if k in ('W', 'b', 'ids', 'weights')}
    del _L3_ffn_all
    return {'x': x, 'cls_tok': cls_tok, 'L0_tok_W': _L0_tok_in['W'], 'L0_tok_b': _L0_tok_in['b'], 'L0_tok_pos_emb': _L0_tok_in['pos_emb'], 'L0_attn_W_q': _L0_attn_in['W_q'], 'L0_attn_W_k': _L0_attn_in['W_k'], 'L0_attn_W_v': _L0_attn_in['W_v'], 'L0_ffn_Wr': _L0_ffn_in['Wr'], 'L0_ffn_Wqkv': _L0_ffn_in['Wqkv'], 'L0_ffn_Wo': _L0_ffn_in['Wo'], 'L1_attn_W_in': _L1_attn_in['W_in'], 'L1_attn_conv_w': _L1_attn_in['conv_w'], 'L1_attn_conv_b': _L1_attn_in['conv_b'], 'L1_attn_A_log': _L1_attn_in['A_log'], 'L1_attn_D': _L1_attn_in['D'], 'L1_attn_W_out': _L1_attn_in['W_out'], 'L1_ffn_W1': _L1_ffn_in['W1'], 'L1_ffn_b1': _L1_ffn_in['b1'], 'L1_ffn_W2': _L1_ffn_in['W2'], 'L1_ffn_b2': _L1_ffn_in['b2'], 'L1_ffn_Wr': _L1_ffn_in['Wr'], 'L1_ffn_br': _L1_ffn_in['br'], 'L2_attn_w_down_q': _L2_attn_in['w_down_q'], 'L2_attn_w_down_kv': _L2_attn_in['w_down_kv'], 'L2_attn_w_up_q': _L2_attn_in['w_up_q'], 'L2_attn_w_up_k': _L2_attn_in['w_up_k'], 'L2_attn_w_up_v': _L2_attn_in['w_up_v'], 'L2_attn_w_out': _L2_attn_in['w_out'], 'L2_attn_ln_scale': _L2_attn_in['ln_scale'], 'L2_attn_ln_bias': _L2_attn_in['ln_bias'], 'L2_ffn_gate_w': _L2_ffn_in['gate_w'], 'L2_ffn_w1': _L2_ffn_in['w1'], 'L2_ffn_w2': _L2_ffn_in['w2'], 'L2_ffn_w3': _L2_ffn_in['w3'], 'L3_attn_Wq': _L3_attn_in['Wq'], 'L3_attn_Wk': _L3_attn_in['Wk'], 'L3_attn_Wv': _L3_attn_in['Wv'], 'L3_attn_Wo': _L3_attn_in['Wo'], 'L3_attn_lambda_q1': _L3_attn_in['lambda_q1'], 'L3_attn_lambda_k1': _L3_attn_in['lambda_k1'], 'L3_attn_lambda_q2': _L3_attn_in['lambda_q2'], 'L3_attn_lambda_k2': _L3_attn_in['lambda_k2'], 'L3_attn_rms_w': _L3_attn_in['rms_w'], 'L3_ffn_W': _L3_ffn_in['W'], 'L3_ffn_b': _L3_ffn_in['b'], 'L3_ffn_ids': _L3_ffn_in['ids'], 'L3_ffn_weights': _L3_ffn_in['weights']}

def reference(x, cls_tok, L0_tok_W, L0_tok_b, L0_tok_pos_emb, L0_attn_W_q, L0_attn_W_k, L0_attn_W_v, L0_ffn_Wr, L0_ffn_Wqkv, L0_ffn_Wo, L1_attn_W_in, L1_attn_conv_w, L1_attn_conv_b, L1_attn_A_log, L1_attn_D, L1_attn_W_out, L1_ffn_W1, L1_ffn_b1, L1_ffn_W2, L1_ffn_b2, L1_ffn_Wr, L1_ffn_br, L2_attn_w_down_q, L2_attn_w_down_kv, L2_attn_w_up_q, L2_attn_w_up_k, L2_attn_w_up_v, L2_attn_w_out, L2_attn_ln_scale, L2_attn_ln_bias, L2_ffn_gate_w, L2_ffn_w1, L2_ffn_w2, L2_ffn_w3, L3_attn_Wq, L3_attn_Wk, L3_attn_Wv, L3_attn_Wo, L3_attn_lambda_q1, L3_attn_lambda_k1, L3_attn_lambda_q2, L3_attn_lambda_k2, L3_attn_rms_w, L3_ffn_W, L3_ffn_b, L3_ffn_ids, L3_ffn_weights):
    import jax
    import jax.numpy as jnp

    def _L0_tok_ref(img, W, b, pos_emb):
        import math
        import jax, jax.numpy as jnp
        import numpy as np
        PATCH = 16
        HIDDEN = 256
        IMG = 64
        GRID = IMG // PATCH
        N_TOK = GRID * GRID
        PDIM = 3 * PATCH * PATCH

        def make_pos_emb(n: int, d: int) -> jnp.ndarray:
            pos = jnp.arange(n, dtype=jnp.float32)[:, None]
            div = jnp.exp(jnp.arange(0, d, 2, dtype=jnp.float32) * (-math.log(10000.0) / d))
            pe = jnp.zeros((n, d), dtype=jnp.float32)
            pe = pe.at[:, 0::2].set(jnp.sin(pos * div))
            pe = pe.at[:, 1::2].set(jnp.cos(pos * div[:d // 2]))
            return pe
        B, C, H, Wd = img.shape
        p = PATCH
        gh, gw = (H // p, Wd // p)
        x = img.reshape(B, C, gh, p, gw, p)
        x = jnp.transpose(x, (0, 2, 4, 1, 3, 5))
        x = x.reshape(B, gh * gw, C * p * p)
        z = jnp.einsum('bnd,hd->bnh', x, W) + b
        return z + pos_emb[None, :, :]

    def _L0_attn_ref(x, W_q, W_k, W_v):
        import jax, jax.numpy as jnp
        import numpy as np
        D_IN = 256
        D_OUT = 256
        CTX_LEN = 512
        BATCH = 4
        SEQ = 512
        b, n, _ = x.shape
        d_out = W_q.shape[1]
        q = x @ W_q
        k = x @ W_k
        v = x @ W_v
        scores = jnp.einsum('bqd,bkd->bqk', q, k)
        causal = jnp.triu(jnp.ones((n, n), dtype=bool), k=1)
        scores = jnp.where(causal, -jnp.inf, scores)
        attn = jax.nn.softmax(scores / jnp.sqrt(jnp.float32(d_out)), axis=-1)
        return jnp.einsum('bqk,bkd->bqd', attn, v)

    def _L0_ffn_ref(X, Wr, Wqkv, Wo):
        import math
        import jax, jax.numpy as jnp
        import numpy as np
        E = 8
        H = 256
        HP = 128
        SPARSITY = 8
        N_ROTATE = 64
        ROPE_BASE = 10000.0

        def _rope(x, pos):
            half = N_ROTATE // 2
            inv_freq = 1.0 / ROPE_BASE ** (jnp.arange(half, dtype=jnp.float32) * 2.0 / N_ROTATE)
            ang = pos.astype(jnp.float32)[..., None] * inv_freq
            sin, cos = (jnp.sin(ang), jnp.cos(ang))
            x1, x2 = (x[..., :half], x[..., half:])
            return jnp.concatenate([x1 * cos - x2 * sin, x2 * cos + x1 * sin], axis=-1)
        B, T, _ = X.shape
        k = min(max(T // SPARSITY, 2), T)
        logits = jax.nn.sigmoid(jnp.einsum('bth,eh->bte', X, Wr))
        topk_vals, topk_I = jax.lax.top_k(logits.transpose(0, 2, 1), k)
        idx_flat = topk_I.reshape(B, E * k)
        Xg = jnp.take_along_axis(X, idx_flat[:, :, None], axis=1).reshape(B, E, k, H)
        QKV = jnp.einsum('beki,eij->bekj', Xg, Wqkv)
        Q, K, V = jnp.split(QKV, 3, axis=-1)
        Q = jnp.concatenate([_rope(Q[..., :N_ROTATE], topk_I), Q[..., N_ROTATE:]], axis=-1)
        K = jnp.concatenate([_rope(K[..., :N_ROTATE], topk_I), K[..., N_ROTATE:]], axis=-1)
        M = topk_I[..., :, None] >= topk_I[..., None, :]
        scores = jnp.einsum('bekd,bemd->bekm', Q, K) / math.sqrt(HP)
        scores = jnp.where(M, scores, -jnp.inf)
        A = jax.nn.softmax(scores, axis=-1)
        AV = jnp.einsum('bekm,bemd->bekd', A, V)
        AV = AV * topk_vals[..., None]
        Xpre = jnp.einsum('bekj,eji->beki', AV, Wo)
        out = jnp.zeros((B, T, H), dtype=X.dtype)
        out = out.at[jnp.arange(B)[:, None], idx_flat].add(Xpre.reshape(B, E * k, H))
        return out

    def _L1_attn_ref(x, W_in, conv_w, conv_b, A_log, D, W_out):
        import jax, jax.numpy as jnp
        from jax import lax
        import numpy as np
        INPUT_DIM, STATE_DIM, CONV_K, EXPAND = (256, 16, 4, 2)
        INNER = INPUT_DIM * EXPAND
        BATCH, SEQ = (2, 512)
        b, s, _ = x.shape
        inner = W_in.shape[0] // 2
        K = conv_w.shape[-1]
        state = A_log.shape[1]
        xr = x @ W_in.T
        x_ssm, res = (xr[..., :inner], xr[..., inner:])
        xc = jnp.transpose(x_ssm, (0, 2, 1))
        xc = jnp.pad(xc, ((0, 0), (0, 0), (K - 1, 0)))
        xc = lax.conv_general_dilated(xc, conv_w, (1,), 'VALID', feature_group_count=inner, dimension_numbers=('NCH', 'OIH', 'NCH'))
        x_conv = jax.nn.silu(jnp.transpose(xc, (0, 2, 1)) + conv_b)
        delta = jax.nn.softplus(x_conv)
        A = -jnp.exp(A_log)
        A_d = jnp.exp(delta[..., None] * A)
        Bx = x_conv * x_conv

        def step(h, inp):
            a_t, bx_t, c_t = inp
            h = a_t * h + bx_t[..., None]
            y = c_t * jnp.sum(h, axis=-1)
            return (h, y)
        h0 = jnp.zeros((b, inner, state), x.dtype)
        _, ys = lax.scan(step, h0, (jnp.moveaxis(A_d, 1, 0), jnp.moveaxis(Bx, 1, 0), jnp.moveaxis(x_conv, 1, 0)))
        y_ssm = jnp.moveaxis(ys, 0, 1)
        y = y_ssm * jax.nn.silu(res) + D * x_conv
        return y @ W_out.T

    def _L1_ffn_ref(x, W1, b1, W2, b2, Wr, br):
        import jax, jax.numpy as jnp
        import numpy as np
        EMBED_DIM = 256
        NUM_EXPERTS = 8
        ACTIVE_EXPERTS = 2
        B, S = (2, 512)
        E, K = (NUM_EXPERTS, ACTIVE_EXPERTS)
        scores = jax.nn.relu(jnp.einsum('bsd,de->bse', x, Wr) + br)
        _, topk_idx = jax.lax.top_k(scores, K)
        mask = jnp.sum(jax.nn.one_hot(topk_idx, E, dtype=scores.dtype), axis=-2)
        masked = jnp.where(mask > 0, scores, -jnp.inf)
        router_weight = jax.nn.softmax(masked, axis=-1) * mask
        h = jax.nn.relu(jnp.einsum('bsd,edh->ebsh', x, W1) + b1[:, None, None, :])
        y = jnp.einsum('ebsh,ehd->ebsd', h, W2) + b2[:, None, None, :]
        out = jnp.einsum('bse,ebsd->bsd', router_weight, y)
        return out

    def _L2_attn_ref(x, w_down_q, w_down_kv, w_up_q, w_up_k, w_up_v, w_out, ln_scale, ln_bias):
        import jax, jax.numpy as jnp
        import numpy as np
        B, S, D = (2, 512, 256)
        H, DH = (16, 64)
        DQL, DKVL = (128, 128)
        DR = 64
        TOPK = 64
        LN_EPS = 1e-05
        ROPE_BASE = 10000.0

        def _rope_tables(seq_len, dim):
            inv_freq = 1.0 / ROPE_BASE ** (np.arange(0, dim, 2, dtype=np.float32) / dim)
            t = np.arange(seq_len, dtype=np.float32)
            freqs = np.outer(t, inv_freq)
            cos = np.concatenate([np.cos(freqs), np.cos(freqs)], -1)[:, ::2]
            sin = np.concatenate([np.sin(freqs), np.sin(freqs)], -1)[:, ::2]
            return (jnp.asarray(cos), jnp.asarray(sin))

        def _apply_rope_subspace(x, d_rope):
            s = x.shape[-2]
            cos, sin = _rope_tables(s, d_rope)
            xr, xp = (x[..., :d_rope], x[..., d_rope:])
            e, o = (xr[..., 0::2], xr[..., 1::2])
            rot = jnp.stack([e * cos - o * sin, e * sin + o * cos], axis=-1).reshape(xr.shape)
            return jnp.concatenate([rot, xp], axis=-1)

        def _reference_tuple_inner(x, w_down_q, w_down_kv, w_up_q, w_up_k, w_up_v, w_out, ln_scale, ln_bias):
            b, s, d = x.shape
            residual = x
            mu = jnp.mean(x, axis=-1, keepdims=True)
            var = jnp.mean((x - mu) ** 2, axis=-1, keepdims=True)
            h = (x - mu) * jax.lax.rsqrt(var + LN_EPS) * ln_scale + ln_bias
            c_q = h @ w_down_q.T
            c_kv = h @ w_down_kv.T
            q = (c_q @ w_up_q.T).reshape(b, s, H, DH).transpose(0, 2, 1, 3)
            k = (c_kv @ w_up_k.T).reshape(b, s, H, DH).transpose(0, 2, 1, 3)
            v = (c_kv @ w_up_v.T).reshape(b, s, H, DH).transpose(0, 2, 1, 3)
            q = _apply_rope_subspace(q, DR)
            k = _apply_rope_subspace(k, DR)
            scale = 1.0 / np.sqrt(DH).astype(np.float32)
            scores = jnp.einsum('bhqd,bhkd->bhqk', q, k) * scale
            _, indices = jax.lax.top_k(scores, min(TOPK, s))
            attn = jax.nn.softmax(scores, axis=-1)
            out = jnp.einsum('bhqk,bhkd->bhqd', attn, v)
            out = out.transpose(0, 2, 1, 3).reshape(b, s, H * DH)
            out = out @ w_out.T + residual
            return (out, indices.astype(jnp.int64))
        return _reference_tuple_inner(x, w_down_q, w_down_kv, w_up_q, w_up_k, w_up_v, w_out, ln_scale, ln_bias)[0]

    def _L2_ffn_ref(x, gate_w, w1, w2, w3):
        import jax, jax.numpy as jnp
        import numpy as np
        B, S, D = (2, 512, 256)
        E, H, K = (8, 1408, 2)
        N_RESERVED = 4
        b, s, d = x.shape
        T = b * s
        xf = x.reshape(T, d)
        logits = xf @ gate_w.T
        expert_ids = jnp.arange(E)
        logits = jnp.where(expert_ids[None, :] >= E - N_RESERVED, -jnp.inf, logits)
        weights = jax.nn.softmax(logits, axis=-1)
        top_w, top_idx = jax.lax.top_k(weights, K)
        top_w = top_w / jnp.sum(top_w, axis=-1, keepdims=True)
        cw = jnp.zeros((T, E), dtype=x.dtype).at[jnp.arange(T)[:, None], top_idx].add(top_w)
        h = jax.nn.silu(jnp.einsum('td,edh->teh', xf, w1)) * jnp.einsum('td,edh->teh', xf, w3)
        y = jnp.einsum('teh,ehd->ted', h, w2)
        out = jnp.einsum('te,ted->td', cw, y)
        return out.reshape(b, s, d)

    def _L3_attn_ref(x, Wq, Wk, Wv, Wo, lambda_q1, lambda_k1, lambda_q2, lambda_k2, rms_w):
        import math
        import jax, jax.numpy as jnp
        import numpy as np
        E = 256
        H = 16
        KVH = 8
        N_REP = H // KVH
        HD = E // H // 2
        DEPTH = 12
        LAMBDA_INIT = 0.8 - 0.6 * math.exp(-0.3 * DEPTH)
        EPS = 1e-06
        ROPE_BASE = 10000.0

        def rope_tables(T):
            inv_freq = 1.0 / ROPE_BASE ** (np.arange(0, HD, 2, dtype=np.float32) / HD)
            t = np.arange(T, dtype=np.float32)
            freqs = np.outer(t, inv_freq)
            return (jnp.asarray(np.cos(freqs)), jnp.asarray(np.sin(freqs)))

        def apply_rope(x, cos, sin):
            d = x.shape[-1] // 2
            c = cos[None, :, None, :]
            s = sin[None, :, None, :]
            x1, x2 = (x[..., :d], x[..., d:])
            return jnp.concatenate([x1 * c + x2 * s, -x1 * s + x2 * c], axis=-1)

        def causal_attn(q, k, v, scale):
            T = q.shape[1]
            mask = jnp.tril(jnp.ones((T, T), dtype=bool))
            s = jnp.einsum('bthd,bshd->bhts', q, k) * scale
            s = jnp.where(mask[None, None], s, jnp.finfo(s.dtype).min)
            p = jax.nn.softmax(s, axis=-1)
            return jnp.einsum('bhts,bshd->bthd', p, v)
        B, T, _ = x.shape
        q = (x @ Wq).reshape(B, T, 2 * H, HD)
        k = (x @ Wk).reshape(B, T, 2 * KVH, HD)
        v = (x @ Wv).reshape(B, T, KVH, 2, HD)
        cos, sin = rope_tables(T)
        q = apply_rope(q, cos, sin)
        k = apply_rope(k, cos, sin)
        q = q.reshape(B, T, H, 2, HD)
        k = k.reshape(B, T, KVH, 2, HD)
        q1, q2 = (q[:, :, :, 0], q[:, :, :, 1])
        k1, k2 = (k[:, :, :, 0], k[:, :, :, 1])
        vcat = v.reshape(B, T, KVH, 2 * HD)
        k1 = jnp.repeat(k1, N_REP, axis=2)
        k2 = jnp.repeat(k2, N_REP, axis=2)
        vcat = jnp.repeat(vcat, N_REP, axis=2)
        scale = HD ** (-0.5)
        attn1 = causal_attn(q1, k1, vcat, scale)
        attn2 = causal_attn(q2, k2, vcat, scale)
        lambda_1 = jnp.exp(jnp.sum(lambda_q1 * lambda_k1))
        lambda_2 = jnp.exp(jnp.sum(lambda_q2 * lambda_k2))
        lambda_full = lambda_1 - lambda_2 + LAMBDA_INIT
        attn = attn1 - lambda_full * attn2
        rms = jnp.sqrt(jnp.mean(attn * attn, axis=-1, keepdims=True) + EPS)
        attn = attn / rms * rms_w
        attn = attn * (1.0 - LAMBDA_INIT)
        attn = attn.reshape(B, T, H * 2 * HD)
        return attn @ Wo

    def _L3_ffn_ref(x, W, b, ids, weights):
        import jax, jax.numpy as jnp
        import numpy as np
        Wsel = W[ids]
        bsel = b[ids]
        out = jnp.einsum('k,kod,bsd->bso', weights, Wsel, x)
        out = out + jnp.einsum('k,ko->o', weights, bsel)
        return out
    h = _L0_tok_ref(x, L0_tok_W, L0_tok_b, L0_tok_pos_emb)
    h = jnp.concatenate([jnp.broadcast_to(cls_tok, (h.shape[0], 1, h.shape[2])), h], axis=1)
    h = h + _L0_attn_ref(_layernorm(h, axis=-1), L0_attn_W_q, L0_attn_W_k, L0_attn_W_v)
    h = h + _L0_ffn_ref(_layernorm(h, axis=-1), L0_ffn_Wr, L0_ffn_Wqkv, L0_ffn_Wo)
    h = h + _L1_attn_ref(_layernorm(h, axis=-1), L1_attn_W_in, L1_attn_conv_w, L1_attn_conv_b, L1_attn_A_log, L1_attn_D, L1_attn_W_out)
    h = h + _L1_ffn_ref(_layernorm(h, axis=-1), L1_ffn_W1, L1_ffn_b1, L1_ffn_W2, L1_ffn_b2, L1_ffn_Wr, L1_ffn_br)
    h = h + _L2_attn_ref(_layernorm(h, axis=-1), L2_attn_w_down_q, L2_attn_w_down_kv, L2_attn_w_up_q, L2_attn_w_up_k, L2_attn_w_up_v, L2_attn_w_out, L2_attn_ln_scale, L2_attn_ln_bias)
    h = h + _L2_ffn_ref(_layernorm(h, axis=-1), L2_ffn_gate_w, L2_ffn_w1, L2_ffn_w2, L2_ffn_w3)
    h = h + _L3_attn_ref(_layernorm(h, axis=-1), L3_attn_Wq, L3_attn_Wk, L3_attn_Wv, L3_attn_Wo, L3_attn_lambda_q1, L3_attn_lambda_k1, L3_attn_lambda_q2, L3_attn_lambda_k2, L3_attn_rms_w)
    h = h + _L3_ffn_ref(_layernorm(h, axis=-1), L3_ffn_W, L3_ffn_b, L3_ffn_ids, L3_ffn_weights)
    return h

_drawn_inputs = setup_inputs


def setup_inputs(seed=0):
    import zlib

    import numpy as np

    out = dict(_drawn_inputs(seed))
    spreads = {'L1_attn_conv_b': (0.0, 0.1),
     'L1_attn_D': (1.0, 0.6),
     'L2_attn_ln_scale': (1.0, 0.6),
     'L2_attn_ln_bias': (0.0, 0.8),
     'L3_attn_rms_w': (1.0, 0.6)}
    factors = {'L1_attn_A_log': 128.407,
     'L1_ffn_b1': 4.679,
     'L1_ffn_b2': 3.706,
     'L2_attn_w_down_q': 8.0,
     'L2_attn_w_down_kv': 3.595,
     'L2_attn_w_up_q': 8.0,
     'L2_attn_w_up_k': 8.0,
     'L2_attn_w_up_v': 3.655,
     'L2_attn_w_out': 3.763,
     'L2_ffn_gate_w': 5.598,
     'L2_ffn_w1': 3.749,
     'L2_ffn_w2': 3.688,
     'L2_ffn_w3': 3.707,
     'L3_attn_Wq': 16.008,
     'L3_attn_Wk': 15.268,
     'L3_attn_lambda_q1': 200.0,
     'L3_attn_lambda_k1': 8.0,
     'L3_attn_lambda_q2': 64.0,
     'L3_attn_lambda_k2': 64.0}
    for name, (base, spread) in spreads.items():
        noise = np.random.default_rng([zlib.crc32(name.encode()), seed]).standard_normal(out[name].shape)
        drawn = base * np.exp(spread * noise) if base else spread * noise
        out[name] = jnp.asarray(drawn.astype(out[name].dtype))
    for name, factor in factors.items():
        out[name] = (out[name] * factor).astype(out[name].dtype)
    return out
```

```python
from contextlib import ExitStack

import numpy as np

import concourse.bass as bass
from concourse import mybir

F32 = mybir.dt.float32
I32 = mybir.dt.int32
ALU = mybir.AluOpType
ACT = mybir.ActivationFunctionType
AX = mybir.AxisListType

BATCH = 32
SEQ = 17
D = 256
KD = D // 128
TOK = BATCH * SEQ
HALF = TOK // 2
GROUP = 7
TILES = -(-BATCH // GROUP)
ROWS = GROUP * SEQ
WIDTH = [min(GROUP, BATCH - GROUP * i) for i in range(TILES)]
N = [w * SEQ for w in WIDTH]
T0 = [ROWS * i for i in range(TILES)]
PK = 3 * 16 * 16 // 128
E0 = 8
HP = 128
QKVW = 3 * HP + 1
ROT = 32
INNER = 4
STATE = 16
E1, F1C = 8, 8
E2, F2C = 4, 11
H2, DH2 = 16, 64
H3, KV3, HD3 = 16, 8, 8
MAPS = 2 * H3
VD3 = 2 * HD3
VP3 = 32
ADAPT = 8
LAMBDA_INIT = 0.8 - 0.6 * float(np.exp(-0.3 * 12))
MASKED = -1.0e30


def constants():
    p = np.arange(128)
    t = np.arange(SEQ, dtype=np.float32)
    parts = {}
    parts["ident"] = np.eye(128)
    q, k = p[:, None], np.arange(ROWS)[None, :]
    same = (q // SEQ) == (k // SEQ)
    parts["block"] = np.where(same, 0.0, MASKED)
    parts["causal"] = np.where(same & (k <= q), 0.0, MASKED)
    parts["image"] = (q // SEQ) == np.arange(GROUP)[None, :]
    parts["place"] = (q % SEQ) == np.arange(SEQ)[None, :]
    parts["spread"] = (q % SEQ == k % SEQ) & (q < 2 * SEQ)
    parts["rank17"] = np.broadcast_to(64.0 - t, (128, SEQ))
    parts["rank8"] = np.broadcast_to(8.0 - np.arange(8), (128, 8))
    inv = (1.0 / 10000.0 ** (np.arange(ROT, dtype=np.float32) * np.float32(2.0) / 64)).astype(np.float32)
    ang = (t[:, None] * inv[None]).astype(np.float32)
    table = np.zeros((128, 2 * ROT + 1), np.float32)
    table[:SEQ] = np.concatenate([np.cos(ang), np.sin(ang), t[:, None]], 1)
    parts["rope0"] = table
    parts["token"] = np.broadcast_to(np.arange(TOK), (128, TOK))
    parts["first"] = (p[:, None] % BATCH) * SEQ
    parts["eps5"] = np.full((128, 1), 1e-5)
    parts["eps6"] = np.full((128, 1), 1e-6)
    inv = (1.0 / 10000.0 ** (np.arange(0, DH2, 2, dtype=np.float32) / DH2)).astype(np.float32)
    ang = np.outer(t, inv[(2 * np.arange(32)) % 32]).astype(np.float32)
    parts["cos2"] = np.cos(ang).T[p % 32]
    parts["sin2"] = np.sin(ang).T[p % 32]
    inv = (1.0 / 10000.0 ** (np.arange(0, HD3, 2, dtype=np.float32) / HD3)).astype(np.float32)
    ang = np.outer(t, inv).astype(np.float32)
    parts["cos3"] = np.cos(ang)[p % SEQ]
    parts["sin3"] = np.sin(ang)[p % SEQ]
    parts["own"] = (p[:, None] // HD3) == np.arange(16)[None, :]
    parts["one"] = np.ones((128, 128))
    at, out = {}, []
    w = 0
    for name, a in parts.items():
        a = np.asarray(a, np.float32)
        at[name] = (w, a.shape[1])
        w += a.shape[1]
        out.append(a)
    return at, np.concatenate(out, 1)


def build(nc, dram, out, stop=99):
    CONST, const_np = constants()
    ctx = ExitStack()
    with ctx:
        sems = {}

        def sem(name):
            if name not in sems:
                sems[name] = ctx.enter_context(nc.semaphore(name))
            return sems[name]

        def sb(name, shape):
            return ctx.enter_context(nc.sbuf_tensor(name, [128] + shape, F32))

        h = sb("h", [TILES, D])
        xn = sb("xn", [TILES, D])
        xT = sb("xT", [KD, TOK])
        cst = sb("cst", [const_np.shape[1]])
        st = sb("st", [TILES, 6])
        mv = sb("mv", [TILES, 2])
        std = sb("std", [TILES])
        rstd = sb("rstd", [TILES])
        w_in = sb("w_in", [KD, 8 * 128])
        w_out = sb("w_out", [INNER, D])
        m_small = sb("m_small", [INNER, 4 + 1 + 1 + STATE])
        w_r0 = sb("w_r0", [KD, E0])
        w_r1 = sb("w_r1", [KD, E1])
        w_br = sb("w_br", [E1])
        w_b1 = sb("w_b1", [E1, F1C])
        w_b2 = sb("w_b2", [D])
        w_gate = sb("w_gate", [KD, E2])
        w_ln = sb("w_ln", [2, KD])
        w_q3 = sb("w_q3", [KD, D])
        w_k3 = sb("w_k3", [KD, D // 2])
        w_v3 = sb("w_v3", [KD, D // 2])
        w_o3 = sb("w_o3", [KD, D])
        w_lam = sb("w_lam", [4, HD3])
        w_rms = sb("w_rms", [VD3])
        w_eff = sb("w_eff", [KD, D])
        w_tmp = sb("w_tmp", [KD, D])
        w_adp = sb("w_adp", [ADAPT])
        w_arep = sb("w_arep", [ROWS])
        w_acol = sb("w_acol", [1])
        b_adp = sb("b_adp", [D])
        misc = sb("misc", [900])
        flag = sb("flag", [8])
        ids = ctx.enter_context(nc.sbuf_tensor("ids", [128, ADAPT], I32))
        PIECE = F2C * D
        RING = sb("ring", [4 * PIECE])
        HEAD, TAIL = 20912, 2 * PIECE
        BC = sb("bc", [HEAD + TAIL])
        PS = ctx.enter_context(nc.psum_tensor("PS", [128, 8, 512], F32))

        def const(name):
            a, w = CONST[name]
            return cst[:, a:a + w]

        def carve(region, start, sizes):
            got = []
            for dims in sizes:
                n = int(np.prod(dims))
                v = region[:, start:start + n]
                if len(dims) == 2:
                    v = v.rearrange("p (a b) -> p a b", a=dims[0])
                if len(dims) == 3:
                    v = v.rearrange("p (a b c) -> p a b c", a=dims[0], b=dims[1])
                got.append(v)
                start += n
            return got, start

        ident = const("ident")

        early, end = carve(BC, HEAD + TAIL - 14544, [(PK, TOK), (PK, D), (3, KD, D), (KD, E0 * QKVW), (E0, D)])
        assert end == HEAD + TAIL
        patch, w_tok, w_qkv0, w_cat, w_o0 = early
        w_cat = w_cat.rearrange("p k (e w) -> p k e w", e=E0)
        pos = misc[:, 0:D]
        LATE = misc[:, D:900]
        raw = RING[:, 0:ADAPT * KD * D].rearrange("p (a b) -> p a b", a=ADAPT)

        (qk0, v0, sm0, p0, pt0, mx0, sum0), _ = carve(
            BC, 0, [(4, TOK), (TILES, D), (TILES, ROWS), (TILES, ROWS), (TILES, ROWS), (TILES,), (2 * TILES,)])
        (sg, sel, t8a, t8b, m8, r8), f0a = carve(
            RING, ADAPT * KD * D, [(TOK,), (2, TOK), (TOK,), (TOK,), (2, BATCH), (BATCH,)])
        assert f0a <= 4 * PIECE
        (G, xg, poh, qkv, prod, GT, avt, av, xp, rt), f0b = carve(
            BC, 0, [(TILES, 2 * E0 * GROUP), (KD, 2 * E0 * BATCH), (2 * E0, BATCH), (4, 450), (512,),
                    (4, TOK), (4, 128), (4, 128), (4, D), (6, 256)])
        assert f0b <= HEAD + TAIL - 14544, f0b
        (xpad, cv, xc, delta, bx, sres, a_ring, hs_ring), mend = carve(
            BC, 0, [(INNER, BATCH * (SEQ + 3)), (INNER, TOK), (INNER, TOK), (INNER, TOK), (INNER, TOK),
                    (INNER, TOK), (8, TOK), (8, TOK)])
        assert mend <= HEAD + TAIL
        hT = [carve(BC, e * F2C * TOK, [(F2C, TOK)])[0][0] for e in range(2)]
        (sil,), _ = carve(BC, 2 * F2C * TOK, [(3, HALF)])
        (w_dq, w_dkv, w_uq, w_uk, w_uv, w_o2), end = carve(
            BC, HEAD, [(KD, 128), (KD, 128), (8, 128), (8, 128), (1024,), (8, D)])
        assert end == HEAD + TAIL
        (q2, k2, v2, rt2), a2end = carve(BC, 0, [(8, TOK), (8, TOK), (TILES, H2 * (DH2 + 1)), (8, TOK)])
        (cT,), a2b = carve(BC, a2end, [(2, TOK)])
        assert a2b <= HEAD, a2b
        (yn, gT), _ = carve(BC, a2end - 8 * TOK, [(TILES, D), (KD, TOK)])
        (sm2, p2, pt2, o2, oT2), end = carve(
            BC, a2end - 8 * TOK, [(3, 4 * ROWS), (2, 4 * ROWS), (2, 4 * ROWS), (1, 1024), (8, ROWS)])
        assert end <= HEAD, end
        o2b, _ = carve(misc, 0, [(4,)] * 5)
        (qt3, kt3, kr3, v3, rt3, qT3, kT3, kx3, o3, sm3, oT3), end = carve(
            BC, 0, [(TILES, D), (TILES, D // 2), (TILES, D), (TILES, KV3 * VP3), (4, TILES * 128),
                    (2, TOK), (2, TOK), (16, TOK), (TILES, MAPS * (VD3 + 1)), (3, 4 * ROWS),
                    (2, 4 * ROWS)])
        assert end <= HEAD + TAIL, end
        (kx3b, p3, pt3), end = carve(RING, 0, [(16, TOK), (2, 4 * ROWS), (3, 4 * ROWS)])
        assert end <= 4 * PIECE
        (at3, sq3, atT3), end = carve(BC, 0, [(TILES, D), (TILES, D), (KD, TOK)])
        assert end <= 3 * TILES * D + 3000

        (rsc, rtmp, rv2, rsel, rw, rt5), _ = carve(
            LATE, 0, [(TILES, 8), (TILES, 8), (TILES, 8), (2 * TILES, 8), (TILES, 8), (TILES, 12)])
        (rwT,), _ = carve(BC, 2 * F2C * TOK + 3 * HALF, [(TOK,)])

        def bc(ap, dims):
            return ap.broadcast_to(dims)

        def four(ap, n):
            return ap.rearrange("p (a b) -> p a b", a=4)[:, :, 0:n]

        def half(a, s):
            return a[:, HALF * s:HALF * (s + 1)]

        def both(bank):
            return PS[:, bank:bank + 2, 0:HALF]

        def halves(ap):
            return ap.rearrange("p (s t) -> p s t", s=2)

        def piece(p):
            if p < 4:
                return RING[:, p * PIECE:(p + 1) * PIECE]
            return BC[:, HEAD + (p - 4) * PIECE:HEAD + (p - 3) * PIECE]

        NORMS = ["n0", "n0f", "n1", "n1f", "n2", "n2b", "n2f", "n3", "n3f"]
        FED = [x for x in NORMS if x != "n2"]

        def nth(L, i=0):
            return TILES * NORMS.index(L) + i + 1

        def nth_T(L, i=0):
            return TILES * FED.index(L) + i + 1

        block = ctx.enter_context(nc.Block())

        @block.sync
        def _(sp):
            loads = {}

            def load(dst, name, s, src=None):
                loads[s] = loads.get(s, 0) + 16
                sp.dma_start(dst, dram[name] if src is None else src).then_inc(sem(s), 16)

            load(cst[:, :], "consts", "ld_const")
            load(pos[0:2 * SEQ, :], "pos", "ld_tok")
            load(patch, "patches", "ld_tok")
            load(w_tok, "w_tok", "ld_tok")
            load(w_qkv0, "w_qkv0", "ld_qkv0")
            load(ids[0:1, :], "ids", "ld_ids")
            load(w_adp[:, :], "w_adp", "ld_adp")
            load(w_acol[0:ADAPT, :], "w_acol", "ld_adp")
            load(w_r0[:, :, :], "w_r0", "ld_f0")
            load(w_cat, "w_cat", "ld_f0")
            load(w_o0, "w_o0", "ld_f0")
            sp.wait_ge(sem("ld_ids"), 16)
            for a in range(ADAPT):
                r = sp.value_load(ids[0:1, a:a + 1], min_val=0, max_val=31)
                sp.dma_start(raw[:, a, :], dram["w_all"][bass.ds(r, 1), :, :].rearrange("a p n -> p (a n)")).then_inc(sem("ld_raw"), 16)
                sp.dma_start(b_adp[a:a + 1, :], dram["b_all"][bass.ds(r, 1), :]).then_inc(sem("ld_badp"), 16)
            load(w_in[:, :, :], "w_in", "ld_m")
            load(w_out[:, :, :], "w_out", "ld_m")
            load(m_small[:, :, :], "m_small", "ld_m")
            load(w_r1[:, :, :], "w_r1", "ld_f1")
            load(w_br[0:1, :], "w_br", "ld_f1")
            load(w_b1[:, :, :], "w_b1", "ld_f1")
            load(w_b2[0:E1, :], "w_b2", "ld_f1")
            load(w_gate[:, :, :], "w_gate", "ld_gate")
            load(w_ln[:, :, :], "w_ln", "ld_ln")
            load(w_q3[:, :, :], "w_q3", "ld_a3")
            load(w_k3[:, :, :], "w_k3", "ld_a3")
            load(w_v3[:, :, :], "w_v3", "ld_a3")
            load(w_o3[:, :, :], "w_o3", "ld_a3")
            load(w_lam[:, :, :], "w_lam", "ld_a3")
            load(w_rms[:, :], "w_rms", "ld_a3")
            if stop >= 4:
                sp.wait_ge(sem("eff"), 1)
                sp.wait_ge(sem("f0_done"), 1)
                for e in range(E1):
                    if e >= 2:
                        sp.wait_ge(sem("f1_z"), 2 * F1C * (e - 1))
                    load(piece(2 * (e % 2))[:, 0:F1C * D], None, f"ld_w1_{e % 2}", dram["w1_1"][e])
                    if e >= 2:
                        sp.wait_ge(sem("f1_y"), TILES * (e - 1))
                    load(piece(2 * (e % 2) + 1)[:, 0:F1C * D], None, f"ld_w2_{e % 2}", dram["w2_1"][e])
                    if e == 3 and stop >= 5:
                        for name, dst in (("w_dq", w_dq), ("w_dkv", w_dkv), ("w_uq", w_uq), ("w_uk", w_uk),
                                          ("w_uv", w_uv), ("w_o2", w_o2)):
                            load(dst, name, "ld_a2")
            if stop >= 6:
                for e in range(E2):
                    for j, name in enumerate(("w1_2", "w3_2", "w2_2")):
                        p = 3 * e + j
                        if p == 0:
                            sp.wait_ge(sem("f1_y"), TILES * E1)
                        if p == 4:
                            sp.wait_ge(sem("a2_done"), 1)
                        if p >= 6:
                            if j == 2:
                                sp.wait_ge(sem("f2_y"), TILES * (e - 1))
                            else:
                                sp.wait_ge(sem("f2_z"), 2 * F2C * (e - 1))
                        load(piece(p % 6), None, f"ld_p{p % 6}", dram[name][e])
            if stop < 8:
                for s, n in loads.items():
                    sp.wait_ge(sem(s), n)
                sp.wait_ge(sem("ld_badp"), 128)
                sp.wait_ge(sem("eff"), 2)
                sp.wait_ge(sem("ld_raw"), 128)
            for i in range(TILES):
                sp.wait_ge(sem("done"), i + 1)
                sp.dma_start(out[T0[i]:T0[i] + N[i], :], h[:N[i], i, :]).then_inc(sem("stored"), 16)
            sp.wait_ge(sem("stored"), 16 * TILES)

        @block.tensor
        def _(pe):
            def mm(dst, lhsT, rhs, start=True, stop=True):
                return nc.tensor.matmul(dst, lhsT, rhs, start=start, stop=stop)

            def norm_T(L):
                for i in range(TILES):
                    pe.wait_ge(sem("norm_xn"), nth(L, i))
                    if i >= 2:
                        pe.wait_ge(sem("norm_xT"), nth_T(L, i - 2))
                    src = yn if L == "n2b" else xn
                    for c in range(KD):
                        last = nc.tensor.transpose(PS[:, i % 2, 128 * c:128 * c + N[i]],
                                                   src[:N[i], i, 128 * c:128 * (c + 1)], ident[:N[i], :N[i]])
                    last.then_inc(sem("norm_tr"), 1)
                pe.wait_ge(sem("norm_xT"), nth_T(L, TILES - 1))

            pe.wait_ge(sem("ld_tok"), 48)
            pe.wait_ge(sem("ld_const"), 16)
            for i in range(TILES):
                o = PS[:N[i], i, 0:D]
                for c in range(PK):
                    mm(o, patch[:, c, T0[i]:T0[i] + N[i]], w_tok[:, c, :], c == 0, False)
                mm(o, const("spread")[0:2 * SEQ, 0:N[i]], pos[0:2 * SEQ, :], False, True).then_inc(sem("t_ps"), 1)

            if stop >= 1:
                norm_T("n0")
                pe.wait_ge(sem("ld_qkv0"), 16)
                for j in range(4):
                    for s in range(2):
                        for c in range(KD):
                            last = mm(PS[:, 2 * j + s, 0:HALF], w_qkv0[:, j // 2, c, 128 * (j % 2):128 * (j % 2) + 128],
                                      half(xT[:, c, :], s), c == 0, c == KD - 1)
                    last.then_inc(sem("a0_qk"), 1)
                for i in range(TILES):
                    if i == 0:
                        pe.wait_ge(sem("a0_q_sb"), 1)
                    if i == 2:
                        pe.wait_ge(sem("a0_k_sb"), 1)
                    if i == 4:
                        pe.wait_ge(sem("a0_q_sb"), 2)
                    for c in range(KD):
                        last = mm(PS[:N[i], i, 0:D], xT[:, c, T0[i]:T0[i] + N[i]], w_qkv0[:, 2, c, :],
                                  c == 0, c == KD - 1)
                    last.then_inc(sem("a0_v"), 1)
                pe.wait_ge(sem("a0_k_sb"), 2)
                for i in range(TILES):
                    pe.wait_ge(sem("a0_v_sb"), i + 1)
                    r = slice(T0[i], T0[i] + N[i])
                    for c in range(KD):
                        last = mm(PS[:N[i], i, 0:N[i]], qk0[:, c, r], qk0[:, 2 + c, r], c == 0, c == KD - 1)
                    last.then_inc(sem("a0_s"), 1)

                def probs_T(i):
                    pe.wait_ge(sem("a0_p"), i + 1)
                    nc.tensor.transpose(PS[:N[i], i, 128:128 + N[i]], p0[:N[i], i, 0:N[i]],
                                        ident[:N[i], :N[i]]).then_inc(sem("a0_t"), 1)

                def mix(i):
                    pe.wait_ge(sem("a0_pt"), i + 1)
                    mm(PS[:N[i], i, 256:512], pt0[:N[i], i, 0:N[i]], v0[:N[i], i, :]).then_inc(sem("a0_o"), 1)

                probs_T(0)
                for i in range(1, TILES):
                    probs_T(i)
                    mix(i - 1)
                mix(TILES - 1)

            if stop >= 2:
                norm_T("n0f")
                pe.wait_ge(sem("ld_f0"), 48)
                for s in range(2):
                    for c in range(KD):
                        last = mm(PS[0:E0, 2 + s, 0:HALF], w_r0[:, c, :], half(xT[:, c, :], s), c == 0, c == KD - 1)
                last.then_inc(sem("f0_lg"), 1)
                pe.wait_ge(sem("f0_sel"), 1)
                for i in range(TILES):
                    for k in range(2):
                        last = nc.tensor.transpose(PS[:N[i], 4, (2 * i + k) * E0:(2 * i + k + 1) * E0],
                                                   sel[0:E0, k, T0[i]:T0[i] + N[i]], ident[0:E0, 0:E0])
                last.then_inc(sem("f0_selT"), 1)
                for i in range(TILES):
                    pe.wait_ge(sem("f0_G"), i + 1)
                    if i >= 2:
                        pe.wait_ge(sem("f0_xg"), i - 1)
                    w = 2 * E0 * WIDTH[i]
                    b = 5 + i % 2
                    for c in range(KD):
                        mm(PS[:, b, 112 * c:112 * c + w], xn[:N[i], i, 128 * c:128 * c + 128], G[:N[i], i, 0:w])
                    mm(PS[0:SEQ, b, 224:224 + w], const("place")[:N[i], :], G[:N[i], i, 0:w]).then_inc(sem("f0_g"), 1)
                pe.wait_ge(sem("f0_xg"), TILES)
                for gk in range(4):
                    g, k = gk // 2, gk % 2
                    for e4 in range(4):
                        e = 4 * g + e4
                        rows = slice(32 * e4, 32 * e4 + 32)
                        slots = slice((k * E0 + e) * BATCH, (k * E0 + e + 1) * BATCH)
                        for c in range(KD):
                            mm(PS[rows, gk, 0:QKVW], xg[:, c, slots], w_cat[:, c, e, :], c == 0, c == KD - 1)
                        last = mm(PS[rows, gk, QKVW:QKVW + 65], poh[0:SEQ, k * E0 + e, :], const("rope0")[0:SEQ, :])
                    last.then_inc(sem("f0_qkv"), 1)
                pe.wait_ge(sem("f0_av"), 1)
                for gk in range(4):
                    last = nc.tensor.transpose(PS[:, 4, 128 * gk:128 * gk + 128], av[:, gk, :], ident)
                last.then_inc(sem("f0_avt"), 1)
                pe.wait_ge(sem("f0_avt_sb"), 1)
                for gk in range(4):
                    for e4 in range(4):
                        last = mm(PS[32 * e4:32 * e4 + 32, gk, 0:D], avt[:, gk, 32 * e4:32 * e4 + 32],
                                  w_o0[:, 4 * (gk // 2) + e4, :])
                    last.then_inc(sem("f0_x"), 1)
                pe.wait_ge(sem("f0_xp"), 4)
                pe.wait_ge(sem("f0_GT"), 4)
                for i in range(TILES):
                    b = 5 + i % 3
                    if i >= 3:
                        pe.wait_ge(sem("f0_h"), i - 2)
                    for gk in range(4):
                        last = mm(PS[:N[i], b, 0:D], GT[:, gk, T0[i]:T0[i] + N[i]], xp[:, gk, :], gk == 0, gk == 3)
                    last.then_inc(sem("f0_out"), 1)

            if stop >= 3:
                norm_T("n1")
                pe.wait_ge(sem("ld_m"), 48)
                for m in range(8):
                    b = 2 * (m % 4)
                    if m >= 4:
                        pe.wait_ge(sem("m_in"), m - 3)
                    for s in range(2):
                        for c in range(KD):
                            last = mm(PS[:, b + s, 0:HALF], w_in[:, c, 128 * m:128 * m + 128], half(xT[:, c, :], s),
                                      c == 0, c == KD - 1)
                    last.then_inc(sem("m_x"), 1)
                for c in range(INNER):
                    b = 2 * (c % 2)
                    if c >= 2:
                        pe.wait_ge(sem("m_t1"), c - 1)
                    if c == 0:
                        pe.wait_ge(sem("m_in"), 8)
                    for q in range(4):
                        pe.wait_ge(sem("m_hs"), 4 * c + q + 1)
                        for j in range(4):
                            for s in range(2):
                                last = mm(PS[:, b + s, 0:HALF], ident, half(hs_ring[:, 4 * ((4 * c + q) % 2) + j, :], s),
                                          q == 0 and j == 0, q == 3 and j == 3)
                        last.then_inc(sem("m_sum"), 1)
                pe.wait_ge(sem("m_y"), INNER)
                for i in range(TILES):
                    b = 4 + i % 4
                    if i >= 4:
                        pe.wait_ge(sem("m_h"), i - 3)
                    for c in range(INNER):
                        last = mm(PS[:N[i], b, 0:D], cv[:, c, T0[i]:T0[i] + N[i]], w_out[:, c, :], c == 0, c == INNER - 1)
                    last.then_inc(sem("m_out"), 1)

            if stop >= 4:
                norm_T("n1f")
                pe.wait_ge(sem("ld_f1"), 64)
                for i in range(TILES):
                    for c in range(KD):
                        mm(PS[:N[i], 6, 8 * i:8 * i + 8], xT[:, c, T0[i]:T0[i] + N[i]], w_r1[:, c, :], c == 0, False)
                    last = mm(PS[:N[i], 6, 8 * i:8 * i + 8], const("one")[0:1, :N[i]], w_br[0:1, :], False, True)
                last.then_inc(sem("f1_sc"), 1)

                def up1(e):
                    pe.wait_ge(sem(f"ld_w1_{e % 2}"), 16 * (e // 2 + 1))
                    w = piece(2 * (e % 2))[:, 0:F1C * D].rearrange("p (c m) -> p c m", c=KD)
                    for c in range(F1C):
                        for s in range(2):
                            u = (e * F1C + c) * 2 + s
                            if u >= 3:
                                pe.wait_ge(sem("f1_h"), u - 2)
                            for k in range(KD):
                                last = mm(PS[:, 2 * (u % 3), 0:HALF], w[:, k, 128 * c:128 * c + 128], half(xT[:, k, :], s),
                                          k == 0, k == KD - 1)
                            last.then_inc(sem("f1_z"), 1)

                def down1(e):
                    pe.wait_ge(sem(f"ld_w2_{e % 2}"), 16 * (e // 2 + 1))
                    pe.wait_ge(sem("f1_h"), 2 * F1C * (e + 1))
                    w = piece(2 * (e % 2) + 1)[:, 0:F1C * D].rearrange("p (c m) -> p c m", c=F1C)
                    for i in range(TILES):
                        n = e * TILES + i
                        if n >= 2:
                            pe.wait_ge(sem("f1_acc"), n - 1)
                        for c in range(F1C):
                            last = mm(PS[:N[i], 6 + n % 2, 0:D], hT[e % 2][:, c, T0[i]:T0[i] + N[i]], w[:, c, :],
                                      c == 0, c == F1C - 1)
                        last.then_inc(sem("f1_y"), 1)

                pe.wait_ge(sem("f1_rs"), 1)
                up1(0)
                for e in range(E1):
                    if e + 1 < E1:
                        up1(e + 1)
                    if e == 0:
                        pe.wait_ge(sem("f1_rw"), 1)
                        for i in range(TILES):
                            nc.tensor.transpose(PS[0:E1, 1 if i < 4 else 3, 128 * (i % 4):128 * (i % 4) + N[i]],
                                                rw[:N[i], i, :], ident[:N[i], :N[i]]).then_inc(sem("f1_rwT"), 1)
                        pe.wait_ge(sem("f1_rwT_sb"), TILES)
                        for i in range(TILES):
                            b = (1, 3, 5)[i % 3]
                            if i >= 3:
                                pe.wait_ge(sem("f1_bh"), i - 2)
                            mm(PS[:N[i], b, 0:D], rwT[0:E1, T0[i]:T0[i] + N[i]], w_b2[0:E1, :]).then_inc(sem("f1_bias"), 1)
                    down1(e)

            if stop >= 5:
                norm_T("n2b")
                pe.wait_ge(sem("ld_a2"), 96)
                for j, w in enumerate((w_dq, w_dkv)):
                    for s in range(2):
                        for c in range(KD):
                            last = mm(PS[:, 2 + 2 * j + s, 0:HALF], w[:, c, :], half(gT[:, c, :], s), c == 0, c == KD - 1)
                    last.then_inc(sem("a2_c"), 1)
                pe.wait_ge(sem("a2_c_sb"), 2)
                for u in range(8):
                    j, pp = u // 4, u % 4
                    b = 4 * (u % 2)
                    if u >= 2:
                        pe.wait_ge(sem("a2_r"), u - 1)
                    for eo in range(2):
                        for s in range(2):
                            last = mm(PS[:, b + 2 * eo + s, 0:HALF], (w_uq, w_uk)[j][:, 2 * pp + eo, :],
                                      half(cT[:, j, :], s))
                    last.then_inc(sem("a2_eo"), 1)
                for i in range(TILES):
                    for g in range(2):
                        n = 2 * i + g
                        if n < 4:
                            pe.wait_ge(sem("a2_r"), 7)
                        elif n < 8:
                            pe.wait_ge(sem("a2_r"), 8)
                        else:
                            pe.wait_ge(sem("a2_v_sb"), n - 7)
                        mm(PS[:N[i], n % 8, :], cT[:, 1, T0[i]:T0[i] + N[i]], w_uv[:, 512 * g:512 * g + 512])\
                            .then_inc(sem("a2_v"), 1)
                pe.wait_ge(sem("a2_v_sb"), 2 * TILES)
                pe.wait_ge(sem("a2_qk_sb"), 16)
                units = 4 * TILES

                def scores2(u):
                    i, g = u // 4, u % 4
                    r = slice(T0[i], T0[i] + N[i])
                    if u >= 2:
                        pe.wait_ge(sem("a2_sm"), u - 1)
                    ro = slice(32 * g, 32 * g + 32)
                    for m in range(4):
                        for eo in range(2):
                            last = mm(PS[:N[i], u % 2, ROWS * m:ROWS * m + N[i]], q2[ro, 2 * m + eo, r],
                                      k2[ro, 2 * m + eo, r], eo == 0, eo == 1)
                    last.then_inc(sem("a2_s"), 1)

                def probs2(u):
                    i = u // 4
                    pe.wait_ge(sem("a2_p"), u + 1)
                    if u >= 2:
                        pe.wait_ge(sem("a2_pt"), u - 1)
                    for hh in range(4):
                        last = nc.tensor.transpose(PS[:N[i], 2 + u % 2, 128 * hh:128 * hh + N[i]],
                                                   p2[:N[i], u % 2, ROWS * hh:ROWS * hh + N[i]], ident[:N[i], :N[i]])
                    last.then_inc(sem("a2_t"), 1)

                def mix2(u):
                    i, g = u // 4, u % 4
                    pe.wait_ge(sem("a2_pt"), u + 1)
                    if u >= 2:
                        pe.wait_ge(sem("a2_osb"), u - 1)
                    w = DH2 + 1
                    for hh in range(4):
                        last = mm(PS[:N[i], 4 + u % 2, w * hh:w * hh + w], pt2[:N[i], u % 2, ROWS * hh:ROWS * hh + N[i]],
                                  v2[:N[i], i, w * (4 * g + hh):w * (4 * g + hh + 1)])
                    last.then_inc(sem("a2_o"), 1)

                def heads_T(u):
                    i, g = u // 4, u % 4
                    pe.wait_ge(sem("a2_osb"), u + 1)
                    if u >= 1:
                        pe.wait_ge(sem("a2_ot"), u)
                    for c in range(2):
                        last = nc.tensor.transpose(PS[:, 6, 128 * c:128 * c + N[i]],
                                                   o2[:N[i], 0, 256 * g + 128 * c:256 * g + 128 * c + 128],
                                                   ident[:N[i], :N[i]])
                    last.then_inc(sem("a2_tr"), 1)
                    if g == 3:
                        pe.wait_ge(sem("a2_ot"), u + 1)
                        if i >= 1:
                            pe.wait_ge(sem("a2_h"), i)
                        for c in range(8):
                            last = mm(PS[:N[i], 7, 0:D], oT2[:, c, 0:N[i]], w_o2[:, c, :], c == 0, c == 7)
                        last.then_inc(sem("a2_out"), 1)

                for u in range(units + 4):
                    if u < units:
                        scores2(u)
                    if 2 <= u <= units + 1:
                        probs2(u - 2)
                    if 3 <= u <= units + 2:
                        mix2(u - 3)
                    if 4 <= u:
                        heads_T(u - 4)

            if stop >= 6:
                norm_T("n2f")
                pe.wait_ge(sem("ld_gate"), 16)
                for i in range(TILES):
                    for c in range(KD):
                        last = mm(PS[:N[i], 6, 8 * i:8 * i + E2], xT[:, c, T0[i]:T0[i] + N[i]], w_gate[:, c, :],
                                  c == 0, c == KD - 1)
                last.then_inc(sem("f2_sc"), 1)

                def arrived(p):
                    pe.wait_ge(sem(f"ld_p{p % 6}"), 16 * (p // 6 + 1))
                    return piece(p % 6)

                def up2(e):
                    w1 = arrived(3 * e).rearrange("p (c m) -> p c m", c=KD)
                    w3 = arrived(3 * e + 1).rearrange("p (c m) -> p c m", c=KD)
                    for c in range(F2C):
                        for s in range(2):
                            u = (e * F2C + c) * 2 + s
                            if u >= 3:
                                pe.wait_ge(sem("f2_h"), u - 2)
                            for j, w in enumerate((w1, w3)):
                                for k in range(KD):
                                    last = mm(PS[:, 2 * (u % 3) + j, 0:HALF], w[:, k, 128 * c:128 * c + 128],
                                              half(xT[:, k, :], s), k == 0, k == KD - 1)
                            last.then_inc(sem("f2_z"), 1)

                def down2(e):
                    w = arrived(3 * e + 2).rearrange("p (c m) -> p c m", c=F2C)
                    pe.wait_ge(sem("f2_h"), 2 * F2C * (e + 1))
                    for i in range(TILES):
                        n = e * TILES + i
                        if n >= 2:
                            pe.wait_ge(sem("f2_acc"), n - 1)
                        for c in range(F2C):
                            last = mm(PS[:N[i], 6 + n % 2, 0:D], hT[e % 2][:, c, T0[i]:T0[i] + N[i]], w[:, c, :],
                                      c == 0, c == F2C - 1)
                        last.then_inc(sem("f2_y"), 1)

                pe.wait_ge(sem("f2_rs"), 1)
                up2(0)
                for e in range(E2):
                    if e + 1 < E2:
                        up2(e + 1)
                    down2(e)

            if stop >= 7:
                norm_T("n3")
                pe.wait_ge(sem("ld_a3"), 96)
                for i in range(TILES):
                    r = slice(T0[i], T0[i] + N[i])
                    b = 2 * (i % 3)
                    if i >= 3:
                        pe.wait_ge(sem("a3_qkv_sb"), i - 2)
                    for o, w in ((PS[:N[i], b, 0:256], w_q3), (PS[:N[i], b + 1, 0:128], w_k3),
                                 (PS[:N[i], b + 1, 128:256], w_v3)):
                        for c in range(KD):
                            last = mm(o, xT[:, c, r], w[:, c, :], c == 0, c == KD - 1)
                    last.then_inc(sem("a3_qkv"), 1)
                pe.wait_ge(sem("a3_qkv_sb"), TILES)
                pe.wait_ge(sem("a3_rope"), 1)
                for i in range(TILES):
                    if i >= 2:
                        pe.wait_ge(sem("a3_qkT"), i - 1)
                    for j, src in enumerate((qt3, kr3)):
                        for c in range(2):
                            last = nc.tensor.transpose(PS[:, i % 2, 256 * j + 128 * c:256 * j + 128 * c + N[i]],
                                                       src[:N[i], i, 128 * c:128 * c + 128], ident[:N[i], :N[i]])
                    last.then_inc(sem("a3_tr"), 1)
                pe.wait_ge(sem("a3_qkT"), TILES)
                pe.wait_ge(sem("a3_kx"), MAPS)
                units = 8 * TILES

                def scores3(u):
                    i, g = u // 8, u % 8
                    r = slice(T0[i], T0[i] + N[i])
                    if u >= 3:
                        pe.wait_ge(sem("a3_sm"), u - 2)
                    kk = kx3[:, 4 * g:4 * g + 4, r] if g < 4 else kx3b[:, 4 * g - 16:4 * g - 12, r]
                    mm(four(PS[:N[i], 1 + u % 3, 0:4 * ROWS], N[i]), qT3[:, g // 4, r], kk).then_inc(sem("a3_s"), 1)

                def probs3(u):
                    i = u // 8
                    pe.wait_ge(sem("a3_p"), u + 1)
                    if u >= 2:
                        pe.wait_ge(sem("a3_pt"), u - 1)
                    for m in range(4):
                        last = nc.tensor.transpose(PS[:N[i], 4 + u % 2, 128 * m:128 * m + N[i]],
                                                   p3[:N[i], u % 2, ROWS * m:ROWS * m + N[i]], ident[:N[i], :N[i]])
                    last.then_inc(sem("a3_t"), 1)

                def mix3(u):
                    i, g = u // 8, u % 8
                    pe.wait_ge(sem("a3_pt"), u + 1)
                    if u % 4 == 0 and u >= 8:
                        pe.wait_ge(sem("a3_oT"), u // 4 - 1)
                    q = 32 * (u % 4)
                    mm(four(PS[q:q + VP3, 6 + u // 4 % 2, 0:4 * ROWS], N[i]), v3[:N[i], i, VP3 * g:VP3 * (g + 1)],
                       four(pt3[:N[i], u % 3, :], N[i])).then_inc(sem("a3_o"), 1)

                def back3(n):
                    i = n // 2
                    pe.wait_ge(sem("a3_oT"), n + 1)
                    if n >= 1:
                        pe.wait_ge(sem("a3_o_sb"), n)
                    for m in range(4):
                        last = nc.tensor.transpose(PS[:N[i], 0, 128 * m:128 * m + 128],
                                                   oT3[:, n % 2, ROWS * m:ROWS * m + N[i]], ident)
                    last.then_inc(sem("a3_back"), 1)

                for u in range(units + 6):
                    if u < units:
                        scores3(u)
                    if 4 <= u <= units + 3:
                        mix3(u - 4)
                    if 2 <= u <= units + 1:
                        probs3(u - 2)
                    if u >= 9 and u % 4 == 1:
                        back3(u // 4 - 2)
                pe.wait_ge(sem("a3_at"), 1)
                for i in range(TILES):
                    if i >= 2:
                        pe.wait_ge(sem("a3_atT"), i - 1)
                    for c in range(KD):
                        last = nc.tensor.transpose(PS[:, i % 2, 128 * c:128 * c + N[i]],
                                                   at3[:N[i], i, 128 * c:128 * c + 128], ident[:N[i], :N[i]])
                    last.then_inc(sem("a3_at_tr"), 1)
                for i in range(TILES):
                    pe.wait_ge(sem("a3_atT"), i + 1)
                    if i >= 2:
                        pe.wait_ge(sem("a3_h"), i - 1)
                    for c in range(KD):
                        last = mm(PS[:N[i], 2 + i % 2, 0:D], atT3[:, c, T0[i]:T0[i] + N[i]], w_o3[:, c, :],
                                  c == 0, c == KD - 1)
                    last.then_inc(sem("a3_out"), 1)

            if stop >= 8:
                norm_T("n3f")
                pe.wait_ge(sem("eff"), 2)
                pe.wait_ge(sem("ld_badp"), 16 * ADAPT)
                for i in range(TILES):
                    b = 2 + i
                    o = PS[:N[i], b, 0:D]
                    for c in range(KD):
                        mm(o, xT[:, c, T0[i]:T0[i] + N[i]], w_eff[:, c, :], c == 0, False)
                    mm(o, w_arep[0:ADAPT, 0:N[i]], b_adp[0:ADAPT, :], False, True).then_inc(sem("f3_y"), 1)

        @block.gpsimd
        def _(pool):
            done = [0]

            def link(ins):
                done[0] += 1
                ins.then_inc(sem("pool_chain"), 1)
                pool.wait_ge(sem("pool_chain"), done[0])

            pool.wait_ge(sem("ld_adp"), 32)
            pool.wait_ge(sem("ld_const"), 16)
            link(nc.gpsimd.tensor_scalar(w_arep[0:ADAPT, :], const("one")[0:ADAPT, 0:ROWS], w_acol[0:ADAPT, 0:1], 1.0,
                                    ALU.mult, ALU.mult))
            pool.wait_ge(sem("ld_raw"), 16 * ADAPT)
            eff = w_eff[:, :, :].rearrange("p a b -> p (a b)")
            tmp = w_tmp[:, :, :].rearrange("p a b -> p (a b)")
            link(nc.gpsimd.tensor_scalar(eff, raw[:, 0, :], w_adp[:, 0:1], 1.0, ALU.mult, ALU.mult))
            for a in range(1, ADAPT):
                link(nc.gpsimd.tensor_scalar(tmp, raw[:, a, :], w_adp[:, a:a + 1], 1.0, ALU.mult, ALU.mult))
                ins = nc.gpsimd.tensor_tensor(eff, eff, tmp, ALU.add)
                if a < ADAPT - 1:
                    link(ins)
            ins.then_inc(sem("eff"), 1)
            pool.wait_ge(sem("eff"), 1)
            nc.gpsimd.memset(w_tmp[:, 0, 0:1], 0.0).then_inc(sem("eff"), 1)

            if stop >= 3:
                pool.wait_ge(sem("f0_done"), 1)
                for c in range(INNER):
                    last = nc.gpsimd.memset(xpad[:, c, :].rearrange("p (b t) -> p b t", b=BATCH)[:, :, 0:3], 0.0)
                last.then_inc(sem("m_pad"), 1)
                for c in range(INNER):
                    pool.wait_ge(sem("m_xc"), c + 1)
                    nc.gpsimd.tensor_tensor(bx[:, c, :], xc[:, c, :], xc[:, c, :], ALU.mult).then_inc(sem("m_bx"), 1)
                for n in range(4 * INNER):
                    pool.wait_ge(sem("m_a"), 4 * (n + 1))
                    sl = a_ring[:, 4 * (n % 2):4 * (n % 2) + 4, :].rearrange("p j (b t) -> p (j b) t", b=BATCH)
                    nc.gpsimd.memset(sl[:, :, 0:1], 0.0).then_inc(sem("m_a0"), 1)
            if stop >= 5:
                for u in range(8):
                    j, pp = u // 4, u % 4
                    pool.wait_ge(sem("a2_r"), u + 1)
                    dst = (q2, k2)[j]
                    t = 4 * (u % 2)
                    nc.gpsimd.tensor_tensor(dst[:, 2 * pp, :], rt2[:, t, :], rt2[:, t + 1, :], ALU.subtract)\
                        .then_inc(sem("a2_qk_sb"), 1)
                    nc.gpsimd.tensor_tensor(dst[:, 2 * pp + 1, :], rt2[:, t + 2, :], rt2[:, t + 3, :], ALU.add)\
                        .then_inc(sem("a2_qk_sb"), 1)
                for u in range(4 * TILES):
                    n = N[u // 4]
                    s = sm2[:n, u % 3, :].rearrange("p (a b) -> p a b", a=4)[:, :, 0:n]
                    pool.wait_ge(sem("a2_mx"), u + 1)
                    nc.gpsimd.tensor_tensor(s, s, bc(o2b[u % 3][:n, :].unsqueeze(2), [n, 4, n]), ALU.subtract)\
                        .then_inc(sem("a2_e"), 1)
            if stop >= 7:
                pool.wait_ge(sem("a3_qkT"), TILES)
                for m in range(1, MAPS, 2):
                    dst = kx3[:, m, :] if m < 16 else kx3b[:, m - 16, :]
                    nc.gpsimd.tensor_scalar(dst, kT3[:, m // 16, :], const("own")[:, m % 16:m % 16 + 1], 1.0,
                                            ALU.mult, ALU.mult).then_inc(sem("a3_kx"), 1)
                for u in range(8 * TILES):
                    n = N[u // 8]
                    s = sm3[:n, u % 3, :].rearrange("p (a b) -> p a b", a=4)[:, :, 0:n]
                    pool.wait_ge(sem("a3_mx"), u + 1)
                    nc.gpsimd.tensor_tensor(s, s, bc(rt5[:n, 1 + u % 3, 0:4].unsqueeze(2), [n, 4, n]), ALU.subtract)\
                        .then_inc(sem("a3_e"), 1)

        @block.scalar
        def _(act):
            A = nc.scalar.activation
            done = [0]

            def link(ins):
                done[0] += 1
                ins.then_inc(sem("act_chain"), 1)
                act.wait_ge(sem("act_chain"), done[0])

            def norm_T(L):
                act.wait_ge(sem("norm_var"), NORMS.index(L) + 1)
                A(std[:ROWS, :], mv[:ROWS, :, 1], ACT.Sqrt, bias=const("eps5")[:ROWS, :]).then_inc(sem("norm_std"), 1)
                for i in range(TILES):
                    act.wait_ge(sem("norm_tr"), nth_T(L, i))
                    src = PS[:, i % 2, 0:256].rearrange("p (c n) -> p c n", c=KD)[:, :, 0:N[i]]
                    if L == "n2b":
                        for c in range(KD):
                            ins = A(gT[:, c, T0[i]:T0[i] + N[i]], src[:, c, :], ACT.Identity,
                                    scale=w_ln[:, 0, c:c + 1], bias=w_ln[:, 1, c:c + 1])
                    else:
                        ins = A(xT[:, :, T0[i]:T0[i] + N[i]], src, ACT.Copy)
                    ins.then_inc(sem("norm_xT"), 1)

            act.wait_ge(sem("ld_const"), 16)
            if stop >= 1:
                norm_T("n0")
                for j in (0, 2):
                    act.wait_ge(sem("a0_qk"), j + 1)
                    A(halves(qk0[:, j, :]), both(2 * j), ACT.Copy).then_inc(sem("a0_q_sb"), 1)

                def exp0(i):
                    act.wait_ge(sem("a0_sm"), i + 1)
                    A(p0[:N[i], i, 0:N[i]], sm0[:N[i], i, 0:N[i]], ACT.Exp, scale=0.0625, bias=mx0[:N[i], i:i + 1],
                      accum_out=sum0[:N[i], i:i + 1]).then_inc(sem("a0_p"), 1)

                def pt0_copy(i):
                    act.wait_ge(sem("a0_t"), i + 1)
                    A(pt0[:N[i], i, 0:N[i]], PS[:N[i], i, 128:128 + N[i]], ACT.Copy).then_inc(sem("a0_pt"), 1)

                exp0(0)
                for i in range(1, TILES):
                    exp0(i)
                    pt0_copy(i - 1)
                pt0_copy(TILES - 1)

            if stop >= 2:
                norm_T("n0f")
                act.wait_ge(sem("f0_lg"), 1)
                A(halves(sg)[0:E0], PS[0:E0, 2:4, 0:HALF], ACT.Sigmoid).then_inc(sem("f0_sg"), 1)
                for i in range(TILES):
                    act.wait_ge(sem("f0_g"), i + 1)
                    w = WIDTH[i]
                    for c in range(KD):
                        ins = A(xg[:, c, :].rearrange("p (ke b) -> p ke b", b=BATCH)[:, :, GROUP * i:GROUP * i + w],
                                PS[:, 5 + i % 2, 112 * c:112 * c + 16 * w].rearrange("p (ke b) -> p ke b", b=w), ACT.Copy)
                    A(poh[0:SEQ, :, GROUP * i:GROUP * i + w],
                      PS[0:SEQ, 5 + i % 2, 224:224 + 16 * w].rearrange("p (a b) -> p a b", b=w), ACT.Copy)\
                        .then_inc(sem("f0_xg"), 1)
                for gk in range(4):
                    act.wait_ge(sem("f0_qkv"), gk + 1)
                    A(qkv[:, gk, :], PS[:, gk, 0:450], ACT.Copy).then_inc(sem("f0_qkv_sb"), 1)
                act.wait_ge(sem("f0_qkv_sb"), 4)
                A(rt[:, 0, 0:4], qkv[:, :, 384], ACT.Sigmoid).then_inc(sem("f0_gate"), 1)
                act.wait_ge(sem("f0_e"), 1)
                A(rt[:, 1, 8:16], rt[:, 1, 0:8], ACT.Exp).then_inc(sem("f0_exp"), 1)
                act.wait_ge(sem("f0_avt"), 1)
                A(avt, PS[:, 4, :].rearrange("p (a b) -> p a b", a=4), ACT.Copy).then_inc(sem("f0_avt_sb"), 1)
                for gk in range(4):
                    act.wait_ge(sem("f0_x"), gk + 1)
                    A(xp[:, gk, :], PS[:, gk, 0:D], ACT.Copy).then_inc(sem("f0_xp"), 1)

            if stop >= 3:
                norm_T("n1")
                act.wait_ge(sem("m_pad"), 1)
                act.wait_ge(sem("ld_m"), 48)
                al = m_small[:, :, 6:6 + STATE]
                for m in range(8):
                    b = 2 * (m % 4)
                    act.wait_ge(sem("m_x"), m + 1)
                    if m < INNER:
                        dst = xpad[:, m, :].rearrange("p (s b t) -> p s b t", s=2, t=SEQ + 3)
                        for s in range(2):
                            ins = A(dst[:, s, :, 3:], PS[:, b + s, 0:HALF].rearrange("p (b t) -> p b t", t=SEQ), ACT.Copy)
                        ins.then_inc(sem("m_in"), 1)
                    else:
                        A(halves(sres[:, m - INNER, :]), both(b), ACT.Silu).then_inc(sem("m_in"), 1)
                for c in range(INNER):
                    act.wait_ge(sem("m_conv"), c + 1)
                    A(xc[:, c, :], cv[:, c, :], ACT.Silu, bias=m_small[:, c, 4:5]).then_inc(sem("m_xc"), 1)
                act.wait_ge(sem("m_abs"), 1)
                A(al, al, ACT.Exp)
                link(A(delta, delta, ACT.Exp))
                A(delta, delta, ACT.Ln, bias=1.0).then_inc(sem("m_ln"), 1)
                act.wait_ge(sem("m_delta"), 1)
                for n in range(4 * INNER):
                    c, q = n // 4, n % 4
                    if n >= 2:
                        act.wait_ge(sem("m_hs"), n - 1)
                    for j in range(4):
                        A(a_ring[:, 4 * (n % 2) + j, :], delta[:, c, :], ACT.Exp,
                          scale=al[:, c, 4 * q + j:4 * q + j + 1]).then_inc(sem("m_a"), 1)

            if stop >= 4:
                norm_T("n1f")
                act.wait_ge(sem("ld_f1"), 64)
                act.wait_ge(sem("f1_d"), 1)
                A(rt5[:ROWS, :, 2], rt5[:ROWS, :, 2], ACT.Exp).then_inc(sem("f1_e"), 1)
                for e in range(E1):
                    if e >= 2:
                        act.wait_ge(sem("f1_y"), TILES * (e - 1))
                    for c in range(F1C):
                        for s in range(2):
                            u = (e * F1C + c) * 2 + s
                            act.wait_ge(sem("f1_z"), u + 1)
                            A(half(hT[e % 2][:, c, :], s), PS[:, 2 * (u % 3), 0:HALF], ACT.Relu,
                              bias=w_b1[:, e, c:c + 1]).then_inc(sem("f1_h"), 1)

            if stop >= 5:
                act.wait_ge(sem("ld_ln"), 16)
                act.wait_ge(sem("norm_var"), NORMS.index("n2") + 1)
                A(std[:ROWS, :], mv[:ROWS, :, 1], ACT.Sqrt, bias=const("eps5")[:ROWS, :]).then_inc(sem("norm_std"), 1)
                norm_T("n2b")
                for j in range(2):
                    act.wait_ge(sem("a2_c"), j + 1)
                    A(halves(cT[:, j, :]), both(2 + 2 * j), ACT.Copy).then_inc(sem("a2_c_sb"), 1)
                for n in range(2 * TILES):
                    i, g = n // 2, n % 2
                    act.wait_ge(sem("a2_v"), n + 1)
                    dst = v2[:N[i], i, 520 * g:520 * g + 520].rearrange("p (a b) -> p a b", b=DH2 + 1)[:, :, 0:DH2]
                    A(dst, PS[:N[i], n % 8, :].rearrange("p (a b) -> p a b", b=DH2), ACT.Copy).then_inc(sem("a2_v_sb"), 1)
                units = 4 * TILES

                def exp2(u):
                    i = u // 4
                    act.wait_ge(sem("a2_e"), u + 1)
                    if u >= 2:
                        act.wait_ge(sem("a2_t"), u - 1)
                    v = lambda b, z: b[:N[i], u % z, :].rearrange("p (a b) -> p a b", a=4)[:, :, 0:N[i]]
                    A(v(p2, 2), v(sm2, 3), ACT.Exp, scale=0.125).then_inc(sem("a2_p"), 1)

                def pt2_copy(u):
                    i = u // 4
                    act.wait_ge(sem("a2_t"), u + 1)
                    if u >= 2:
                        act.wait_ge(sem("a2_o"), u - 1)
                    A(pt2[:N[i], u % 2, :].rearrange("p (a b) -> p a b", a=4)[:, :, 0:N[i]],
                      PS[:N[i], 2 + u % 2, :].rearrange("p (a b) -> p a b", a=4)[:, :, 0:N[i]], ACT.Copy)\
                        .then_inc(sem("a2_pt"), 1)

                def ot2_copy(u):
                    i, g = u // 4, u % 4
                    act.wait_ge(sem("a2_tr"), u + 1)
                    if g == 0 and i >= 1:
                        act.wait_ge(sem("a2_out"), i)
                    A(oT2[:, 2 * g:2 * g + 2, 0:N[i]],
                      PS[:, 6, 0:256].rearrange("p (a b) -> p a b", a=2)[:, :, 0:N[i]], ACT.Copy).then_inc(sem("a2_ot"), 1)

                for u in range(units + 4):
                    if u < units:
                        exp2(u)
                    if 2 <= u <= units + 1:
                        pt2_copy(u - 2)
                    if 4 <= u:
                        ot2_copy(u - 4)

            if stop >= 6:
                norm_T("n2f")
                act.wait_ge(sem("f2_d"), 1)
                A(rsc[:ROWS, :, 0:E2], rsc[:ROWS, :, 0:E2], ACT.Exp).then_inc(sem("f2_e"), 1)
                for u in range(2 * F2C * E2):
                    act.wait_ge(sem("f2_z"), u + 1)
                    if u >= 3:
                        act.wait_ge(sem("f2_h"), u - 2)
                    A(sil[:, u % 3, :], PS[:, 2 * (u % 3), 0:HALF], ACT.Silu).then_inc(sem("f2_s"), 1)

            if stop >= 7:
                norm_T("n3")
                act.wait_ge(sem("ld_a3"), 96)
                act.wait_ge(sem("a3_lam"), 1)
                A(rt5[:, 0, 2:4], rt5[:, 0, 0:2], ACT.Exp).then_inc(sem("a3_lam_e"), 1)
                act.wait_ge(sem("a3_zero"), 1)
                for i in range(TILES):
                    act.wait_ge(sem("a3_qkv"), i + 1)
                    b = 2 * (i % 3)
                    A(qt3[:N[i], i, :], PS[:N[i], b, 0:256], ACT.Copy)
                    A(kt3[:N[i], i, :], PS[:N[i], b + 1, 0:128], ACT.Copy)
                    A(v3[:N[i], i, :].rearrange("p (a b) -> p a b", b=VP3)[:, :, 0:VD3],
                      PS[:N[i], b + 1, 128:256].rearrange("p (a b) -> p a b", b=VD3), ACT.Copy)\
                        .then_inc(sem("a3_qkv_sb"), 1)
                for i in range(TILES):
                    act.wait_ge(sem("a3_tr"), i + 1)
                    s = PS[:, i % 2, :].rearrange("p (a c b) -> p a c b", a=2, c=2)
                    A(qT3[:, :, T0[i]:T0[i] + N[i]], s[:, 0, :, 0:N[i]], ACT.Copy)
                    A(kT3[:, :, T0[i]:T0[i] + N[i]], s[:, 1, :, 0:N[i]], ACT.Copy).then_inc(sem("a3_qkT"), 1)
                units = 8 * TILES

                def exp3(u):
                    i = u // 8
                    act.wait_ge(sem("a3_e"), u + 1)
                    if u >= 2:
                        act.wait_ge(sem("a3_t"), u - 1)
                    v = lambda b, z: b[:N[i], u % z, :].rearrange("p (a b) -> p a b", a=4)[:, :, 0:N[i]]
                    A(v(p3, 2), v(sm3, 3), ACT.Exp, scale=float(HD3) ** -0.5).then_inc(sem("a3_p"), 1)

                def pt3_copy(u):
                    i = u // 8
                    act.wait_ge(sem("a3_t"), u + 1)
                    if u >= 3:
                        act.wait_ge(sem("a3_o"), u - 2)
                    A(pt3[:N[i], u % 3, :].rearrange("p (a b) -> p a b", a=4)[:, :, 0:N[i]],
                      PS[:N[i], 4 + u % 2, :].rearrange("p (a b) -> p a b", a=4)[:, :, 0:N[i]], ACT.Copy)\
                        .then_inc(sem("a3_pt"), 1)

                def oT3_copy(n):
                    i = n // 2
                    act.wait_ge(sem("a3_o"), 4 * (n + 1))
                    if n >= 2:
                        act.wait_ge(sem("a3_back"), n - 1)
                    A(four(oT3[:, n % 2, :], N[i]), four(PS[:, 6 + n % 2, 0:4 * ROWS], N[i]), ACT.Copy)\
                        .then_inc(sem("a3_oT"), 1)

                for u in range(units + 4):
                    if u < units:
                        exp3(u)
                    if 2 <= u <= units + 1:
                        pt3_copy(u - 2)
                    if u >= 7 and u % 4 == 3:
                        oT3_copy(u // 4 - 1)
                act.wait_ge(sem("a3_ms"), 1)
                rr, root = [rt3[:ROWS, z, 0:TILES * H3] for z in (0, 2)]
                A(root, rr, ACT.Sqrt, bias=const("eps6")[:ROWS, :], scale=1.0 / VD3).then_inc(sem("a3_rms"), 1)
                for i in range(TILES):
                    act.wait_ge(sem("a3_at_tr"), i + 1)
                    A(atT3[:, :, T0[i]:T0[i] + N[i]],
                      PS[:, i % 2, 0:256].rearrange("p (c n) -> p c n", c=KD)[:, :, 0:N[i]], ACT.Copy)\
                        .then_inc(sem("a3_atT"), 1)
            if stop >= 8:
                norm_T("n3f")

        @block.vector
        def _(dve):
            V = nc.vector
            done = [0]

            def link(ins):
                done[0] += 1
                ins.then_inc(sem("dve_chain"), 1)
                dve.wait_ge(sem("dve_chain"), done[0])

            def norm(L, src, dst):
                for i in range(TILES):
                    ins = V.bn_stats(st[:N[i], i, :], src[:N[i], i, :])
                link(ins)
                for i in range(TILES):
                    ins = V.bn_aggr(mv[:N[i], i, :], st[:N[i], i, :])
                ins.then_inc(sem("norm_var"), 1)
                dve.wait_ge(sem("norm_std"), NORMS.index(L) + 1)
                link(V.reciprocal(rstd[:ROWS, :], std[:ROWS, :]))
                for i in range(TILES):
                    V.tensor_scalar(dst[:N[i], i, :], src[:N[i], i, :], mv[:N[i], i, 0:1], rstd[:N[i], i:i + 1],
                                    ALU.subtract, ALU.mult).then_inc(sem("norm_xn"), 1)

            def top2(vals, rank, m, r, tmp, v2, sels):
                P, g, n = vals.shape
                for k in range(2):
                    src = vals if k == 0 else v2
                    link(V.tensor_reduce(m[k], src, AX.X, ALU.max))
                    link(V.tensor_tensor(tmp, src, bc(m[k].unsqueeze(2), [P, g, n]), ALU.is_equal))
                    link(V.tensor_tensor(tmp, tmp, bc(rank.unsqueeze(1), [P, g, n]), ALU.mult))
                    link(V.tensor_reduce(r, tmp, AX.X, ALU.max))
                    link(V.tensor_tensor(sels[k], tmp, bc(r.unsqueeze(2), [P, g, n]), ALU.is_equal))
                    if k == 0:
                        link(V.tensor_scalar(tmp, sels[0], -1.0, 1.0, ALU.mult, ALU.add))
                        link(V.tensor_tensor(v2, vals, tmp, ALU.mult))
                        link(V.tensor_tensor(v2, v2, sels[0], ALU.subtract))

            def add_out(ready, freed, banks):
                for i in range(TILES):
                    dve.wait_ge(sem(ready), i + 1)
                    ins = V.tensor_tensor(h[:N[i], i, :], PS[:N[i], banks[i], 0:D], h[:N[i], i, :], ALU.add)
                    ins.then_inc(sem(freed), 1)
                dve.wait_ge(sem(freed), TILES)

            V.memset(mv[:, :, :], 1.0)
            link(V.memset(misc[:, D:900], 0.0))

            for i in range(TILES):
                dve.wait_ge(sem("t_ps"), i + 1)
                ins = V.tensor_copy(h[:N[i], i, :], PS[:N[i], i, 0:D])
            link(ins)

            if stop >= 1:
                norm("n0", h, xn)
                for j in (1, 3):
                    dve.wait_ge(sem("a0_qk"), j + 1)
                    V.tensor_copy(halves(qk0[:, j, :]), both(2 * j)).then_inc(sem("a0_k_sb"), 1)
                for i in range(TILES):
                    dve.wait_ge(sem("a0_v"), i + 1)
                    V.tensor_copy(v0[:N[i], i, :], PS[:N[i], i, 0:D]).then_inc(sem("a0_v_sb"), 1)
                for i in range(TILES):
                    n = N[i]
                    dve.wait_ge(sem("a0_s"), i + 1)
                    link(V.tensor_tensor(sm0[:n, i, 0:n], PS[:n, i, 0:n], const("causal")[:n, 0:n], ALU.add))
                    link(V.tensor_reduce(mx0[:n, i:i + 1], sm0[:n, i, 0:n], AX.X, ALU.max))
                    V.tensor_scalar(mx0[:n, i:i + 1], mx0[:n, i:i + 1], -0.0625, None, ALU.mult).then_inc(sem("a0_sm"), 1)
                for i in range(TILES):
                    n = N[i]
                    dve.wait_ge(sem("a0_o"), i + 1)
                    link(V.reciprocal(sum0[:n, TILES + i:TILES + i + 1], sum0[:n, i:i + 1]))
                    ins = V.scalar_tensor_tensor(h[:n, i, :], PS[:n, i, 256:512], sum0[:n, TILES + i:TILES + i + 1],
                                                 h[:n, i, :], ALU.mult, ALU.add)
                link(ins)

            if stop >= 2:
                norm("n0f", h, xn)
                dve.wait_ge(sem("f0_sg"), 1)
                three = lambda a: a[0:E0].rearrange("p (b t) -> p b t", t=SEQ)
                top2(three(sg), const("rank17")[0:E0, :], [m8[0:E0, 0, :], m8[0:E0, 1, :]], r8[0:E0, :],
                     three(t8a), three(t8b), [three(sel[:, 0, :]), three(sel[:, 1, :])])
                V.memset(r8[0:E0, 0:1], 0.0).then_inc(sem("f0_sel"), 1)
                dve.wait_ge(sem("f0_selT"), 1)
                for i in range(TILES):
                    n, w = N[i], WIDTH[i]
                    V.tensor_tensor(G[:n, i, 0:16 * w].rearrange("p (a b) -> p a b", b=w),
                                    bc(PS[:n, 4, 16 * i:16 * i + 16].unsqueeze(2), [n, 16, w]),
                                    bc(const("image")[:n, 0:w].unsqueeze(1), [n, 16, w]), ALU.mult)\
                        .then_inc(sem("f0_G"), 1)
                dve.wait_ge(sem("f0_qkv_sb"), 4)
                q4 = qkv[:, :, 0:256].rearrange("p g (j d) -> p g j d", j=2)
                x1, x2 = q4[:, :, :, 0:ROT], q4[:, :, :, ROT:2 * ROT]
                cos = bc(qkv[:, :, 385:385 + ROT].unsqueeze(2), [128, 4, 2, ROT])
                sin = bc(qkv[:, :, 417:417 + ROT].unsqueeze(2), [128, 4, 2, ROT])
                ra, rb, rc, rd = [rt[:, 2 + z, :].rearrange("p (g j d) -> p g j d", g=4, j=2) for z in range(4)]
                V.tensor_tensor(ra, x1, cos, ALU.mult)
                V.tensor_tensor(rb, x2, sin, ALU.mult)
                V.tensor_tensor(rc, x2, cos, ALU.mult)
                link(V.tensor_tensor(rd, x1, sin, ALU.mult))
                V.tensor_tensor(x1, ra, rb, ALU.subtract)
                link(V.tensor_tensor(x2, rc, rd, ALU.add))
                s8 = rt[:, 1, 0:8]
                for g in range(2):
                    gk = slice(2 * g, 2 * g + 2)
                    link(V.tensor_tensor(prod.rearrange("p (k m d) -> p k m d", k=2, m=2),
                                         bc(qkv[:, gk, 0:128].unsqueeze(2), [128, 2, 2, 128]),
                                         bc(qkv[:, gk, 128:256].unsqueeze(1), [128, 2, 2, 128]), ALU.mult))
                    link(V.tensor_reduce(s8[:, 4 * g:4 * g + 4], prod.rearrange("p (a d) -> p a d", a=4),
                                         AX.X, ALU.add))
                pos4 = qkv[:, :, 449].rearrange("p (g k) -> p g k", g=2)
                al = rt[:, 1, 16:24].rearrange("p (g k m) -> p g k m", g=2, k=2)
                link(V.tensor_tensor(al, bc(pos4.unsqueeze(3), [128, 2, 2, 2]), bc(pos4.unsqueeze(2), [128, 2, 2, 2]),
                                     ALU.is_ge))
                link(V.tensor_scalar(rt[:, 1, 16:24], rt[:, 1, 16:24], -MASKED, MASKED, ALU.mult, ALU.add))
                link(V.scalar_tensor_tensor(s8, s8, float(HP) ** -0.5, rt[:, 1, 16:24], ALU.mult, ALU.add))
                s42 = s8.rearrange("p (a m) -> p a m", m=2)
                mx = rt[:, 1, 24:28]
                link(V.tensor_reduce(mx, s42, AX.X, ALU.max))
                V.tensor_tensor(s42, s42, bc(mx.unsqueeze(2), [128, 4, 2]), ALU.subtract).then_inc(sem("f0_e"), 1)
                dve.wait_ge(sem("f0_exp"), 1)
                e42 = rt[:, 1, 8:16].rearrange("p (a m) -> p a m", m=2)
                link(V.tensor_reduce(rt[:, 1, 28:32], e42, AX.X, ALU.add))
                link(V.reciprocal(rt[:, 1, 28:32], rt[:, 1, 28:32]))
                dve.wait_ge(sem("f0_gate"), 1)
                link(V.tensor_tensor(rt[:, 1, 28:32], rt[:, 1, 28:32], rt[:, 0, 0:4], ALU.mult))
                link(V.tensor_tensor(e42, e42, bc(rt[:, 1, 28:32].unsqueeze(2), [128, 4, 2]), ALU.mult))
                for gk in range(4):
                    V.tensor_scalar(av[:, gk, :], qkv[:, 2 * (gk // 2), 256:384], rt[:, 1, 8 + 2 * gk:9 + 2 * gk], None, ALU.mult)
                link(V.memset(rt[:, 0, 8:9], 0.0))
                for gk in range(4):
                    ins = V.scalar_tensor_tensor(av[:, gk, :], qkv[:, 2 * (gk // 2) + 1, 256:384],
                                                 rt[:, 1, 9 + 2 * gk:10 + 2 * gk], av[:, gk, :], ALU.mult, ALU.add)
                ins.then_inc(sem("f0_av"), 1)
                link(V.tensor_scalar(rt[:, 0, 4:8], qkv[:, :, 449], const("first"), None, ALU.add))
                for gk in range(4):
                    V.tensor_scalar(GT[:, gk, :], const("token"), rt[:, 0, 4 + gk:5 + gk], None, ALU.is_equal)\
                        .then_inc(sem("f0_GT"), 1)
                add_out("f0_out", "f0_h", [5 + i % 3 for i in range(TILES)])
                V.memset(flag[:, 0:1], 0.0).then_inc(sem("f0_done"), 1)

            if stop >= 3:
                norm("n1", h, xn)
                dve.wait_ge(sem("ld_m"), 48)
                al = m_small[:, :, 6:6 + STATE]
                link(V.tensor_scalar(al, al, 80.0, None, ALU.min))
                for c in range(INNER):
                    dve.wait_ge(sem("m_in"), c + 1)
                    xp_c = xpad[:, c, :].rearrange("p (b t) -> p b t", b=BATCH)
                    o = cv[:, c, :].rearrange("p (b t) -> p b t", b=BATCH)
                    link(V.tensor_scalar(o, xp_c[:, :, 0:SEQ], m_small[:, c, 0:1], None, ALU.mult))
                    for k in range(1, 4):
                        ins = V.scalar_tensor_tensor(o, xp_c[:, :, k:k + SEQ], m_small[:, c, k:k + 1], o,
                                                     ALU.mult, ALU.add)
                        if k < 3:
                            link(ins)
                    ins.then_inc(sem("m_conv"), 1)
                for c in range(INNER):
                    dve.wait_ge(sem("m_xc"), c + 1)
                    ins = V.scalar_tensor_tensor(delta[:, c, :], xc[:, c, :], -1.0, xc[:, c, :], ALU.mult, ALU.min)
                ins.then_inc(sem("m_abs"), 1)
                dve.wait_ge(sem("m_ln"), 1)
                link(V.tensor_scalar(al, al, -1.0, None, ALU.mult))
                V.scalar_tensor_tensor(delta, xc, 0.0, delta, ALU.max, ALU.add).then_inc(sem("m_delta"), 1)

                def gate_y(c):
                    b = 2 * (c % 2)
                    dve.wait_ge(sem("m_sum"), 4 * (c + 1))
                    V.tensor_tensor(halves(cv[:, c, :]), both(b), halves(xc[:, c, :]), ALU.mult).then_inc(sem("m_t1"), 1)
                    dve.wait_ge(sem("m_t1"), c + 1)
                    link(V.tensor_tensor(cv[:, c, :], cv[:, c, :], sres[:, c, :], ALU.mult))
                    V.scalar_tensor_tensor(cv[:, c, :], xc[:, c, :], m_small[:, c, 5:6], cv[:, c, :],
                                           ALU.mult, ALU.add).then_inc(sem("m_y"), 1)

                dve.wait_ge(sem("m_bx"), INNER)
                dve.wait_ge(sem("m_in"), 8)
                for n in range(4 * INNER):
                    c = n // 4
                    dve.wait_ge(sem("m_a0"), n + 1)
                    if n >= 2:
                        dve.wait_ge(sem("m_sum"), n - 1)
                    for j in range(4):
                        ins = V.tensor_tensor_scan(hs_ring[:, 4 * (n % 2) + j, :], a_ring[:, 4 * (n % 2) + j, :],
                                                   bx[:, c, :], 0.0, ALU.mult, ALU.add)
                    ins.then_inc(sem("m_hs"), 1)
                    if n % 4 == 1 and c >= 1:
                        gate_y(c - 1)
                gate_y(INNER - 1)
                add_out("m_out", "m_h", [4 + i % 4 for i in range(TILES)])

            if stop >= 4:
                norm("n1f", h, xn)
                R = slice(0, ROWS)
                dve.wait_ge(sem("f1_sc"), 1)
                for i in range(TILES):
                    ins = V.tensor_scalar(rsc[:N[i], i, :], PS[:N[i], 6, 8 * i:8 * i + 8], 0.0, None, ALU.max)
                ins.then_inc(sem("f1_rs"), 1)
                dve.wait_ge(sem("f1_rs"), 1)
                sels = [rsel[R, 0:TILES, :], rsel[R, TILES:2 * TILES, :]]
                m = [rt5[R, :, 0], rt5[R, :, 1]]
                top2(rsc[R], const("rank8")[R, :], m, rt5[R, :, 3], rtmp[R], rv2[R], sels)
                V.tensor_tensor(rt5[R, :, 2], m[1], m[0], ALU.subtract).then_inc(sem("f1_d"), 1)
                dve.wait_ge(sem("f1_e"), 1)
                link(V.tensor_scalar(rt5[R, :, 4], rt5[R, :, 2], 1.0, None, ALU.add))
                link(V.reciprocal(rt5[R, :, 4], rt5[R, :, 4]))
                link(V.tensor_tensor(rt5[R, :, 5], rt5[R, :, 2], rt5[R, :, 4], ALU.mult))
                w3d = lambda a: bc(a.unsqueeze(2), [ROWS, TILES, 8])
                link(V.tensor_tensor(rtmp[R], sels[0], w3d(rt5[R, :, 4]), ALU.mult))
                link(V.tensor_tensor(rv2[R], sels[1], w3d(rt5[R, :, 5]), ALU.mult))
                V.tensor_tensor(rw[R], rtmp[R], rv2[R], ALU.add).then_inc(sem("f1_rw"), 1)
                for i in range(TILES):
                    dve.wait_ge(sem("f1_rwT"), TILES)
                    V.tensor_copy(rwT[0:E1, T0[i]:T0[i] + N[i]],
                                  PS[0:E1, 1 if i < 4 else 3, 128 * (i % 4):128 * (i % 4) + N[i]]).then_inc(sem("f1_rwT_sb"), 1)
                for i in range(TILES):
                    dve.wait_ge(sem("f1_bias"), i + 1)
                    V.tensor_tensor(h[:N[i], i, :], PS[:N[i], (1, 3, 5)[i % 3], 0:D], h[:N[i], i, :], ALU.add)\
                        .then_inc(sem("f1_bh"), 1)
                dve.wait_ge(sem("f1_bh"), TILES)
                for n in range(E1 * TILES):
                    e, i = n // TILES, n % TILES
                    dve.wait_ge(sem("f1_y"), n + 1)
                    V.scalar_tensor_tensor(h[:N[i], i, :], PS[:N[i], 6 + n % 2, 0:D], rw[:N[i], i, e:e + 1],
                                           h[:N[i], i, :], ALU.mult, ALU.add).then_inc(sem("f1_acc"), 1)
                dve.wait_ge(sem("f1_acc"), E1 * TILES)

            if stop >= 5:
                norm("n2", h, xn)
                dve.wait_ge(sem("norm_xn"), nth("n2", TILES - 1))
                norm("n2b", xn, yn)
                for i in range(TILES):
                    ins = V.tensor_tensor(h[:N[i], i, :], h[:N[i], i, :], xn[:N[i], i, :], ALU.add)
                link(ins)
                v4 = v2.rearrange("p i (a b) -> p (i a) b", b=DH2 + 1)
                V.memset(v4[:, :, DH2:DH2 + 1], 1.0)
                cos = bc(const("cos2").unsqueeze(1), [128, 16, SEQ])
                sin = bc(const("sin2").unsqueeze(1), [128, 16, SEQ])
                for u in range(8):
                    b = 4 * (u % 2)
                    t = 4 * (u % 2)
                    dve.wait_ge(sem("a2_eo"), u + 1)
                    if u >= 2:
                        dve.wait_ge(sem("a2_qk_sb"), 2 * (u - 1))
                    for z, (eo, tab) in enumerate(((0, cos), (1, sin), (0, sin), (1, cos))):
                        for s in range(2):
                            ins = V.tensor_tensor(half(rt2[:, t + z, :], s).rearrange("p (b t) -> p b t", t=SEQ),
                                                  PS[:, b + 2 * eo + s, 0:HALF].rearrange("p (b t) -> p b t", t=SEQ),
                                                  tab, ALU.mult)
                    ins.then_inc(sem("a2_r"), 1)
                units = 4 * TILES

                def soft2(u):
                    i = u // 4
                    n = N[i]
                    dve.wait_ge(sem("a2_s"), u + 1)
                    if u >= 3:
                        dve.wait_ge(sem("a2_p"), u - 2)
                    if u == 0:
                        dve.wait_ge(sem("a2_qk_sb"), 16)
                    s = sm2[:n, u % 3, :].rearrange("p (a b) -> p a b", a=4)[:, :, 0:n]
                    V.tensor_tensor(s, PS[:n, u % 2, 0:4 * ROWS].rearrange("p (a b) -> p a b", a=4)[:, :, 0:n],
                                    bc(const("block")[:n, 0:n].unsqueeze(1), [n, 4, n]), ALU.add).then_inc(sem("a2_sm"), 1)
                    dve.wait_ge(sem("a2_sm"), u + 1)
                    V.tensor_reduce(o2b[u % 3][:n, :], s, AX.X, ALU.max).then_inc(sem("a2_mx"), 1)

                def norm2(u):
                    i, g = u // 4, u % 4
                    n = N[i]
                    dve.wait_ge(sem("a2_o"), u + 1)
                    if u >= 4:
                        dve.wait_ge(sem("a2_tr"), u - 3)
                    s = PS[:n, 4 + u % 2, 0:4 * (DH2 + 1)].rearrange("p (a b) -> p a b", a=4)
                    link(V.reciprocal(o2b[3 + u % 2][:n, :], s[:, :, DH2]))
                    V.tensor_tensor(o2[:n, 0, 256 * g:256 * g + 256].rearrange("p (a b) -> p a b", a=4), s[:, :, 0:DH2],
                                    bc(o2b[3 + u % 2][:n, :].unsqueeze(2), [n, 4, DH2]), ALU.mult).then_inc(sem("a2_osb"), 1)

                def out2(i):
                    dve.wait_ge(sem("a2_out"), i + 1)
                    V.tensor_tensor(h[:N[i], i, :], PS[:N[i], 7, 0:D], h[:N[i], i, :], ALU.add).then_inc(sem("a2_h"), 1)

                for u in range(units + 4):
                    if u < units:
                        soft2(u)
                    if 3 <= u <= units + 2:
                        norm2(u - 3)
                    if 4 <= u and u % 4 == 3 and u >= 7:
                        out2(u // 4 - 1)
                dve.wait_ge(sem("a2_h"), TILES)
                V.memset(flag[:, 1:2], 0.0).then_inc(sem("a2_done"), 1)

            if stop >= 6:
                norm("n2f", h, xn)
                R = slice(0, ROWS)
                lg = rsc[R, :, 0:E2]
                w3d = lambda a: bc(a.unsqueeze(2), [ROWS, TILES, E2])
                dve.wait_ge(sem("f2_sc"), 1)
                for i in range(TILES):
                    ins = V.tensor_copy(rsc[:N[i], i, 0:E2], PS[:N[i], 6, 8 * i:8 * i + E2])
                ins.then_inc(sem("f2_rs"), 1)
                dve.wait_ge(sem("f2_rs"), 1)
                link(V.tensor_reduce(rt5[R, :, 0], lg, AX.X, ALU.max))
                V.tensor_tensor(lg, lg, w3d(rt5[R, :, 0]), ALU.subtract).then_inc(sem("f2_d"), 1)
                dve.wait_ge(sem("f2_e"), 1)
                link(V.tensor_reduce(rt5[R, :, 1], lg, AX.X, ALU.add))
                link(V.reciprocal(rt5[R, :, 1], rt5[R, :, 1]))
                link(V.tensor_tensor(lg, lg, w3d(rt5[R, :, 1]), ALU.mult))
                sels = [rsel[R, 0:TILES, 0:E2], rsel[R, TILES:2 * TILES, 0:E2]]
                m = [rt5[R, :, 0], rt5[R, :, 1]]
                top2(lg, const("rank8")[R, 0:E2], m, rt5[R, :, 3], rtmp[R, :, 0:E2], rv2[R, :, 0:E2], sels)
                link(V.tensor_tensor(rt5[R, :, 4], m[0], m[1], ALU.add))
                link(V.reciprocal(rt5[R, :, 4], rt5[R, :, 4]))
                link(V.tensor_tensor(rt5[R, :, 5], m[0], rt5[R, :, 4], ALU.mult))
                link(V.tensor_tensor(rt5[R, :, 6], m[1], rt5[R, :, 4], ALU.mult))
                link(V.tensor_tensor(rtmp[R, :, 0:E2], sels[0], w3d(rt5[R, :, 5]), ALU.mult))
                link(V.tensor_tensor(rv2[R, :, 0:E2], sels[1], w3d(rt5[R, :, 6]), ALU.mult))
                link(V.tensor_tensor(rw[R, :, 0:E2], rtmp[R, :, 0:E2], rv2[R, :, 0:E2], ALU.add))

                def prod2(e):
                    if e >= 2:
                        dve.wait_ge(sem("f2_y"), TILES * (e - 1))
                    for c in range(F2C):
                        for s in range(2):
                            u = (e * F2C + c) * 2 + s
                            dve.wait_ge(sem("f2_s"), u + 1)
                            V.tensor_tensor(half(hT[e % 2][:, c, :], s), sil[:, u % 3, :],
                                            PS[:, 2 * (u % 3) + 1, 0:HALF], ALU.mult).then_inc(sem("f2_h"), 1)

                def acc2(e):
                    for i in range(TILES):
                        n = e * TILES + i
                        dve.wait_ge(sem("f2_y"), n + 1)
                        V.scalar_tensor_tensor(h[:N[i], i, :], PS[:N[i], 6 + n % 2, 0:D], rw[:N[i], i, e:e + 1],
                                               h[:N[i], i, :], ALU.mult, ALU.add).then_inc(sem("f2_acc"), 1)
                    dve.wait_ge(sem("f2_acc"), TILES * (e + 1))

                prod2(0)
                for e in range(E2):
                    if e + 1 < E2:
                        prod2(e + 1)
                    acc2(e)

            if stop >= 7:
                norm("n3", h, xn)
                dve.wait_ge(sem("ld_a3"), 96)
                lt = rt5[:, 0, :]
                link(V.tensor_tensor(w_lam[:, 0:3:2, :], w_lam[:, 0:3:2, :], w_lam[:, 1:4:2, :], ALU.mult))
                V.tensor_reduce(lt[:, 0:2], w_lam[:, 0:3:2, :], AX.X, ALU.add).then_inc(sem("a3_lam"), 1)
                dve.wait_ge(sem("a3_lam_e"), 1)
                link(V.tensor_tensor(lt[:, 4:5], lt[:, 2:3], lt[:, 3:4], ALU.subtract))
                link(V.tensor_scalar(lt[:, 4:5], lt[:, 4:5], LAMBDA_INIT, None, ALU.add))
                V.memset(v3.rearrange("p i (a b) -> p (i a) b", b=VP3)[:, :, VD3:VP3], 1.0)
                V.memset(qt3[64:128, TILES - 1, :], 0.0)
                V.memset(kt3[64:128, TILES - 1, :], 0.0)
                V.memset(o3[64:128, TILES - 1, :], 1.0).then_inc(sem("a3_zero"), 1)
                dve.wait_ge(sem("a3_zero"), 1)
                dve.wait_ge(sem("a3_qkv_sb"), TILES)
                HR = HD3 // 2
                for src, dst, n, rep in ((qt3, qt3, 32, 1), (kt3, kr3, 16, 2)):
                    G3 = TILES * n
                    flat = src.rearrange("p i (m d) -> p (i m) d", d=HD3)[:ROWS]
                    x1, x2 = flat[:, :, 0:HR], flat[:, :, HR:HD3]
                    cos = bc(const("cos3")[:ROWS].unsqueeze(1), [ROWS, G3, HR])
                    sin = bc(const("sin3")[:ROWS].unsqueeze(1), [ROWS, G3, HR])
                    t = [rt3[:ROWS, z, 0:G3 * HR].rearrange("p (m d) -> p m d", d=HR) for z in range(4)]
                    V.tensor_tensor(t[0], x1, cos, ALU.mult)
                    V.tensor_tensor(t[1], x2, sin, ALU.mult)
                    V.tensor_tensor(t[2], x2, cos, ALU.mult)
                    link(V.tensor_tensor(t[3], x1, sin, ALU.mult))
                    if rep == 1:
                        V.tensor_tensor(x1, t[0], t[1], ALU.add)
                        link(V.tensor_tensor(x2, t[2], t[3], ALU.subtract))
                    else:
                        for r in range(rep):
                            o = dst.rearrange("p i (v r w) -> p (i v) r w", r=2, w=2 * HD3)[:ROWS, :, r, :]\
                                .rearrange("p v (w d) -> p v w d", w=2)
                            tt = [z.rearrange("p (v w) d -> p v w d", w=2) for z in t]
                            V.tensor_tensor(o[:, :, :, 0:HR], tt[0], tt[1], ALU.add)
                            ins = V.tensor_tensor(o[:, :, :, HR:HD3], tt[2], tt[3], ALU.subtract)
                        ins.then_inc(sem("a3_rope"), 1)
                dve.wait_ge(sem("a3_qkT"), TILES)
                for m in range(0, MAPS, 2):
                    dst = kx3[:, m, :] if m < 16 else kx3b[:, m - 16, :]
                    V.tensor_scalar(dst, kT3[:, m // 16, :], const("own")[:, m % 16:m % 16 + 1], None, ALU.mult)\
                        .then_inc(sem("a3_kx"), 1)
                units = 8 * TILES

                def o3_copy(k):
                    i, G = k // 2, k % 2
                    w = 16 * (VD3 + 1)
                    dve.wait_ge(sem("a3_back"), k + 1)
                    V.tensor_copy(o3[:N[i], i, w * G:w * G + w].rearrange("p (q m d) -> p m q d", q=4, m=4),
                                  PS[:N[i], 0, :].rearrange("p (m q d) -> p m q d", m=4, q=4)[:, :, :, 0:VD3 + 1])\
                        .then_inc(sem("a3_o_sb"), 1)

                for u in range(units):
                    if u >= 10 and u % 4 == 2:
                        o3_copy(u // 4 - 2)
                    n = N[u // 8]
                    dve.wait_ge(sem("a3_s"), u + 1)
                    if u >= 3:
                        dve.wait_ge(sem("a3_p"), u - 2)
                    s = sm3[:n, u % 3, :].rearrange("p (a b) -> p a b", a=4)[:, :, 0:n]
                    V.tensor_tensor(s, PS[:n, 1 + u % 3, 0:4 * ROWS].rearrange("p (a b) -> p a b", a=4)[:, :, 0:n],
                                    bc(const("causal")[:n, 0:n].unsqueeze(1), [n, 4, n]), ALU.add).then_inc(sem("a3_sm"), 1)
                    dve.wait_ge(sem("a3_sm"), u + 1)
                    V.tensor_reduce(rt5[:n, 1 + u % 3, 0:4], s, AX.X, ALU.max).then_inc(sem("a3_mx"), 1)
                for k in range(units // 4 - 2, units // 4):
                    o3_copy(k)
                dve.wait_ge(sem("a3_o_sb"), units // 4)
                M5 = TILES * H3
                W1 = VD3 + 1
                ov = o3.rearrange("p i (m d) -> p (i m) d", d=W1)[:ROWS]
                rs = rt3[:ROWS, 0, 0:2 * M5]
                link(V.reciprocal(rs, ov[:, :, VD3]))
                rs2 = rs.rearrange("p (m w) -> p m w", w=2)
                link(V.tensor_scalar(rs2[:, :, 1], rs2[:, :, 1], lt[:ROWS, 4:5], None, ALU.mult))
                link(V.tensor_tensor(ov[:, :, 0:VD3], ov[:, :, 0:VD3], bc(rs.unsqueeze(2), [ROWS, 2 * M5, VD3]), ALU.mult))
                o4 = o3.rearrange("p i (m w d) -> p (i m) w d", w=2, d=W1)[:ROWS]
                a3 = at3.rearrange("p i (m d) -> p (i m) d", d=VD3)[:ROWS]
                s3 = sq3.rearrange("p i (m d) -> p (i m) d", d=VD3)[:ROWS]
                link(V.tensor_tensor(a3, o4[:, :, 0, 0:VD3], o4[:, :, 1, 0:VD3], ALU.subtract))
                rr, big, fac = [rt3[:ROWS, z, 0:M5] for z in range(3)]
                link(V.tensor_reduce(big, a3, AX.X, ALU.max, apply_absolute_value=True))
                link(V.tensor_scalar(big, big, 2.0 ** 60, None, ALU.is_gt))
                link(V.tensor_scalar(fac, big, 2.0 ** -40 - 1.0, 1.0, ALU.mult, ALU.add))
                link(V.tensor_scalar(fac, fac, 2.0 ** -40, None, ALU.max))
                link(V.tensor_tensor(a3, a3, bc(fac.unsqueeze(2), [ROWS, M5, VD3]), ALU.mult))
                link(V.tensor_scalar(a3, a3, 2.0 ** 60, -(2.0 ** 60), ALU.min, ALU.max))
                link(V.tensor_tensor(s3, a3, a3, ALU.mult))
                V.tensor_reduce(rr, s3, AX.X, ALU.add).then_inc(sem("a3_ms"), 1)
                dve.wait_ge(sem("a3_ms"), 1)
                link(V.scalar_tensor_tensor(big, rr, 2.0 ** 48, big, ALU.is_ge, ALU.mult))
                link(V.tensor_scalar(big, big, LAMBDA_INIT - 1.0, 1.0 - LAMBDA_INIT, ALU.mult, ALU.add))
                dve.wait_ge(sem("a3_rms"), 1)
                link(V.reciprocal(rr, fac))
                link(V.tensor_tensor(rr, rr, big, ALU.mult))
                link(V.tensor_tensor(a3, a3, bc(rr.unsqueeze(2), [ROWS, M5, VD3]), ALU.mult))
                V.tensor_tensor(a3, a3, bc(w_rms[:ROWS].unsqueeze(1), [ROWS, M5, VD3]), ALU.mult).then_inc(sem("a3_at"), 1)
                add_out("a3_out", "a3_h", [2 + i % 2 for i in range(TILES)])

            if stop >= 8:
                norm("n3f", h, xn)
                for i in range(TILES):
                    dve.wait_ge(sem("f3_y"), i + 1)
                    V.tensor_tensor(h[:N[i], i, :], PS[:N[i], 2 + i, 0:D], h[:N[i], i, :], ALU.add).then_inc(sem("done"), 1)
            else:
                for i in range(TILES):
                    V.memset(flag[:, 2 + i:3 + i], 0.0).then_inc(sem("done"), 1)


def arrange(x):
    c = np.ascontiguousarray
    g = {}
    g["consts"] = constants()[1]
    p = np.asarray(x["x"]).reshape(BATCH, 3, 4, 16, 4, 16).transpose(1, 3, 5, 0, 2, 4).reshape(PK, 128, BATCH, 16)
    p = np.concatenate([np.zeros((PK, 128, BATCH, 1), np.float32), p], 3)
    g["patches"] = p.reshape(PK, 128, TOK).transpose(1, 0, 2)

    def rows(w, k):
        w = np.asarray(w)
        return w.reshape(k, 128, w.shape[1]).transpose(1, 0, 2)

    g["w_tok"] = rows(np.asarray(x["L0_tok_W"]).T, PK)
    bias = np.broadcast_to(np.asarray(x["L0_tok_b"])[None], (SEQ - 1, D))
    g["pos"] = np.concatenate([np.asarray(x["cls_tok"]).reshape(1, D), np.asarray(x["L0_tok_pos_emb"]),
                               np.zeros((1, D), np.float32), bias], 0)
    g["w_qkv0"] = np.stack([rows(x[f"L0_attn_W_{k}"], KD) for k in "qkv"], 1)
    g["w_r0"] = rows(np.asarray(x["L0_ffn_Wr"]).T, KD)
    cat = np.concatenate([np.asarray(x["L0_ffn_Wqkv"]), np.asarray(x["L0_ffn_Wr"])[:, :, None]], 2)
    g["w_cat"] = cat.reshape(E0, KD, 128, QKVW).transpose(2, 1, 0, 3)
    g["w_o0"] = np.asarray(x["L0_ffn_Wo"]).transpose(1, 0, 2)
    g["w_in"] = rows(np.asarray(x["L1_attn_W_in"]).T, KD)
    g["w_out"] = rows(np.asarray(x["L1_attn_W_out"]).T, INNER)
    chan = lambda a, n: np.asarray(a).reshape(INNER, 128, n).transpose(1, 0, 2)
    g["m_small"] = np.concatenate([chan(x["L1_attn_conv_w"], 4), chan(x["L1_attn_conv_b"], 1), chan(x["L1_attn_D"], 1),
                                   chan(x["L1_attn_A_log"], STATE)], 2)
    g["w_r1"] = rows(x["L1_ffn_Wr"], KD)
    g["w_br"] = np.asarray(x["L1_ffn_br"])[None]
    g["w_b1"] = np.asarray(x["L1_ffn_b1"]).reshape(E1, F1C, 128).transpose(2, 0, 1)
    g["w_b2"] = np.asarray(x["L1_ffn_b2"])
    g["w1_1"] = np.asarray(x["L1_ffn_W1"]).reshape(E1, KD, 128, F1C * 128).transpose(0, 2, 1, 3).reshape(E1, 128, -1)
    g["w2_1"] = np.asarray(x["L1_ffn_W2"]).reshape(E1, F1C, 128, D).transpose(0, 2, 1, 3).reshape(E1, 128, -1)
    g["w_ln"] = np.stack([np.asarray(x["L2_attn_ln_scale"]).reshape(KD, 128).T,
                          np.asarray(x["L2_attn_ln_bias"]).reshape(KD, 128).T], 1)
    g["w_dq"] = rows(np.asarray(x["L2_attn_w_down_q"]).T, KD)
    g["w_dkv"] = rows(np.asarray(x["L2_attn_w_down_kv"]).T, KD)

    def pairs(w):
        w = np.asarray(w).reshape(4, 4, 32, 2, 128).transpose(4, 0, 3, 1, 2)
        return w.reshape(128, 8, 128)

    g["w_uq"] = pairs(x["L2_attn_w_up_q"])
    g["w_uk"] = pairs(x["L2_attn_w_up_k"])
    g["w_uv"] = np.asarray(x["L2_attn_w_up_v"]).reshape(4, 4, DH2, 128).transpose(3, 1, 0, 2).reshape(128, 1024)
    g["w_o2"] = rows(np.asarray(x["L2_attn_w_out"]).T.reshape(4, 4, DH2, D).transpose(1, 0, 2, 3).reshape(1024, D), 8)
    g["w_gate"] = rows(np.asarray(x["L2_ffn_gate_w"])[:E2].T, KD)
    for n, k in (("w1", KD), ("w3", KD), ("w2", F2C)):
        w = np.asarray(x[f"L2_ffn_{n}"])[:E2]
        g[n + "_2"] = w.reshape(E2, k, 128, w.shape[2]).transpose(0, 2, 1, 3).reshape(E2, 128, -1)
    g["w_q3"] = rows(x["L3_attn_Wq"], KD)
    g["w_k3"] = rows(x["L3_attn_Wk"], KD)
    g["w_v3"] = rows(x["L3_attn_Wv"], KD)
    g["w_o3"] = rows(x["L3_attn_Wo"], KD)
    lam = np.stack([np.asarray(x["L3_attn_lambda_" + k]) for k in ("q1", "k1", "q2", "k2")])
    g["w_lam"] = np.broadcast_to(lam[None], (128, 4, HD3))
    g["w_rms"] = np.broadcast_to(np.asarray(x["L3_attn_rms_w"])[None], (128, VD3))
    g["ids"] = np.asarray(x["L3_ffn_ids"])[None]
    g["w_adp"] = np.broadcast_to(np.asarray(x["L3_ffn_weights"])[None], (128, ADAPT))
    g["w_acol"] = np.asarray(x["L3_ffn_weights"])[:, None]
    w = np.asarray(x["L3_ffn_W"])
    g["w_all"] = w.transpose(0, 2, 1).reshape(w.shape[0], KD, 128, D).transpose(0, 2, 1, 3).reshape(w.shape[0], 128, -1)
    g["b_all"] = np.asarray(x["L3_ffn_b"])
    return {k: c(v) for k, v in g.items()}


def kernel(**inputs):
    import concourse.bacc as bacc
    from concourse.bass_utils import run_bass_kernel_spmd

    nc = bacc.Bacc("TRN2", target_bir_lowering=False, num_devices=1)
    arrays = arrange(inputs)
    dram = {n: nc.dram_tensor(n + "_dram", a.shape, mybir.dt.from_np(a.dtype), kind="ExternalInput").ap()
            for n, a in arrays.items()}
    out = nc.dram_tensor("out", (TOK, D), F32, kind="ExternalOutput").ap()
    build(nc, dram, out)
    r = run_bass_kernel_spmd(nc, [{n + "_dram": a for n, a in arrays.items()}], core_ids=[0])
    return r.results[0]["out"].reshape(BATCH, SEQ, D)
```

```python
from contextlib import ExitStack

import numpy as np

import concourse.bass as bass
from concourse import mybir

F32 = mybir.dt.float32
I32 = mybir.dt.int32
F32R = mybir.dt.float32r
ALU = mybir.AluOpType
ACT = mybir.ActivationFunctionType
AX = mybir.AxisListType

BATCH = 32
SEQ = 17
D = 256
KD = D // 128
TOK = BATCH * SEQ
HALF = TOK // 2
GROUP = 7
TILES = -(-BATCH // GROUP)
ROWS = GROUP * SEQ
WIDTH = [min(GROUP, BATCH - GROUP * i) for i in range(TILES)]
N = [w * SEQ for w in WIDTH]
T0 = [ROWS * i for i in range(TILES)]
PK = 3 * 16 * 16 // 128
E0 = 8
HP = 128
QKVW = 3 * HP + 1
ROT = 32
INNER = 4
STATE = 16
E1, F1C = 8, 8
E2, F2C = 4, 11
UNITS2 = 4 * TILES
AHEAD = 3
SLOTS = F1C + AHEAD
HI, LO = 0, 1
PARTS = ((HI, HI), (HI, LO), (LO, HI))
H2, DH2 = 16, 64
H3, KV3, HD3 = 16, 8, 8
MAPS = 2 * H3
VD3 = 2 * HD3
VP3 = 32
ADAPT = 8
LAMBDA_INIT = 0.8 - 0.6 * float(np.exp(-0.3 * 12))
MASKED = -1.0e30


def constants():
    p = np.arange(128)
    t = np.arange(SEQ, dtype=np.float32)
    parts = {}
    parts["ident"] = np.eye(128)
    q, k = p[:, None], np.arange(ROWS)[None, :]
    same = (q // SEQ) == (k // SEQ)
    parts["block"] = np.where(same, 0.0, MASKED)
    parts["causal"] = np.where(same & (k <= q), 0.0, MASKED)
    parts["image"] = (q // SEQ) == np.arange(GROUP)[None, :]
    parts["place"] = (q % SEQ) == np.arange(SEQ)[None, :]
    parts["spread"] = (q % SEQ == k % SEQ) & (q < 2 * SEQ)
    parts["rank17"] = np.broadcast_to(64.0 - t, (128, SEQ))
    parts["rank8"] = np.broadcast_to(8.0 - np.arange(8), (128, 8))
    inv = (1.0 / 10000.0 ** (np.arange(ROT, dtype=np.float32) * np.float32(2.0) / 64)).astype(np.float32)
    ang = (t[:, None] * inv[None]).astype(np.float32)
    table = np.zeros((128, 2 * ROT + 1), np.float32)
    table[:SEQ] = np.concatenate([np.cos(ang), np.sin(ang), t[:, None]], 1)
    parts["rope0"] = table
    parts["token"] = np.broadcast_to(np.arange(TOK), (128, TOK))
    parts["first"] = (p[:, None] % BATCH) * SEQ
    parts["mhalf"] = np.full((128, 1), -0.5)
    parts["eps6"] = np.full((128, 1), 1e-6)
    inv = (1.0 / 10000.0 ** (np.arange(0, DH2, 2, dtype=np.float32) / DH2)).astype(np.float32)
    ang = np.outer(t, inv[(2 * np.arange(32)) % 32]).astype(np.float32)
    parts["cos2"] = np.cos(ang).T[p % 32]
    parts["sin2"] = np.sin(ang).T[p % 32]
    inv = (1.0 / 10000.0 ** (np.arange(0, HD3, 2, dtype=np.float32) / HD3)).astype(np.float32)
    ang = np.outer(t, inv).astype(np.float32)
    parts["cos3"] = np.cos(ang)[p % SEQ]
    parts["sin3"] = np.sin(ang)[p % SEQ]
    parts["own"] = (p[:, None] // HD3) == np.arange(16)[None, :]
    parts["quad"] = (p[:, None] // 32) == np.arange(4)[None, :]
    parts["one"] = np.ones((128, 128))
    at, out = {}, []
    w = 0
    for name, a in parts.items():
        a = np.asarray(a, np.float32)
        at[name] = (w, a.shape[1])
        w += a.shape[1]
        out.append(a)
    return at, np.concatenate(out, 1)


def build(nc, dram, out, stop=99):
    CONST, const_np = constants()
    ctx = ExitStack()
    with ctx:
        sems = {}

        def sem(name):
            if name not in sems:
                sems[name] = ctx.enter_context(nc.semaphore(name))
            return sems[name]

        def sb(name, shape):
            return ctx.enter_context(nc.sbuf_tensor(name, [128] + shape, F32))

        h = sb("h", [TILES, D])
        xn = sb("xn", [TILES, D])
        xT = sb("xT", [KD, TOK])
        cst = sb("cst", [const_np.shape[1]])
        st = sb("st", [TILES, 6])
        mv = sb("mv", [TILES, 2])
        var = sb("var", [TILES])
        rstd = sb("rstd", [TILES])
        w_in = sb("w_in", [KD, 8 * 128])
        w_out = sb("w_out", [INNER, D])
        m_small = sb("m_small", [INNER, 4 + 1 + 1 + STATE])
        w_r0 = sb("w_r0", [KD, E0])
        w_r1 = sb("w_r1", [KD, E1])
        w_br = sb("w_br", [E1])
        w_b1 = sb("w_b1", [E1, F1C])
        w_b2 = sb("w_b2", [D])
        w_gate = sb("w_gate", [KD, E2])
        w_ln = sb("w_ln", [2, KD])
        w_q3 = sb("w_q3", [KD, D])
        w_k3 = sb("w_k3", [KD, D // 2])
        w_v3 = sb("w_v3", [KD, D // 2])
        w_o3 = sb("w_o3", [KD, D])
        w_lam = sb("w_lam", [4, HD3])
        w_rms = sb("w_rms", [VD3])
        w_eff = sb("w_eff", [KD, D])
        w_tmp = sb("w_tmp", [KD, D])
        w_adp = sb("w_adp", [ADAPT])
        w_arep = sb("w_arep", [ROWS])
        w_acol = sb("w_acol", [1])
        b_adp = sb("b_adp", [D])
        misc = sb("misc", [900])
        flag = sb("flag", [8])
        ids = ctx.enter_context(nc.sbuf_tensor("ids", [128, ADAPT], I32))
        PIECE = F2C * D
        HEAD, TAIL = 20912, 2 * PIECE
        with nc.sbuf_tensor("ring", [128, 4 * PIECE], F32) as RING:
            with nc.sbuf_tensor("bc", [128, HEAD + TAIL], F32) as BC:
                pass
        RINGR = ctx.enter_context(nc.sbuf_tensor("ring_r", [128, 4 * PIECE], F32R))
        BCR = ctx.enter_context(nc.sbuf_tensor("bc_r", [128, HEAD + TAIL], F32R))
        PS = ctx.enter_context(nc.psum_tensor("PS", [128, 8, 512], F32))

        def const(name):
            a, w = CONST[name]
            return cst[:, a:a + w]

        def carve(region, start, sizes):
            got = []
            for dims in sizes:
                n = int(np.prod(dims))
                v = region[:, start:start + n]
                if len(dims) == 2:
                    v = v.rearrange("p (a b) -> p a b", a=dims[0])
                if len(dims) == 3:
                    v = v.rearrange("p (a b c) -> p a b c", a=dims[0], b=dims[1])
                got.append(v)
                start += n
            return got, start

        ident = const("ident")

        early, end = carve(BC, HEAD + TAIL - 14544, [(PK, TOK), (PK, D), (3, KD, D), (KD, E0 * QKVW), (E0, D)])
        assert end == HEAD + TAIL
        patch, w_tok, w_qkv0, w_cat, w_o0 = early
        w_cat = w_cat.rearrange("p k (e w) -> p k e w", e=E0)
        pos = misc[:, 0:D]
        LATE = misc[:, D:900]
        raw = RING[:, 0:ADAPT * KD * D].rearrange("p (a b) -> p a b", a=ADAPT)

        (qk0, v0, sm0, p0, pt0, mx0, sum0), _ = carve(
            BC, 0, [(4, TOK), (TILES, D), (TILES, ROWS), (TILES, ROWS), (TILES, ROWS), (TILES,), (2 * TILES,)])
        (sg, sel, t8a, t8b, m8, r8), f0a = carve(
            RING, ADAPT * KD * D, [(TOK,), (2, TOK), (TOK,), (TOK,), (2, BATCH), (BATCH,)])
        assert f0a <= 4 * PIECE
        (G, xg, poh, qkv, prod, GT, avt, av, xp, rt), f0b = carve(
            BC, 0, [(TILES, 2 * E0 * GROUP), (KD, 2 * E0 * BATCH), (2 * E0, BATCH), (4, 450), (512,),
                    (4, TOK), (4, 128), (4, 128), (4, D), (6, 256)])
        assert f0b <= HEAD + TAIL - 14544, f0b
        (xpad, cv, xc, delta, bx, sres, a_ring, hs_ring), mend = carve(
            BC, 0, [(INNER, BATCH * (SEQ + 3)), (INNER, TOK), (INNER, TOK), (INNER, TOK), (INNER, TOK),
                    (INNER, TOK), (8, TOK), (12, TOK)])
        assert mend <= HEAD + TAIL
        flat_in = w_in[:, :, :].rearrange("p a b -> p (a b)")
        (act_f, sil), end = carve(flat_in, 0, [(3, HALF), (3, HALF)])
        assert end <= KD * 8 * 128
        F1P = F1C * D
        (w1hi,), f1h = carve(BCR, 0, [(4, F1P)])
        (h1,), end = carve(BCR, f1h, [(SLOTS * 2, TOK)])
        assert end <= HEAD
        (xs1,), end = carve(RINGR, 4 * F1P, [(2 * KD, TOK)])
        assert end <= 4 * PIECE
        (w2hi, h2, xs2), end = carve(BCR, 0, [(4, PIECE), (F2C * 2, TOK), (2 * KD, TOK)])
        assert end <= HEAD + TAIL
        rwT = w_out[:, :, :].rearrange("p a b -> p (a b)")[:, 0:TOK]
        (w_dq, w_dkv, w_uq, w_uk, w_uv, w_o2), end = carve(
            BC, HEAD, [(KD, 128), (KD, 128), (8, 128), (8, 128), (1024,), (8, D)])
        assert end == HEAD + TAIL
        (q2, k2, v2, rt2), a2end = carve(BC, 0, [(8, TOK), (8, TOK), (TILES, H2 * DH2), (8, TOK)])
        (cT,), a2b = carve(BC, a2end, [(2, TOK)])
        assert a2b <= HEAD, a2b
        (yn, gT), _ = carve(BC, a2end - 8 * TOK, [(TILES, D), (KD, TOK)])
        (sm2, p2, pt2, oT2), end = carve(
            BC, a2end - 8 * TOK, [(3, 4 * ROWS), (4, 4 * ROWS), (2, 4 * ROWS), (2 * 8, ROWS)])
        assert end <= HEAD, end
        (qm2,), end = carve(flat_in, 0, [(2 * 8, ROWS)])
        assert end <= KD * 8 * 128
        o2b, _ = carve(misc, 0, [(4,)] * 5)
        (qt3, kt3, kr3, v3, rt3, qT3, kT3, kx3, o3, sm3, oT3), end = carve(
            BC, 0, [(TILES, D), (TILES, D // 2), (TILES, D), (TILES, KV3 * VP3), (4, TILES * 128),
                    (2, TOK), (2, TOK), (16, TOK), (TILES, MAPS * (VD3 + 1)), (3, 4 * ROWS),
                    (2, 4 * ROWS)])
        assert end <= HEAD + TAIL, end
        (kx3b, p3, pt3), end = carve(RING, 0, [(16, TOK), (2, 4 * ROWS), (3, 4 * ROWS)])
        assert end <= 4 * PIECE
        (at3, sq3, atT3), end = carve(BC, 0, [(TILES, D), (TILES, D), (KD, TOK)])
        assert end <= 3 * TILES * D + 3000

        (rsc, rtmp, rv2, rsel, rw, rt5), _ = carve(
            LATE, 0, [(TILES, 8), (TILES, 8), (TILES, 8), (2 * TILES, 8), (TILES, 8), (TILES, 12)])

        def bc(ap, dims):
            return ap.broadcast_to(dims)

        def four(ap, n):
            return ap.rearrange("p (a b) -> p a b", a=4)[:, :, 0:n]

        def half(a, s):
            return a[:, HALF * s:HALF * (s + 1)]

        def both(bank):
            return PS[:, bank:bank + 2, 0:HALF]

        def halves(ap):
            return ap.rearrange("p (s t) -> p s t", s=2)

        def raw1(q, region=None):
            return (RING if region is None else region)[:, (q % 4) * F1P:(q % 4 + 1) * F1P]

        def raw2(p, region=None):
            return (RING if region is None else region)[:, (p % 4) * PIECE:(p % 4 + 1) * PIECE]

        def as_f32(ap):
            return ap.bitcast(F32)

        NORMS = ["n0", "n0f", "n1", "n1f", "n2", "n2b", "n2f", "n3", "n3f"]
        FED = [x for x in NORMS if x != "n2"]

        def nth(L, i=0):
            return TILES * NORMS.index(L) + i + 1

        def nth_T(L, i=0):
            return TILES * FED.index(L) + i + 1

        block = ctx.enter_context(nc.Block())

        @block.sync
        def _(sp):
            loads = {}

            def load(dst, name, s, src=None):
                loads[s] = loads.get(s, 0) + 16
                sp.dma_start(dst, dram[name] if src is None else src).then_inc(sem(s), 16)

            load(cst[:, :], "consts", "ld_const")
            load(pos[0:2 * SEQ, :], "pos", "ld_tok")
            load(patch, "patches", "ld_tok")
            load(w_tok, "w_tok", "ld_tok")
            load(w_qkv0, "w_qkv0", "ld_qkv0")
            load(ids[0:1, :], "ids", "ld_ids")
            load(w_adp[:, :], "w_adp", "ld_adp")
            load(w_acol[0:ADAPT, :], "w_acol", "ld_adp")
            load(w_r0[:, :, :], "w_r0", "ld_f0")
            load(w_cat, "w_cat", "ld_f0")
            load(w_o0, "w_o0", "ld_f0")
            sp.wait_ge(sem("ld_ids"), 16)
            for a in range(ADAPT):
                r = sp.value_load(ids[0:1, a:a + 1], min_val=0, max_val=31)
                sp.dma_start(raw[:, a, :], dram["w_all"][bass.ds(r, 1), :, :].rearrange("a p n -> p (a n)")).then_inc(sem("ld_raw"), 16)
                sp.dma_start(b_adp[a:a + 1, :], dram["b_all"][bass.ds(r, 1), :]).then_inc(sem("ld_badp"), 16)
            load(w_in[:, :, :], "w_in", "ld_m")
            load(w_out[:, :, :], "w_out", "ld_m")
            load(m_small[:, :, :], "m_small", "ld_m")
            load(w_r1[:, :, :], "w_r1", "ld_f1")
            load(w_br[0:1, :], "w_br", "ld_f1")
            load(w_b1[:, :, :], "w_b1", "ld_f1")
            load(w_b2[0:E1, :], "w_b2", "ld_f1")
            load(w_gate[:, :, :], "w_gate", "ld_f1")
            load(w_ln[:, :, :], "w_ln", "ld_f1")
            load(w_q3[:, :, :], "w_q3", "ld_a3")
            load(w_k3[:, :, :], "w_k3", "ld_a3")
            load(w_v3[:, :, :], "w_v3", "ld_a3")
            load(w_o3[:, :, :], "w_o3", "ld_a3")
            load(w_lam[:, :, :], "w_lam", "ld_a3")
            load(w_rms[:, :], "w_rms", "ld_a3")
            if stop >= 4:
                sp.wait_ge(sem("eff"), 1)
                sp.wait_ge(sem("f0_done"), 1)
                for e in range(E1):
                    if e >= 2:
                        sp.wait_ge(sem("f1_z"), 2 * F1C * (e - 1))
                    load(raw1(2 * e), None, f"ld_p{2 * e % 4}", dram["w1_1"][e])
                    if e >= 2:
                        sp.wait_ge(sem("f1_y"), TILES * (e - 1))
                    load(raw1(2 * e + 1), None, f"ld_p{(2 * e + 1) % 4}", dram["w2_1"][e])
                    if e == 3 and stop >= 5:
                        for name, dst in (("w_dq", w_dq), ("w_dkv", w_dkv), ("w_uq", w_uq), ("w_uk", w_uk),
                                          ("w_uv", w_uv), ("w_o2", w_o2)):
                            load(dst, name, "ld_a2")
            if stop >= 6:
                for e in range(E2):
                    for j, name in enumerate(("w1_2", "w3_2", "w2_2")):
                        p = 3 * e + j
                        if p == 0:
                            sp.wait_ge(sem("f1_y"), TILES * E1)
                        if p >= 4:
                            if (p - 4) % 3 == 2:
                                sp.wait_ge(sem("f2_y"), TILES * ((p - 4) // 3 + 1))
                            else:
                                sp.wait_ge(sem("f2_z"), 2 * F2C * ((p - 4) // 3 + 1))
                        load(raw2(p), None, f"ld_p{p % 4}", dram[name][e])
            if stop < 8:
                for s, n in loads.items():
                    sp.wait_ge(sem(s), n)
                sp.wait_ge(sem("ld_badp"), 128)
                sp.wait_ge(sem("eff"), 2)
                sp.wait_ge(sem("ld_raw"), 128)
            for i in range(TILES):
                sp.wait_ge(sem("done"), i + 1)
                sp.dma_start(out[T0[i]:T0[i] + N[i], :], h[:N[i], i, :]).then_inc(sem("stored"), 16)
            sp.wait_ge(sem("stored"), 16 * TILES)

        @block.tensor
        def _(pe):
            def mm(dst, lhsT, rhs, start=True, stop=True):
                return nc.tensor.matmul(dst, lhsT, rhs, start=start, stop=stop)

            def norm_T(L):
                for i in range(TILES):
                    pe.wait_ge(sem("norm_xn"), nth(L, i))
                    if i >= 2:
                        pe.wait_ge(sem("norm_xT"), nth_T(L, i - 2))
                    src = yn if L == "n2b" else xn
                    for c in range(KD):
                        last = nc.tensor.transpose(PS[:, i % 2, 128 * c:128 * c + N[i]],
                                                   src[:N[i], i, 128 * c:128 * (c + 1)], ident[:N[i], :N[i]])
                    last.then_inc(sem("norm_tr"), 1)
                pe.wait_ge(sem("norm_xT"), nth_T(L, TILES - 1))

            pe.wait_ge(sem("ld_tok"), 48)
            pe.wait_ge(sem("ld_const"), 16)
            for i in range(TILES):
                o = PS[:N[i], i, 0:D]
                for c in range(PK):
                    mm(o, patch[:, c, T0[i]:T0[i] + N[i]], w_tok[:, c, :], c == 0, False)
                mm(o, const("spread")[0:2 * SEQ, 0:N[i]], pos[0:2 * SEQ, :], False, True).then_inc(sem("t_ps"), 1)

            if stop >= 1:
                norm_T("n0")
                pe.wait_ge(sem("ld_qkv0"), 16)
                for j in range(4):
                    for s in range(2):
                        for c in range(KD):
                            last = mm(PS[:, 2 * j + s, 0:HALF], w_qkv0[:, j // 2, c, 128 * (j % 2):128 * (j % 2) + 128],
                                      half(xT[:, c, :], s), c == 0, c == KD - 1)
                    last.then_inc(sem("a0_qk"), 1)
                for i in range(TILES):
                    if i == 0:
                        pe.wait_ge(sem("a0_q_sb"), 1)
                    if i == 2:
                        pe.wait_ge(sem("a0_k_sb"), 1)
                    if i == 4:
                        pe.wait_ge(sem("a0_q_sb"), 2)
                    for c in range(KD):
                        last = mm(PS[:N[i], i, 0:D], xT[:, c, T0[i]:T0[i] + N[i]], w_qkv0[:, 2, c, :],
                                  c == 0, c == KD - 1)
                    last.then_inc(sem("a0_v"), 1)
                pe.wait_ge(sem("a0_k_sb"), 2)
                for i in range(TILES):
                    pe.wait_ge(sem("a0_v_sb"), i + 1)
                    r = slice(T0[i], T0[i] + N[i])
                    for c in range(KD):
                        last = mm(PS[:N[i], i, 0:N[i]], qk0[:, c, r], qk0[:, 2 + c, r], c == 0, c == KD - 1)
                    last.then_inc(sem("a0_s"), 1)

                def probs_T(i):
                    pe.wait_ge(sem("a0_p"), i + 1)
                    nc.tensor.transpose(PS[:N[i], i, 128:128 + N[i]], p0[:N[i], i, 0:N[i]],
                                        ident[:N[i], :N[i]]).then_inc(sem("a0_t"), 1)

                def mix(i):
                    pe.wait_ge(sem("a0_pt"), i + 1)
                    mm(PS[:N[i], i, 256:512], pt0[:N[i], i, 0:N[i]], v0[:N[i], i, :]).then_inc(sem("a0_o"), 1)

                probs_T(0)
                for i in range(1, TILES):
                    probs_T(i)
                    mix(i - 1)
                mix(TILES - 1)

            if stop >= 2:
                norm_T("n0f")
                pe.wait_ge(sem("ld_f0"), 48)
                for s in range(2):
                    for c in range(KD):
                        last = mm(PS[0:E0, 2 + s, 0:HALF], w_r0[:, c, :], half(xT[:, c, :], s), c == 0, c == KD - 1)
                last.then_inc(sem("f0_lg"), 1)
                pe.wait_ge(sem("f0_sel"), 1)
                for i in range(TILES):
                    for k in range(2):
                        last = nc.tensor.transpose(PS[:N[i], 4, (2 * i + k) * E0:(2 * i + k + 1) * E0],
                                                   sel[0:E0, k, T0[i]:T0[i] + N[i]], ident[0:E0, 0:E0])
                last.then_inc(sem("f0_selT"), 1)
                for i in range(TILES):
                    pe.wait_ge(sem("f0_G"), i + 1)
                    if i >= 2:
                        pe.wait_ge(sem("f0_xg"), i - 1)
                    w = 2 * E0 * WIDTH[i]
                    b = 5 + i % 2
                    for c in range(KD):
                        mm(PS[:, b, 112 * c:112 * c + w], xn[:N[i], i, 128 * c:128 * c + 128], G[:N[i], i, 0:w])
                    mm(PS[0:SEQ, b, 224:224 + w], const("place")[:N[i], :], G[:N[i], i, 0:w]).then_inc(sem("f0_g"), 1)
                pe.wait_ge(sem("f0_xg"), TILES)
                for gk in range(4):
                    g, k = gk // 2, gk % 2
                    for e4 in range(4):
                        e = 4 * g + e4
                        rows = slice(32 * e4, 32 * e4 + 32)
                        slots = slice((k * E0 + e) * BATCH, (k * E0 + e + 1) * BATCH)
                        for c in range(KD):
                            mm(PS[rows, gk, 0:QKVW], xg[:, c, slots], w_cat[:, c, e, :], c == 0, c == KD - 1)
                        last = mm(PS[rows, gk, QKVW:QKVW + 65], poh[0:SEQ, k * E0 + e, :], const("rope0")[0:SEQ, :])
                    last.then_inc(sem("f0_qkv"), 1)
                pe.wait_ge(sem("f0_av"), 1)
                for gk in range(4):
                    last = nc.tensor.transpose(PS[:, 4, 128 * gk:128 * gk + 128], av[:, gk, :], ident)
                last.then_inc(sem("f0_avt"), 1)
                pe.wait_ge(sem("f0_avt_sb"), 1)
                for gk in range(4):
                    for e4 in range(4):
                        last = mm(PS[32 * e4:32 * e4 + 32, gk, 0:D], avt[:, gk, 32 * e4:32 * e4 + 32],
                                  w_o0[:, 4 * (gk // 2) + e4, :])
                    last.then_inc(sem("f0_x"), 1)
                pe.wait_ge(sem("f0_xp"), 4)
                pe.wait_ge(sem("f0_GT"), 4)
                for i in range(TILES):
                    b = 5 + i % 3
                    if i >= 3:
                        pe.wait_ge(sem("f0_h"), i - 2)
                    for gk in range(4):
                        last = mm(PS[:N[i], b, 0:D], GT[:, gk, T0[i]:T0[i] + N[i]], xp[:, gk, :], gk == 0, gk == 3)
                    last.then_inc(sem("f0_out"), 1)

            if stop >= 3:
                norm_T("n1")
                pe.wait_ge(sem("ld_m"), 48)
                for m in range(8):
                    b = 2 * (m % 4)
                    if m >= 4:
                        pe.wait_ge(sem("m_in"), m - 3)
                    for s in range(2):
                        for c in range(KD):
                            last = mm(PS[:, b + s, 0:HALF], w_in[:, c, 128 * m:128 * m + 128], half(xT[:, c, :], s),
                                      c == 0, c == KD - 1)
                    last.then_inc(sem("m_x"), 1)
                for c in range(INNER):
                    b = 2 * (c % 2)
                    if c >= 2:
                        pe.wait_ge(sem("m_t1"), c - 1)
                    if c == 0:
                        pe.wait_ge(sem("m_in"), 8)
                    for q in range(4):
                        pe.wait_ge(sem("m_pair"), 4 * c + q + 1)
                        for j in range(2):
                            for s in range(2):
                                last = mm(PS[:, b + s, 0:HALF], ident, half(hs_ring[:, 4 * ((4 * c + q) % 3) + j, :], s),
                                          q == 0 and j == 0, q == 3 and j == 1)
                        last.then_inc(sem("m_sum"), 1)
                pe.wait_ge(sem("m_y"), INNER)
                for i in range(TILES):
                    b = 4 + i % 4
                    if i >= 4:
                        pe.wait_ge(sem("m_h"), i - 3)
                    for c in range(INNER):
                        last = mm(PS[:N[i], b, 0:D], cv[:, c, T0[i]:T0[i] + N[i]], w_out[:, c, :], c == 0, c == INNER - 1)
                    last.then_inc(sem("m_out"), 1)

            if stop >= 4:
                norm_T("n1f")
                pe.wait_ge(sem("ld_f1"), 96)
                for i in range(TILES):
                    for c in range(KD):
                        mm(PS[:N[i], 6, 8 * i:8 * i + 8], xT[:, c, T0[i]:T0[i] + N[i]], w_r1[:, c, :], c == 0, False)
                    last = mm(PS[:N[i], 6, 8 * i:8 * i + 8], const("one")[0:1, :N[i]], w_br[0:1, :], False, True)
                last.then_inc(sem("f1_sc"), 1)

                def up1(C):
                    e, c = C // F1C, C % F1C
                    pe.wait_ge(sem("w_lo"), 2 * e + 1)
                    w = [v.rearrange("p (c m) -> p c m", c=KD)
                         for v in (w1hi[:, 2 * e % 4, :], raw1(2 * e, RINGR))]
                    for s in range(2):
                        u = 2 * C + s
                        if u >= 3:
                            pe.wait_ge(sem("f1_f"), u - 2)
                        for k in range(KD):
                            for a, b in PARTS:
                                last = mm(PS[:, 2 * (u % 3), 0:HALF], w[a][:, k, 128 * c:128 * c + 128],
                                          half(xs1[:, KD * b + k, :], s), k == 0 and a == b,
                                          k == KD - 1 and a == LO)
                        last.then_inc(sem("f1_z"), 1)

                def down1(e):
                    pe.wait_ge(sem("w_lo"), 2 * e + 2)
                    pe.wait_ge(sem("f1_h"), 2 * F1C * (e + 1))
                    w = [v.rearrange("p (c m) -> p c m", c=F1C)
                         for v in (w1hi[:, (2 * e + 1) % 4, :], raw1(2 * e + 1, RINGR))]
                    for i in range(TILES):
                        n = e * TILES + i
                        if n >= 2:
                            pe.wait_ge(sem("f1_acc"), n - 1)
                        for c in range(F1C):
                            for a, b in PARTS:
                                last = mm(PS[:N[i], 6 + n % 2, 0:D],
                                          h1[:, 2 * ((e * F1C + c) % SLOTS) + a, T0[i]:T0[i] + N[i]], w[b][:, c, :],
                                          c == 0 and a == b, c == F1C - 1 and a == LO)
                        last.then_inc(sem("f1_y"), 1)

                pe.wait_ge(sem("f1_x"), 1)
                pe.wait_ge(sem("f1_rs"), 1)
                for C in range(F1C * E1 + AHEAD):
                    if C < F1C * E1:
                        up1(C)
                    if C < F1C + AHEAD - 1 or (C - AHEAD) % F1C != F1C - 1:
                        continue
                    e = (C - AHEAD) // F1C
                    if e == 0:
                        pe.wait_ge(sem("f1_rw"), 1)
                        for i in range(TILES):
                            nc.tensor.transpose(PS[0:E1, 1 if i < 4 else 3, 128 * (i % 4):128 * (i % 4) + N[i]],
                                                rw[:N[i], i, :], ident[:N[i], :N[i]]).then_inc(sem("f1_rwT"), 1)
                        pe.wait_ge(sem("f1_rwT_sb"), TILES)
                        for i in range(TILES):
                            b = (1, 3, 5)[i % 3]
                            if i >= 3:
                                pe.wait_ge(sem("f1_bh"), i - 2)
                            mm(PS[:N[i], b, 0:D], rwT[0:E1, T0[i]:T0[i] + N[i]], w_b2[0:E1, :]).then_inc(sem("f1_bias"), 1)
                    down1(e)

            if stop >= 5:
                norm_T("n2b")
                pe.wait_ge(sem("ld_a2"), 96)
                for j, w in enumerate((w_dq, w_dkv)):
                    for s in range(2):
                        for c in range(KD):
                            last = mm(PS[:, 2 + 2 * j + s, 0:HALF], w[:, c, :], half(gT[:, c, :], s), c == 0, c == KD - 1)
                    last.then_inc(sem("a2_c"), 1)
                pe.wait_ge(sem("a2_c_sb"), 2)
                for u in range(8):
                    j, pp = u // 4, u % 4
                    b = 4 * (u % 2)
                    if u >= 2:
                        pe.wait_ge(sem("a2_r"), u - 1)
                    for eo in range(2):
                        for s in range(2):
                            last = mm(PS[:, b + 2 * eo + s, 0:HALF], (w_uq, w_uk)[j][:, 2 * pp + eo, :],
                                      half(cT[:, j, :], s))
                    last.then_inc(sem("a2_eo"), 1)
                for i in range(TILES):
                    for g in range(2):
                        n = 2 * i + g
                        if n < 4:
                            pe.wait_ge(sem("a2_r"), 7)
                        elif n < 8:
                            pe.wait_ge(sem("a2_r"), 8)
                        else:
                            pe.wait_ge(sem("a2_v_sb"), n - 7)
                        mm(PS[:N[i], n % 8, :], cT[:, 1, T0[i]:T0[i] + N[i]], w_uv[:, 512 * g:512 * g + 512])\
                            .then_inc(sem("a2_v"), 1)
                pe.wait_ge(sem("a2_v_sb"), 2 * TILES)
                pe.wait_ge(sem("a2_qk_sb"), 16)
                units = 4 * TILES

                def scores2(u):
                    i, g = u // 4, u % 4
                    r = slice(T0[i], T0[i] + N[i])
                    if u >= 3:
                        pe.wait_ge(sem("u_sm"), u - 2)
                    pe.wait_ge(sem("a2_qm"), u + 1)
                    for m in range(4):
                        for eo in range(2):
                            last = mm(PS[:N[i], (0, 1, 6)[u % 3], ROWS * m:ROWS * m + N[i]],
                                      qm2[:, 8 * (u % 2) + 2 * m + eo, 0:N[i]], k2[:, 2 * m + eo, r], eo == 0, eo == 1)
                    last.then_inc(sem("u_s"), 1)

                def probs2(u):
                    i = u // 4
                    pe.wait_ge(sem("a2_pn"), u + 1)
                    if u >= 2:
                        pe.wait_ge(sem("u_pt"), u - 1)
                    for hh in range(4):
                        last = nc.tensor.transpose(PS[:N[i], 2 + u % 2, 128 * hh:128 * hh + N[i]],
                                                   p2[:N[i], u % 4, ROWS * hh:ROWS * hh + N[i]], ident[:N[i], :N[i]])
                    last.then_inc(sem("u_t"), 1)

                def mix2(u):
                    i, g = u // 4, u % 4
                    pe.wait_ge(sem("u_pt"), u + 1)
                    if u >= 2:
                        pe.wait_ge(sem("a2_ot"), u - 1)
                    for hh in range(4):
                        q = DH2 * (hh % 2)
                        last = mm(PS[q:q + DH2, 4 + u % 2, 128 * (hh // 2):128 * (hh // 2) + N[i]],
                                  v2[:N[i], i, DH2 * (4 * g + hh):DH2 * (4 * g + hh + 1)],
                                  pt2[:N[i], u % 2, ROWS * hh:ROWS * hh + N[i]])
                    last.then_inc(sem("a2_o"), 1)

                def project2(i):
                    pe.wait_ge(sem("a2_ot"), 4 * (i + 1))
                    if i >= 1:
                        pe.wait_ge(sem("a2_h"), i)
                    for c in range(8):
                        last = mm(PS[:N[i], 7, 0:D], oT2[:, 8 * (i % 2) + c, 0:N[i]], w_o2[:, c, :], c == 0, c == 7)
                    last.then_inc(sem("a2_out"), 1)

                for u in range(units + 5):
                    if u < units:
                        scores2(u)
                    if 4 <= u <= units + 3:
                        mix2(u - 4)
                    if 3 <= u <= units + 2:
                        probs2(u - 3)
                    if u >= 8 and u % 4 == 0:
                        project2(u // 4 - 2)

            if stop >= 6:
                norm_T("n2f")
                pe.wait_ge(sem("ld_f1"), 96)
                for i in range(TILES):
                    for c in range(KD):
                        last = mm(PS[:N[i], 6, 8 * i:8 * i + E2], xT[:, c, T0[i]:T0[i] + N[i]], w_gate[:, c, :],
                                  c == 0, c == KD - 1)
                last.then_inc(sem("f2_sc"), 1)

                def split(p, c):
                    pe.wait_ge(sem("w_lo"), 2 * E1 + p + 1)
                    return [v.rearrange("p (c m) -> p c m", c=c) for v in (w2hi[:, p % 4, :], raw2(p, RINGR))]

                def up2(e):
                    w1, w3 = split(3 * e, KD), split(3 * e + 1, KD)
                    for c in range(F2C):
                        for s in range(2):
                            u = (e * F2C + c) * 2 + s
                            if u >= 3:
                                pe.wait_ge(sem("f2_g"), u - 2)
                            for j, w in enumerate((w1, w3)):
                                for k in range(KD):
                                    for a, b in PARTS:
                                        last = mm(PS[:, 2 * (u % 3) + j, 0:HALF], w[a][:, k, 128 * c:128 * c + 128],
                                                  half(xs2[:, KD * b + k, :], s), k == 0 and a == b,
                                                  k == KD - 1 and a == LO)
                            last.then_inc(sem("f2_z"), 1)

                def down2(e):
                    w = split(3 * e + 2, F2C)
                    pe.wait_ge(sem("f2_h"), 2 * F2C * (e + 1))
                    for i in range(TILES):
                        n = e * TILES + i
                        if n >= 2:
                            pe.wait_ge(sem("f2_acc"), n - 1)
                        for c in range(F2C):
                            for a, b in PARTS:
                                last = mm(PS[:N[i], 6 + n % 2, 0:D], h2[:, 2 * c + a, T0[i]:T0[i] + N[i]], w[b][:, c, :],
                                          c == 0 and a == b, c == F2C - 1 and a == LO)
                        last.then_inc(sem("f2_y"), 1)

                pe.wait_ge(sem("f2_x"), 1)
                pe.wait_ge(sem("f2_rs"), 1)
                for e in range(E2):
                    up2(e)
                    down2(e)

            if stop >= 7:
                norm_T("n3")
                pe.wait_ge(sem("ld_a3"), 96)
                for i in range(TILES):
                    r = slice(T0[i], T0[i] + N[i])
                    b = 2 * (i % 3)
                    if i >= 3:
                        pe.wait_ge(sem("a3_qkv_sb"), i - 2)
                    for o, w in ((PS[:N[i], b, 0:256], w_q3), (PS[:N[i], b + 1, 0:128], w_k3),
                                 (PS[:N[i], b + 1, 128:256], w_v3)):
                        for c in range(KD):
                            last = mm(o, xT[:, c, r], w[:, c, :], c == 0, c == KD - 1)
                    last.then_inc(sem("a3_qkv"), 1)
                pe.wait_ge(sem("a3_qkv_sb"), TILES)
                pe.wait_ge(sem("a3_rope"), 1)
                for i in range(TILES):
                    if i >= 2:
                        pe.wait_ge(sem("a3_qkT"), i - 1)
                    for j, src in enumerate((qt3, kr3)):
                        for c in range(2):
                            last = nc.tensor.transpose(PS[:, i % 2, 256 * j + 128 * c:256 * j + 128 * c + N[i]],
                                                       src[:N[i], i, 128 * c:128 * c + 128], ident[:N[i], :N[i]])
                    last.then_inc(sem("a3_tr"), 1)
                pe.wait_ge(sem("a3_qkT"), TILES)
                pe.wait_ge(sem("a3_kx"), MAPS)
                units = 8 * TILES

                def scores3(u):
                    i, g = u // 8, u % 8
                    r = slice(T0[i], T0[i] + N[i])
                    if u >= 3:
                        pe.wait_ge(sem("u_sm"), UNITS2 + u - 2)
                    kk = kx3[:, 4 * g:4 * g + 4, r] if g < 4 else kx3b[:, 4 * g - 16:4 * g - 12, r]
                    mm(four(PS[:N[i], 1 + u % 3, 0:4 * ROWS], N[i]), qT3[:, g // 4, r], kk).then_inc(sem("u_s"), 1)

                def probs3(u):
                    i = u // 8
                    pe.wait_ge(sem("u_p"), UNITS2 + u + 1)
                    if u >= 2:
                        pe.wait_ge(sem("u_pt"), UNITS2 + u - 1)
                    for m in range(4):
                        last = nc.tensor.transpose(PS[:N[i], 4 + u % 2, 128 * m:128 * m + N[i]],
                                                   p3[:N[i], u % 2, ROWS * m:ROWS * m + N[i]], ident[:N[i], :N[i]])
                    last.then_inc(sem("u_t"), 1)

                def mix3(u):
                    i, g = u // 8, u % 8
                    pe.wait_ge(sem("u_pt"), UNITS2 + u + 1)
                    if u % 4 == 0 and u >= 8:
                        pe.wait_ge(sem("a3_oT"), u // 4 - 1)
                    q = 32 * (u % 4)
                    mm(four(PS[q:q + VP3, 6 + u // 4 % 2, 0:4 * ROWS], N[i]), v3[:N[i], i, VP3 * g:VP3 * (g + 1)],
                       four(pt3[:N[i], u % 3, :], N[i])).then_inc(sem("a3_o"), 1)

                def back3(n):
                    i = n // 2
                    pe.wait_ge(sem("a3_oT"), n + 1)
                    if n >= 1:
                        pe.wait_ge(sem("a3_o_sb"), n)
                    for m in range(4):
                        last = nc.tensor.transpose(PS[:N[i], 0, 128 * m:128 * m + 128],
                                                   oT3[:, n % 2, ROWS * m:ROWS * m + N[i]], ident)
                    last.then_inc(sem("a3_back"), 1)

                for u in range(units + 6):
                    if u < units:
                        scores3(u)
                    if 4 <= u <= units + 3:
                        mix3(u - 4)
                    if 2 <= u <= units + 1:
                        probs3(u - 2)
                    if u >= 9 and u % 4 == 1:
                        back3(u // 4 - 2)
                pe.wait_ge(sem("a3_at"), 1)
                for i in range(TILES):
                    if i >= 2:
                        pe.wait_ge(sem("a3_atT"), i - 1)
                    for c in range(KD):
                        last = nc.tensor.transpose(PS[:, i % 2, 128 * c:128 * c + N[i]],
                                                   at3[:N[i], i, 128 * c:128 * c + 128], ident[:N[i], :N[i]])
                    last.then_inc(sem("a3_at_tr"), 1)
                for i in range(TILES):
                    pe.wait_ge(sem("a3_atT"), i + 1)
                    if i >= 2:
                        pe.wait_ge(sem("a3_h"), i - 1)
                    for c in range(KD):
                        last = mm(PS[:N[i], 2 + i % 2, 0:D], atT3[:, c, T0[i]:T0[i] + N[i]], w_o3[:, c, :],
                                  c == 0, c == KD - 1)
                    last.then_inc(sem("a3_out"), 1)

            if stop >= 8:
                norm_T("n3f")
                pe.wait_ge(sem("eff"), 2)
                pe.wait_ge(sem("ld_badp"), 16 * ADAPT)
                for i in range(TILES):
                    b = 2 + i
                    o = PS[:N[i], b, 0:D]
                    for c in range(KD):
                        mm(o, xT[:, c, T0[i]:T0[i] + N[i]], w_eff[:, c, :], c == 0, False)
                    mm(o, w_arep[0:ADAPT, 0:N[i]], b_adp[0:ADAPT, :], False, True).then_inc(sem("f3_y"), 1)

        @block.gpsimd
        def _(pool):
            done = [0]

            def link(ins):
                done[0] += 1
                ins.then_inc(sem("pool_chain"), 1)
                pool.wait_ge(sem("pool_chain"), done[0])

            def rstd_of(L):
                pool.wait_ge(sem("norm_var"), NORMS.index(L) + 1)
                nc.gpsimd.tensor_tensor(rstd[:ROWS, :], var[:ROWS, :], bc(const("mhalf")[:ROWS, :], [ROWS, TILES]),
                                        ALU.pow).then_inc(sem("norm_rstd"), 1)

            pool.wait_ge(sem("ld_const"), 16)
            rstd_of("n0")
            pool.wait_ge(sem("ld_adp"), 32)
            link(nc.gpsimd.tensor_scalar(w_arep[0:ADAPT, :], const("one")[0:ADAPT, 0:ROWS], w_acol[0:ADAPT, 0:1], 1.0,
                                    ALU.mult, ALU.mult))
            pool.wait_ge(sem("ld_raw"), 16 * ADAPT)
            eff = w_eff[:, :, :].rearrange("p a b -> p (a b)")
            tmp = w_tmp[:, :, :].rearrange("p a b -> p (a b)")
            link(nc.gpsimd.tensor_scalar(eff, raw[:, 0, :], w_adp[:, 0:1], 1.0, ALU.mult, ALU.mult))
            for a in range(1, ADAPT):
                link(nc.gpsimd.tensor_scalar(tmp, raw[:, a, :], w_adp[:, a:a + 1], 1.0, ALU.mult, ALU.mult))
                ins = nc.gpsimd.tensor_tensor(eff, eff, tmp, ALU.add)
                if a < ADAPT - 1:
                    link(ins)
            ins.then_inc(sem("eff"), 1)
            pool.wait_ge(sem("eff"), 1)
            nc.gpsimd.memset(w_tmp[:, 0, 0:1], 0.0).then_inc(sem("eff"), 1)

            for L in ("n0f", "n1"):
                rstd_of(L)
            if stop >= 3:
                pool.wait_ge(sem("f0_done"), 1)
                for c in range(INNER):
                    last = nc.gpsimd.memset(xpad[:, c, :].rearrange("p (b t) -> p b t", b=BATCH)[:, :, 0:3], 0.0)
                last.then_inc(sem("m_pad"), 1)
                for c in range(INNER):
                    pool.wait_ge(sem("m_xc"), c + 1)
                    nc.gpsimd.tensor_tensor(bx[:, c, :], xc[:, c, :], xc[:, c, :], ALU.mult).then_inc(sem("m_bx"), 1)
                for n in range(4 * INNER + 1):
                    if n < 4 * INNER:
                        pool.wait_ge(sem("m_a"), 4 * (n + 1))
                        sl = a_ring[:, 4 * (n % 2):4 * (n % 2) + 4, :].rearrange("p j (b t) -> p (j b) t", b=BATCH)
                        nc.gpsimd.memset(sl[:, :, 0:1], 0.0).then_inc(sem("m_a0"), 1)
                    if n >= 1:
                        pool.wait_ge(sem("m_hs"), n)
                        k = 4 * ((n - 1) % 3)
                        nc.gpsimd.tensor_tensor(hs_ring[:, k:k + 2, :], hs_ring[:, k:k + 2, :],
                                                hs_ring[:, k + 2:k + 4, :], ALU.add).then_inc(sem("m_pair"), 1)
            if stop >= 4:
                rstd_of("n1f")
                for q in range(2 * E1):
                    pool.wait_ge(sem("w_hi"), q + 1)
                    nc.gpsimd.tensor_tensor(raw1(q, RINGR), raw1(q), as_f32(w1hi[:, q % 4, :]), ALU.subtract)\
                        .then_inc(sem("w_lo"), 1)
                for L in ("n2", "n2b"):
                    rstd_of(L)
            if stop >= 5:
                for u in range(8):
                    j, pp = u // 4, u % 4
                    pool.wait_ge(sem("a2_r"), u + 1)
                    dst = (q2, k2)[j]
                    t = 4 * (u % 2)
                    nc.gpsimd.tensor_tensor(dst[:, 2 * pp, :], rt2[:, t, :], rt2[:, t + 1, :], ALU.subtract)\
                        .then_inc(sem("a2_qk_sb"), 1)
                    nc.gpsimd.tensor_tensor(dst[:, 2 * pp + 1, :], rt2[:, t + 2, :], rt2[:, t + 3, :], ALU.add)\
                        .then_inc(sem("a2_qk_sb"), 1)
                for u in range(UNITS2 + 1):
                    if u < UNITS2:
                        n = N[u // 4]
                        s = four(sm2[:n, u % 3, :], n)
                        pool.wait_ge(sem("u_mx"), u + 1)
                        nc.gpsimd.tensor_tensor(s, s, bc(o2b[u % 3][:n, :].unsqueeze(2), [n, 4, n]), ALU.subtract)\
                            .then_inc(sem("u_e"), 1)
                    if u >= 1:
                        k = u - 1
                        n = N[k // 4]
                        s = four(p2[:n, k % 4, :], n)
                        pool.wait_ge(sem("a2_rc"), k + 1)
                        nc.gpsimd.tensor_tensor(s, s, bc(o2b[3 + k % 2][:n, :].unsqueeze(2), [n, 4, n]), ALU.mult)\
                            .then_inc(sem("a2_pn"), 1)
                rstd_of("n2f")
            if stop >= 6:
                for p in range(3 * E2):
                    pool.wait_ge(sem("w_hi"), 2 * E1 + p + 1)
                    nc.gpsimd.tensor_tensor(raw2(p, RINGR), raw2(p), as_f32(w2hi[:, p % 4, :]), ALU.subtract)\
                        .then_inc(sem("w_lo"), 1)
                rstd_of("n3")
            if stop >= 7:
                pool.wait_ge(sem("a3_qkT"), TILES)
                for m in range(1, MAPS, 3):
                    dst = kx3[:, m, :] if m < 16 else kx3b[:, m - 16, :]
                    nc.gpsimd.tensor_scalar(dst, kT3[:, m // 16, :], const("own")[:, m % 16:m % 16 + 1], 1.0,
                                            ALU.mult, ALU.mult).then_inc(sem("a3_kx"), 1)
                for u in range(8 * TILES):
                    n = N[u // 8]
                    s = sm3[:n, u % 3, :].rearrange("p (a b) -> p a b", a=4)[:, :, 0:n]
                    pool.wait_ge(sem("u_mx"), UNITS2 + u + 1)
                    nc.gpsimd.tensor_tensor(s, s, bc(rt5[:n, 1 + u % 3, 0:4].unsqueeze(2), [n, 4, n]), ALU.subtract)\
                        .then_inc(sem("u_e"), 1)
                rstd_of("n3f")


        @block.scalar
        def _(act):
            A = nc.scalar.activation
            done = [0]

            def link(ins):
                done[0] += 1
                ins.then_inc(sem("act_chain"), 1)
                act.wait_ge(sem("act_chain"), done[0])

            def norm_T(L):
                for i in range(TILES):
                    act.wait_ge(sem("norm_tr"), nth_T(L, i))
                    src = PS[:, i % 2, 0:256].rearrange("p (c n) -> p c n", c=KD)[:, :, 0:N[i]]
                    if L == "n2b":
                        for c in range(KD):
                            ins = A(gT[:, c, T0[i]:T0[i] + N[i]], src[:, c, :], ACT.Identity,
                                    scale=w_ln[:, 0, c:c + 1], bias=w_ln[:, 1, c:c + 1])
                    else:
                        ins = A(xT[:, :, T0[i]:T0[i] + N[i]], src, ACT.Copy)
                    ins.then_inc(sem("norm_xT"), 1)

            act.wait_ge(sem("ld_const"), 16)
            if stop >= 1:
                norm_T("n0")
                for j in (0, 2):
                    act.wait_ge(sem("a0_qk"), j + 1)
                    A(halves(qk0[:, j, :]), both(2 * j), ACT.Copy).then_inc(sem("a0_q_sb"), 1)

                def exp0(i):
                    act.wait_ge(sem("a0_sm"), i + 1)
                    A(p0[:N[i], i, 0:N[i]], sm0[:N[i], i, 0:N[i]], ACT.Exp, scale=0.0625, bias=mx0[:N[i], i:i + 1],
                      accum_out=sum0[:N[i], i:i + 1]).then_inc(sem("a0_p"), 1)

                def pt0_copy(i):
                    act.wait_ge(sem("a0_t"), i + 1)
                    A(pt0[:N[i], i, 0:N[i]], PS[:N[i], i, 128:128 + N[i]], ACT.Copy).then_inc(sem("a0_pt"), 1)

                exp0(0)
                for i in range(1, TILES):
                    exp0(i)
                    pt0_copy(i - 1)
                pt0_copy(TILES - 1)

            if stop >= 2:
                norm_T("n0f")
                act.wait_ge(sem("f0_lg"), 1)
                A(halves(sg)[0:E0], PS[0:E0, 2:4, 0:HALF], ACT.Sigmoid).then_inc(sem("f0_sg"), 1)
                for i in range(TILES):
                    act.wait_ge(sem("f0_g"), i + 1)
                    w = WIDTH[i]
                    for c in range(KD):
                        ins = A(xg[:, c, :].rearrange("p (ke b) -> p ke b", b=BATCH)[:, :, GROUP * i:GROUP * i + w],
                                PS[:, 5 + i % 2, 112 * c:112 * c + 16 * w].rearrange("p (ke b) -> p ke b", b=w), ACT.Copy)
                    A(poh[0:SEQ, :, GROUP * i:GROUP * i + w],
                      PS[0:SEQ, 5 + i % 2, 224:224 + 16 * w].rearrange("p (a b) -> p a b", b=w), ACT.Copy)\
                        .then_inc(sem("f0_xg"), 1)
                for gk in range(4):
                    act.wait_ge(sem("f0_qkv"), gk + 1)
                    A(qkv[:, gk, :], PS[:, gk, 0:450], ACT.Copy).then_inc(sem("f0_qkv_sb"), 1)
                act.wait_ge(sem("f0_qkv_sb"), 4)
                A(rt[:, 0, 0:4], qkv[:, :, 384], ACT.Sigmoid).then_inc(sem("f0_gate"), 1)
                act.wait_ge(sem("f0_e"), 1)
                A(rt[:, 1, 8:16], rt[:, 1, 0:8], ACT.Exp).then_inc(sem("f0_exp"), 1)
                act.wait_ge(sem("f0_avt"), 1)
                A(avt, PS[:, 4, :].rearrange("p (a b) -> p a b", a=4), ACT.Copy).then_inc(sem("f0_avt_sb"), 1)
                for gk in range(4):
                    act.wait_ge(sem("f0_x"), gk + 1)
                    A(xp[:, gk, :], PS[:, gk, 0:D], ACT.Copy).then_inc(sem("f0_xp"), 1)

            if stop >= 3:
                norm_T("n1")
                act.wait_ge(sem("m_pad"), 1)
                act.wait_ge(sem("ld_m"), 48)
                al = m_small[:, :, 6:6 + STATE]
                for m in range(8):
                    b = 2 * (m % 4)
                    act.wait_ge(sem("m_x"), m + 1)
                    if m < INNER:
                        dst = xpad[:, m, :].rearrange("p (s b t) -> p s b t", s=2, t=SEQ + 3)
                        for s in range(2):
                            ins = A(dst[:, s, :, 3:], PS[:, b + s, 0:HALF].rearrange("p (b t) -> p b t", t=SEQ), ACT.Copy)
                        ins.then_inc(sem("m_in"), 1)
                    else:
                        A(halves(sres[:, m - INNER, :]), both(b), ACT.Silu).then_inc(sem("m_in"), 1)
                for c in range(INNER):
                    act.wait_ge(sem("m_conv"), c + 1)
                    A(xc[:, c, :], cv[:, c, :], ACT.Silu, bias=m_small[:, c, 4:5]).then_inc(sem("m_xc"), 1)
                act.wait_ge(sem("m_abs"), 1)
                A(al, al, ACT.Exp)
                link(A(delta, delta, ACT.Exp))
                A(delta, delta, ACT.Ln, bias=1.0).then_inc(sem("m_ln"), 1)
                act.wait_ge(sem("m_delta"), 1)
                for n in range(4 * INNER):
                    c, q = n // 4, n % 4
                    if n >= 2:
                        act.wait_ge(sem("m_hs"), n - 1)
                    for j in range(4):
                        A(a_ring[:, 4 * (n % 2) + j, :], delta[:, c, :], ACT.Exp,
                          scale=al[:, c, 4 * q + j:4 * q + j + 1]).then_inc(sem("m_a"), 1)

            if stop >= 4:
                def high1(q):
                    e, j = q // 2, q % 2
                    act.wait_ge(sem(f"ld_p{q % 4}"), 16 * (q // 4 + 1))
                    if e >= 2:
                        act.wait_ge(sem(("f1_z", "f1_y")[j]), (2 * F1C, TILES)[j] * (e - 1))
                    A(w1hi[:, q % 4, :], raw1(q), ACT.Copy).then_inc(sem("w_hi"), 1)

                act.wait_ge(sem("m_out"), TILES)
                high1(0)
                norm_T("n1f")
                act.wait_ge(sem("ld_f1"), 96)
                act.wait_ge(sem("f1_d"), 1)
                A(rt5[:ROWS, :, 2], rt5[:ROWS, :, 2], ACT.Exp).then_inc(sem("f1_e"), 1)
                for C in range(F1C * E1):
                    e, c = C // F1C, C % F1C
                    if c == 1:
                        high1(2 * e + 1)
                    if c == 2 and e + 1 < E1:
                        high1(2 * e + 2)
                    for s in range(2):
                        u = 2 * C + s
                        act.wait_ge(sem("f1_z"), u + 1)
                        if u >= 3:
                            act.wait_ge(sem("f1_h"), u - 2)
                        A(act_f[:, u % 3, :], PS[:, 2 * (u % 3), 0:HALF], ACT.Relu,
                          bias=w_b1[:, e, c:c + 1]).then_inc(sem("f1_f"), 1)

            if stop >= 5:
                act.wait_ge(sem("ld_f1"), 96)
                norm_T("n2b")
                for j in range(2):
                    act.wait_ge(sem("a2_c"), j + 1)
                    A(halves(cT[:, j, :]), both(2 + 2 * j), ACT.Copy).then_inc(sem("a2_c_sb"), 1)
                for n in range(2 * TILES):
                    i, g = n // 2, n % 2
                    act.wait_ge(sem("a2_v"), n + 1)
                    A(v2[:N[i], i, 512 * g:512 * g + 512], PS[:N[i], n % 8, :], ACT.Copy).then_inc(sem("a2_v_sb"), 1)
                units = 4 * TILES

                def mask2(u):
                    i, g = u // 4, u % 4
                    if u >= 2:
                        act.wait_ge(sem("u_s"), u - 1)
                    A(qm2[:, 8 * (u % 2):8 * (u % 2) + 8, 0:N[i]], q2[:, :, T0[i]:T0[i] + N[i]], ACT.Identity,
                      scale=const("quad")[:, g:g + 1]).then_inc(sem("a2_qm"), 1)

                act.wait_ge(sem("a2_qk_sb"), 16)
                mask2(0)
                mask2(1)

                def exp2(u):
                    i = u // 4
                    act.wait_ge(sem("u_e"), u + 1)
                    if u >= 4:
                        act.wait_ge(sem("u_t"), u - 3)
                    v = lambda b, z: b[:N[i], u % z, :].rearrange("p (a b) -> p a b", a=4)[:, :, 0:N[i]]
                    A(v(p2, 4), v(sm2, 3), ACT.Exp, scale=0.125).then_inc(sem("u_p"), 1)

                def pt2_copy(u):
                    i = u // 4
                    act.wait_ge(sem("u_t"), u + 1)
                    if u >= 2:
                        act.wait_ge(sem("a2_o"), u - 1)
                    A(pt2[:N[i], u % 2, :].rearrange("p (a b) -> p a b", a=4)[:, :, 0:N[i]],
                      PS[:N[i], 2 + u % 2, :].rearrange("p (a b) -> p a b", a=4)[:, :, 0:N[i]], ACT.Copy)\
                        .then_inc(sem("u_pt"), 1)

                def ot2_copy(u):
                    i, g = u // 4, u % 4
                    act.wait_ge(sem("a2_o"), u + 1)
                    if g == 0 and i >= 2:
                        act.wait_ge(sem("a2_out"), i - 1)
                    c = 8 * (i % 2) + 2 * g
                    A(oT2[:, c:c + 2, 0:N[i]],
                      PS[:, 4 + u % 2, 0:256].rearrange("p (a b) -> p a b", a=2)[:, :, 0:N[i]], ACT.Copy).then_inc(sem("a2_ot"), 1)

                for u in range(units + 4):
                    if u < units:
                        exp2(u)
                    if 3 <= u <= units + 2:
                        pt2_copy(u - 3)
                    if 4 <= u:
                        ot2_copy(u - 4)
                    if u + 2 < units:
                        mask2(u + 2)

            if stop >= 6:
                def high2(p):
                    act.wait_ge(sem(f"ld_p{p % 4}"), 16 * ((2 * E1 + p) // 4 + 1))
                    A(w2hi[:, p % 4, :], raw2(p), ACT.Copy).then_inc(sem("w_hi"), 1)

                act.wait_ge(sem("a2_done"), 1)
                high2(0)
                norm_T("n2f")
                high2(1)
                act.wait_ge(sem("f2_d"), 1)
                A(rsc[:ROWS, :, 0:E2], rsc[:ROWS, :, 0:E2], ACT.Exp).then_inc(sem("f2_e"), 1)
                high2(2)
                for e in range(E2):
                    for c in range(F2C):
                        if c == 6 and e + 1 < E2:
                            high2(3 * e + 3)
                        for s in range(2):
                            u = (e * F2C + c) * 2 + s
                            act.wait_ge(sem("f2_z"), u + 1)
                            if u >= 3:
                                act.wait_ge(sem("f2_g"), u - 2)
                            A(sil[:, u % 3, :], PS[:, 2 * (u % 3), 0:HALF], ACT.Silu).then_inc(sem("f2_s"), 1)
                    if e + 1 < E2:
                        high2(3 * e + 4)
                        high2(3 * e + 5)

            if stop >= 7:
                norm_T("n3")
                act.wait_ge(sem("ld_a3"), 96)
                act.wait_ge(sem("a3_lam"), 1)
                A(rt5[:, 0, 2:4], rt5[:, 0, 0:2], ACT.Exp).then_inc(sem("a3_lam_e"), 1)
                act.wait_ge(sem("a3_zero"), 1)
                for i in range(TILES):
                    act.wait_ge(sem("a3_qkv"), i + 1)
                    b = 2 * (i % 3)
                    A(qt3[:N[i], i, :], PS[:N[i], b, 0:256], ACT.Copy)
                    A(kt3[:N[i], i, :], PS[:N[i], b + 1, 0:128], ACT.Copy)
                    A(v3[:N[i], i, :].rearrange("p (a b) -> p a b", b=VP3)[:, :, 0:VD3],
                      PS[:N[i], b + 1, 128:256].rearrange("p (a b) -> p a b", b=VD3), ACT.Copy)\
                        .then_inc(sem("a3_qkv_sb"), 1)
                for i in range(TILES):
                    act.wait_ge(sem("a3_tr"), i + 1)
                    s = PS[:, i % 2, :].rearrange("p (a c b) -> p a c b", a=2, c=2)
                    A(qT3[:, :, T0[i]:T0[i] + N[i]], s[:, 0, :, 0:N[i]], ACT.Copy)
                    A(kT3[:, :, T0[i]:T0[i] + N[i]], s[:, 1, :, 0:N[i]], ACT.Copy).then_inc(sem("a3_qkT"), 1)
                units = 8 * TILES

                def exp3(u):
                    i = u // 8
                    act.wait_ge(sem("u_e"), UNITS2 + u + 1)
                    if u >= 2:
                        act.wait_ge(sem("u_t"), UNITS2 + u - 1)
                    v = lambda b, z: b[:N[i], u % z, :].rearrange("p (a b) -> p a b", a=4)[:, :, 0:N[i]]
                    A(v(p3, 2), v(sm3, 3), ACT.Exp, scale=float(HD3) ** -0.5).then_inc(sem("u_p"), 1)

                def pt3_copy(u):
                    i = u // 8
                    act.wait_ge(sem("u_t"), UNITS2 + u + 1)
                    if u >= 3:
                        act.wait_ge(sem("a3_o"), u - 2)
                    A(pt3[:N[i], u % 3, :].rearrange("p (a b) -> p a b", a=4)[:, :, 0:N[i]],
                      PS[:N[i], 4 + u % 2, :].rearrange("p (a b) -> p a b", a=4)[:, :, 0:N[i]], ACT.Copy)\
                        .then_inc(sem("u_pt"), 1)

                def oT3_copy(n):
                    i = n // 2
                    act.wait_ge(sem("a3_o"), 4 * (n + 1))
                    if n >= 2:
                        act.wait_ge(sem("a3_back"), n - 1)
                    A(four(oT3[:, n % 2, :], N[i]), four(PS[:, 6 + n % 2, 0:4 * ROWS], N[i]), ACT.Copy)\
                        .then_inc(sem("a3_oT"), 1)

                for u in range(units + 4):
                    if u < units:
                        exp3(u)
                    if 2 <= u <= units + 1:
                        pt3_copy(u - 2)
                    if u >= 7 and u % 4 == 3:
                        oT3_copy(u // 4 - 1)
                act.wait_ge(sem("a3_ms"), 1)
                rr, root = [rt3[:ROWS, z, 0:TILES * H3] for z in (0, 2)]
                A(root, rr, ACT.Sqrt, bias=const("eps6")[:ROWS, :], scale=1.0 / VD3).then_inc(sem("a3_rms"), 1)
                for i in range(TILES):
                    act.wait_ge(sem("a3_at_tr"), i + 1)
                    A(atT3[:, :, T0[i]:T0[i] + N[i]],
                      PS[:, i % 2, 0:256].rearrange("p (c n) -> p c n", c=KD)[:, :, 0:N[i]], ACT.Copy)\
                        .then_inc(sem("a3_atT"), 1)
            if stop >= 8:
                norm_T("n3f")

        @block.vector
        def _(dve):
            V = nc.vector
            done = [0]

            def link(ins):
                done[0] += 1
                ins.then_inc(sem("dve_chain"), 1)
                dve.wait_ge(sem("dve_chain"), done[0])

            def norm_stats(L, i, src, ready=None):
                if 1 <= i <= TILES:
                    if ready is not None:
                        dve.wait_ge(sem(ready[0]), ready[1])
                    V.bn_stats(st[:N[i - 1], i - 1, :], src[:N[i - 1], i - 1, :]).then_inc(sem("norm_bn"), 1)
                if i >= 2:
                    dve.wait_ge(sem("norm_bn"), nth(L, i - 2))
                    ins = V.bn_aggr(mv[:N[i - 2], i - 2, :], st[:N[i - 2], i - 2, :])
                    if i == TILES + 1:
                        link(ins)

            def norm(L, src, dst, ready=None):
                norm_stats(L, TILES, src, ready)
                norm_stats(L, TILES + 1, src)
                V.tensor_scalar(var[:ROWS, :], mv[:ROWS, :, 1], 1e-5, None, ALU.add).then_inc(sem("norm_var"), 1)
                dve.wait_ge(sem("norm_rstd"), NORMS.index(L) + 1)
                for i in range(TILES):
                    V.tensor_scalar(dst[:N[i], i, :], src[:N[i], i, :], mv[:N[i], i, 0:1], rstd[:N[i], i:i + 1],
                                    ALU.subtract, ALU.mult).then_inc(sem("norm_xn"), 1)

            def top2(vals, rank, m, r, tmp, v2, sels):
                P, g, n = vals.shape
                for k in range(2):
                    src = vals if k == 0 else v2
                    link(V.tensor_reduce(m[k], src, AX.X, ALU.max))
                    link(V.tensor_tensor(tmp, src, bc(m[k].unsqueeze(2), [P, g, n]), ALU.is_equal))
                    link(V.tensor_tensor(tmp, tmp, bc(rank.unsqueeze(1), [P, g, n]), ALU.mult))
                    link(V.tensor_reduce(r, tmp, AX.X, ALU.max))
                    link(V.tensor_tensor(sels[k], tmp, bc(r.unsqueeze(2), [P, g, n]), ALU.is_equal))
                    if k == 0:
                        link(V.tensor_scalar(tmp, sels[0], -1.0, 1.0, ALU.mult, ALU.add))
                        link(V.tensor_tensor(v2, vals, tmp, ALU.mult))
                        link(V.tensor_tensor(v2, v2, sels[0], ALU.subtract))

            def split_x(L, parts, ready):
                dve.wait_ge(sem("norm_xT"), nth_T(L, TILES - 1))
                link(V.tensor_copy(parts[:, 0:KD, :], xT[:, :, :]))
                V.tensor_tensor(parts[:, KD:2 * KD, :], xT[:, :, :], as_f32(parts[:, 0:KD, :]), ALU.subtract)\
                    .then_inc(sem(ready), 1)

            def split_h(f, hi, lo, ready):
                link(V.tensor_copy(hi, f))
                V.tensor_tensor(lo, f, as_f32(hi), ALU.subtract).then_inc(sem(ready), 1)

            def add_out(ready, freed, banks, L):
                for i in range(TILES):
                    dve.wait_ge(sem(ready), i + 1)
                    V.tensor_tensor(h[:N[i], i, :], PS[:N[i], banks[i], 0:D], h[:N[i], i, :], ALU.add)\
                        .then_inc(sem(freed), 1)
                    norm_stats(L, i, h, (freed, i))
                norm(L, h, xn, (freed, TILES))

            V.memset(mv[:, :, :], 1.0)
            link(V.memset(misc[:, D:900], 0.0))

            for i in range(TILES):
                dve.wait_ge(sem("t_ps"), i + 1)
                V.tensor_copy(h[:N[i], i, :], PS[:N[i], i, 0:D]).then_inc(sem("h_new"), 1)
                norm_stats("n0", i, h, ("h_new", i))
            norm("n0", h, xn, ("h_new", TILES))

            if stop >= 1:
                for j in (1, 3):
                    dve.wait_ge(sem("a0_qk"), j + 1)
                    V.tensor_copy(halves(qk0[:, j, :]), both(2 * j)).then_inc(sem("a0_k_sb"), 1)
                for i in range(TILES):
                    dve.wait_ge(sem("a0_v"), i + 1)
                    V.tensor_copy(v0[:N[i], i, :], PS[:N[i], i, 0:D]).then_inc(sem("a0_v_sb"), 1)
                for i in range(TILES):
                    n = N[i]
                    dve.wait_ge(sem("a0_s"), i + 1)
                    link(V.tensor_tensor(sm0[:n, i, 0:n], PS[:n, i, 0:n], const("causal")[:n, 0:n], ALU.add))
                    link(V.tensor_reduce(mx0[:n, i:i + 1], sm0[:n, i, 0:n], AX.X, ALU.max))
                    V.tensor_scalar(mx0[:n, i:i + 1], mx0[:n, i:i + 1], -0.0625, None, ALU.mult).then_inc(sem("a0_sm"), 1)
                for i in range(TILES):
                    n = N[i]
                    dve.wait_ge(sem("a0_o"), i + 1)
                    link(V.reciprocal(sum0[:n, TILES + i:TILES + i + 1], sum0[:n, i:i + 1]))
                    V.scalar_tensor_tensor(h[:n, i, :], PS[:n, i, 256:512], sum0[:n, TILES + i:TILES + i + 1],
                                           h[:n, i, :], ALU.mult, ALU.add).then_inc(sem("h_new"), 1)
                    norm_stats("n0f", i, h, ("h_new", TILES + i))
                norm("n0f", h, xn, ("h_new", 2 * TILES))

            if stop >= 2:
                dve.wait_ge(sem("f0_sg"), 1)
                three = lambda a: a[0:E0].rearrange("p (b t) -> p b t", t=SEQ)
                top2(three(sg), const("rank17")[0:E0, :], [m8[0:E0, 0, :], m8[0:E0, 1, :]], r8[0:E0, :],
                     three(t8a), three(t8b), [three(sel[:, 0, :]), three(sel[:, 1, :])])
                V.memset(r8[0:E0, 0:1], 0.0).then_inc(sem("f0_sel"), 1)
                dve.wait_ge(sem("f0_selT"), 1)
                for i in range(TILES):
                    n, w = N[i], WIDTH[i]
                    V.tensor_tensor(G[:n, i, 0:16 * w].rearrange("p (a b) -> p a b", b=w),
                                    bc(PS[:n, 4, 16 * i:16 * i + 16].unsqueeze(2), [n, 16, w]),
                                    bc(const("image")[:n, 0:w].unsqueeze(1), [n, 16, w]), ALU.mult)\
                        .then_inc(sem("f0_G"), 1)
                dve.wait_ge(sem("f0_qkv_sb"), 4)
                q4 = qkv[:, :, 0:256].rearrange("p g (j d) -> p g j d", j=2)
                x1, x2 = q4[:, :, :, 0:ROT], q4[:, :, :, ROT:2 * ROT]
                cos = bc(qkv[:, :, 385:385 + ROT].unsqueeze(2), [128, 4, 2, ROT])
                sin = bc(qkv[:, :, 417:417 + ROT].unsqueeze(2), [128, 4, 2, ROT])
                ra, rb, rc, rd = [rt[:, 2 + z, :].rearrange("p (g j d) -> p g j d", g=4, j=2) for z in range(4)]
                V.tensor_tensor(ra, x1, cos, ALU.mult)
                V.tensor_tensor(rb, x2, sin, ALU.mult)
                V.tensor_tensor(rc, x2, cos, ALU.mult)
                link(V.tensor_tensor(rd, x1, sin, ALU.mult))
                V.tensor_tensor(x1, ra, rb, ALU.subtract)
                link(V.tensor_tensor(x2, rc, rd, ALU.add))
                s8 = rt[:, 1, 0:8]
                for g in range(2):
                    gk = slice(2 * g, 2 * g + 2)
                    link(V.tensor_tensor(prod.rearrange("p (k m d) -> p k m d", k=2, m=2),
                                         bc(qkv[:, gk, 0:128].unsqueeze(2), [128, 2, 2, 128]),
                                         bc(qkv[:, gk, 128:256].unsqueeze(1), [128, 2, 2, 128]), ALU.mult))
                    link(V.tensor_reduce(s8[:, 4 * g:4 * g + 4], prod.rearrange("p (a d) -> p a d", a=4),
                                         AX.X, ALU.add))
                pos4 = qkv[:, :, 449].rearrange("p (g k) -> p g k", g=2)
                al = rt[:, 1, 16:24].rearrange("p (g k m) -> p g k m", g=2, k=2)
                link(V.tensor_tensor(al, bc(pos4.unsqueeze(3), [128, 2, 2, 2]), bc(pos4.unsqueeze(2), [128, 2, 2, 2]),
                                     ALU.is_ge))
                link(V.tensor_scalar(rt[:, 1, 16:24], rt[:, 1, 16:24], -MASKED, MASKED, ALU.mult, ALU.add))
                link(V.scalar_tensor_tensor(s8, s8, float(HP) ** -0.5, rt[:, 1, 16:24], ALU.mult, ALU.add))
                s42 = s8.rearrange("p (a m) -> p a m", m=2)
                mx = rt[:, 1, 24:28]
                link(V.tensor_reduce(mx, s42, AX.X, ALU.max))
                V.tensor_tensor(s42, s42, bc(mx.unsqueeze(2), [128, 4, 2]), ALU.subtract).then_inc(sem("f0_e"), 1)
                dve.wait_ge(sem("f0_exp"), 1)
                e42 = rt[:, 1, 8:16].rearrange("p (a m) -> p a m", m=2)
                link(V.tensor_reduce(rt[:, 1, 28:32], e42, AX.X, ALU.add))
                link(V.reciprocal(rt[:, 1, 28:32], rt[:, 1, 28:32]))
                dve.wait_ge(sem("f0_gate"), 1)
                link(V.tensor_tensor(rt[:, 1, 28:32], rt[:, 1, 28:32], rt[:, 0, 0:4], ALU.mult))
                link(V.tensor_tensor(e42, e42, bc(rt[:, 1, 28:32].unsqueeze(2), [128, 4, 2]), ALU.mult))
                for gk in range(4):
                    V.tensor_scalar(av[:, gk, :], qkv[:, 2 * (gk // 2), 256:384], rt[:, 1, 8 + 2 * gk:9 + 2 * gk], None, ALU.mult)
                link(V.memset(rt[:, 0, 8:9], 0.0))
                for gk in range(4):
                    ins = V.scalar_tensor_tensor(av[:, gk, :], qkv[:, 2 * (gk // 2) + 1, 256:384],
                                                 rt[:, 1, 9 + 2 * gk:10 + 2 * gk], av[:, gk, :], ALU.mult, ALU.add)
                ins.then_inc(sem("f0_av"), 1)
                link(V.tensor_scalar(rt[:, 0, 4:8], qkv[:, :, 449], const("first"), None, ALU.add))
                for gk in range(4):
                    V.tensor_scalar(GT[:, gk, :], const("token"), rt[:, 0, 4 + gk:5 + gk], None, ALU.is_equal)\
                        .then_inc(sem("f0_GT"), 1)
                add_out("f0_out", "f0_h", [5 + i % 3 for i in range(TILES)], "n1")
                V.memset(flag[:, 0:1], 0.0).then_inc(sem("f0_done"), 1)

            if stop >= 3:
                dve.wait_ge(sem("ld_m"), 48)
                al = m_small[:, :, 6:6 + STATE]
                link(V.tensor_scalar(al, al, 80.0, None, ALU.min))
                for c in range(INNER):
                    dve.wait_ge(sem("m_in"), c + 1)
                    xp_c = xpad[:, c, :].rearrange("p (b t) -> p b t", b=BATCH)
                    o = cv[:, c, :].rearrange("p (b t) -> p b t", b=BATCH)
                    link(V.tensor_scalar(o, xp_c[:, :, 0:SEQ], m_small[:, c, 0:1], None, ALU.mult))
                    for k in range(1, 4):
                        ins = V.scalar_tensor_tensor(o, xp_c[:, :, k:k + SEQ], m_small[:, c, k:k + 1], o,
                                                     ALU.mult, ALU.add)
                        if k < 3:
                            link(ins)
                    ins.then_inc(sem("m_conv"), 1)
                for c in range(INNER):
                    dve.wait_ge(sem("m_xc"), c + 1)
                    ins = V.scalar_tensor_tensor(delta[:, c, :], xc[:, c, :], -1.0, xc[:, c, :], ALU.mult, ALU.min)
                ins.then_inc(sem("m_abs"), 1)
                dve.wait_ge(sem("m_ln"), 1)
                link(V.tensor_scalar(al, al, -1.0, None, ALU.mult))
                V.scalar_tensor_tensor(delta, xc, 0.0, delta, ALU.max, ALU.add).then_inc(sem("m_delta"), 1)

                def gate_y(c):
                    b = 2 * (c % 2)
                    dve.wait_ge(sem("m_sum"), 4 * (c + 1))
                    V.tensor_tensor(halves(cv[:, c, :]), both(b), halves(xc[:, c, :]), ALU.mult).then_inc(sem("m_t1"), 1)
                    dve.wait_ge(sem("m_t1"), c + 1)
                    link(V.tensor_tensor(cv[:, c, :], cv[:, c, :], sres[:, c, :], ALU.mult))
                    V.scalar_tensor_tensor(cv[:, c, :], xc[:, c, :], m_small[:, c, 5:6], cv[:, c, :],
                                           ALU.mult, ALU.add).then_inc(sem("m_y"), 1)

                dve.wait_ge(sem("m_bx"), INNER)
                dve.wait_ge(sem("m_in"), 8)
                for n in range(4 * INNER):
                    c = n // 4
                    dve.wait_ge(sem("m_a0"), n + 1)
                    if n >= 3:
                        dve.wait_ge(sem("m_sum"), n - 2)
                    for j in range(4):
                        ins = V.tensor_tensor_scan(hs_ring[:, 4 * (n % 3) + j, :], a_ring[:, 4 * (n % 2) + j, :],
                                                   bx[:, c, :], 0.0, ALU.mult, ALU.add)
                    ins.then_inc(sem("m_hs"), 1)
                    if n % 4 == 1 and c >= 1:
                        gate_y(c - 1)
                gate_y(INNER - 1)
                add_out("m_out", "m_h", [4 + i % 4 for i in range(TILES)], "n1f")

            if stop >= 4:
                R = slice(0, ROWS)
                split_x("n1f", xs1, "f1_x")
                dve.wait_ge(sem("f1_sc"), 1)
                for i in range(TILES):
                    ins = V.tensor_scalar(rsc[:N[i], i, :], PS[:N[i], 6, 8 * i:8 * i + 8], 0.0, None, ALU.max)
                ins.then_inc(sem("f1_rs"), 1)
                dve.wait_ge(sem("f1_rs"), 1)
                sels = [rsel[R, 0:TILES, :], rsel[R, TILES:2 * TILES, :]]
                m = [rt5[R, :, 0], rt5[R, :, 1]]
                top2(rsc[R], const("rank8")[R, :], m, rt5[R, :, 3], rtmp[R], rv2[R], sels)
                V.tensor_tensor(rt5[R, :, 2], m[1], m[0], ALU.subtract).then_inc(sem("f1_d"), 1)
                dve.wait_ge(sem("f1_e"), 1)
                link(V.tensor_scalar(rt5[R, :, 4], rt5[R, :, 2], 1.0, None, ALU.add))
                link(V.reciprocal(rt5[R, :, 4], rt5[R, :, 4]))
                link(V.tensor_tensor(rt5[R, :, 5], rt5[R, :, 2], rt5[R, :, 4], ALU.mult))
                w3d = lambda a: bc(a.unsqueeze(2), [ROWS, TILES, 8])
                link(V.tensor_tensor(rtmp[R], sels[0], w3d(rt5[R, :, 4]), ALU.mult))
                link(V.tensor_tensor(rv2[R], sels[1], w3d(rt5[R, :, 5]), ALU.mult))
                V.tensor_tensor(rw[R], rtmp[R], rv2[R], ALU.add).then_inc(sem("f1_rw"), 1)
                def split1(C):
                    if C >= SLOTS:
                        dve.wait_ge(sem("f1_y"), TILES * ((C - SLOTS) // F1C + 1))
                    for s in range(2):
                        u = 2 * C + s
                        dve.wait_ge(sem("f1_f"), u + 1)
                        split_h(act_f[:, u % 3, :], half(h1[:, 2 * (C % SLOTS) + HI, :], s),
                                half(h1[:, 2 * (C % SLOTS) + LO, :], s), "f1_h")

                def acc1(e):
                    for i in range(TILES):
                        n = e * TILES + i
                        dve.wait_ge(sem("f1_y"), n + 1)
                        if e >= 1 and i == 0:
                            dve.wait_ge(sem("f1_acc"), n)
                        V.scalar_tensor_tensor(h[:N[i], i, :], PS[:N[i], 6 + n % 2, 0:D], rw[:N[i], i, e:e + 1],
                                               h[:N[i], i, :], ALU.mult, ALU.add).then_inc(sem("f1_acc"), 1)
                        if e == E1 - 1:
                            norm_stats("n2", i, h, ("f1_acc", n))

                def bias1():
                    for i in range(TILES):
                        dve.wait_ge(sem("f1_rwT"), TILES)
                        V.tensor_copy(rwT[0:E1, T0[i]:T0[i] + N[i]],
                                      PS[0:E1, 1 if i < 4 else 3, 128 * (i % 4):128 * (i % 4) + N[i]]).then_inc(sem("f1_rwT_sb"), 1)
                    for i in range(TILES):
                        dve.wait_ge(sem("f1_bias"), i + 1)
                        V.tensor_tensor(h[:N[i], i, :], PS[:N[i], (1, 3, 5)[i % 3], 0:D], h[:N[i], i, :], ALU.add)\
                            .then_inc(sem("f1_bh"), 1)
                    dve.wait_ge(sem("f1_bh"), TILES)

                for C in range(F1C * E1):
                    split1(C)
                    if C == F1C + AHEAD - 1:
                        bias1()
                    if C >= F1C + AHEAD - 1 and (C - AHEAD) % F1C == F1C - 1:
                        acc1((C - AHEAD) // F1C)
                acc1(E1 - 1)
                norm("n2", h, xn, ("f1_acc", E1 * TILES))

            if stop >= 5:
                dve.wait_ge(sem("norm_xn"), nth("n2", TILES - 1))
                for i in range(TILES):
                    norm_stats("n2b", i, xn)
                norm("n2b", xn, yn)
                for i in range(TILES):
                    ins = V.tensor_tensor(h[:N[i], i, :], h[:N[i], i, :], xn[:N[i], i, :], ALU.add)
                link(ins)
                cos = bc(const("cos2").unsqueeze(1), [128, 16, SEQ])
                sin = bc(const("sin2").unsqueeze(1), [128, 16, SEQ])
                for u in range(8):
                    b = 4 * (u % 2)
                    t = 4 * (u % 2)
                    dve.wait_ge(sem("a2_eo"), u + 1)
                    if u >= 2:
                        dve.wait_ge(sem("a2_qk_sb"), 2 * (u - 1))
                    for z, (eo, tab) in enumerate(((0, cos), (1, sin), (0, sin), (1, cos))):
                        for s in range(2):
                            ins = V.tensor_tensor(half(rt2[:, t + z, :], s).rearrange("p (b t) -> p b t", t=SEQ),
                                                  PS[:, b + 2 * eo + s, 0:HALF].rearrange("p (b t) -> p b t", t=SEQ),
                                                  tab, ALU.mult)
                    ins.then_inc(sem("a2_r"), 1)
                units = 4 * TILES

                def soft2(u):
                    i = u // 4
                    n = N[i]
                    dve.wait_ge(sem("u_s"), u + 1)
                    if u >= 3:
                        dve.wait_ge(sem("u_p"), u - 2)
                    if u == 0:
                        dve.wait_ge(sem("a2_qk_sb"), 16)
                    s = sm2[:n, u % 3, :].rearrange("p (a b) -> p a b", a=4)[:, :, 0:n]
                    V.tensor_tensor(s, PS[:n, (0, 1, 6)[u % 3], 0:4 * ROWS].rearrange("p (a b) -> p a b", a=4)[:, :, 0:n],
                                    bc(const("block")[:n, 0:n].unsqueeze(1), [n, 4, n]), ALU.add).then_inc(sem("u_sm"), 1)
                    dve.wait_ge(sem("u_sm"), u + 1)
                    V.tensor_reduce(o2b[u % 3][:n, :], s, AX.X, ALU.max).then_inc(sem("u_mx"), 1)

                def sum2(u):
                    i = u // 4
                    dve.wait_ge(sem("u_p"), u + 1)
                    if u >= 2:
                        dve.wait_ge(sem("a2_pn"), u - 1)
                    r = o2b[3 + u % 2][:N[i], :]
                    link(V.tensor_reduce(r, four(p2[:N[i], u % 4, :], N[i]), AX.X, ALU.add))
                    V.reciprocal(r, r).then_inc(sem("a2_rc"), 1)

                def out2(i):
                    dve.wait_ge(sem("a2_out"), i + 1)
                    V.tensor_tensor(h[:N[i], i, :], PS[:N[i], 7, 0:D], h[:N[i], i, :], ALU.add).then_inc(sem("a2_h"), 1)
                    norm_stats("n2f", i, h, ("a2_h", i))

                for u in range(units + 5):
                    if u < units:
                        soft2(u)
                    if 1 <= u <= units:
                        sum2(u - 1)
                    if u >= 8 and u % 4 == 0:
                        out2(u // 4 - 2)
                dve.wait_ge(sem("a2_h"), TILES)
                V.memset(flag[:, 1:2], 0.0).then_inc(sem("a2_done"), 1)
                norm("n2f", h, xn)

            if stop >= 6:
                R = slice(0, ROWS)
                split_x("n2f", xs2, "f2_x")
                lg = rsc[R, :, 0:E2]
                w3d = lambda a: bc(a.unsqueeze(2), [ROWS, TILES, E2])
                dve.wait_ge(sem("f2_sc"), 1)
                for i in range(TILES):
                    ins = V.tensor_copy(rsc[:N[i], i, 0:E2], PS[:N[i], 6, 8 * i:8 * i + E2])
                ins.then_inc(sem("f2_rs"), 1)
                dve.wait_ge(sem("f2_rs"), 1)
                link(V.tensor_reduce(rt5[R, :, 0], lg, AX.X, ALU.max))
                V.tensor_tensor(lg, lg, w3d(rt5[R, :, 0]), ALU.subtract).then_inc(sem("f2_d"), 1)
                dve.wait_ge(sem("f2_e"), 1)
                link(V.tensor_reduce(rt5[R, :, 1], lg, AX.X, ALU.add))
                link(V.reciprocal(rt5[R, :, 1], rt5[R, :, 1]))
                link(V.tensor_tensor(lg, lg, w3d(rt5[R, :, 1]), ALU.mult))
                sels = [rsel[R, 0:TILES, 0:E2], rsel[R, TILES:2 * TILES, 0:E2]]
                m = [rt5[R, :, 0], rt5[R, :, 1]]
                top2(lg, const("rank8")[R, 0:E2], m, rt5[R, :, 3], rtmp[R, :, 0:E2], rv2[R, :, 0:E2], sels)
                link(V.tensor_tensor(rt5[R, :, 4], m[0], m[1], ALU.add))
                link(V.reciprocal(rt5[R, :, 4], rt5[R, :, 4]))
                link(V.tensor_tensor(rt5[R, :, 5], m[0], rt5[R, :, 4], ALU.mult))
                link(V.tensor_tensor(rt5[R, :, 6], m[1], rt5[R, :, 4], ALU.mult))
                link(V.tensor_tensor(rtmp[R, :, 0:E2], sels[0], w3d(rt5[R, :, 5]), ALU.mult))
                link(V.tensor_tensor(rv2[R, :, 0:E2], sels[1], w3d(rt5[R, :, 6]), ALU.mult))
                link(V.tensor_tensor(rw[R, :, 0:E2], rtmp[R, :, 0:E2], rv2[R, :, 0:E2], ALU.add))

                def prod2(e):
                    if e >= 1:
                        dve.wait_ge(sem("f2_y"), TILES * e)
                    for c in range(F2C):
                        for s in range(2):
                            u = (e * F2C + c) * 2 + s
                            dve.wait_ge(sem("f2_s"), u + 1)
                            V.tensor_tensor(act_f[:, u % 3, :], sil[:, u % 3, :], PS[:, 2 * (u % 3) + 1, 0:HALF],
                                            ALU.mult).then_inc(sem("f2_g"), 1)
                            dve.wait_ge(sem("f2_g"), u + 1)
                            split_h(act_f[:, u % 3, :], half(h2[:, 2 * c + HI, :], s),
                                    half(h2[:, 2 * c + LO, :], s), "f2_h")

                def acc2(e):
                    for i in range(TILES):
                        n = e * TILES + i
                        dve.wait_ge(sem("f2_y"), n + 1)
                        V.scalar_tensor_tensor(h[:N[i], i, :], PS[:N[i], 6 + n % 2, 0:D], rw[:N[i], i, e:e + 1],
                                               h[:N[i], i, :], ALU.mult, ALU.add).then_inc(sem("f2_acc"), 1)
                        if e == E2 - 1:
                            norm_stats("n3", i, h, ("f2_acc", n))
                    dve.wait_ge(sem("f2_acc"), TILES * (e + 1))

                for e in range(E2):
                    prod2(e)
                    acc2(e)
                norm("n3", h, xn)

            if stop >= 7:
                dve.wait_ge(sem("ld_a3"), 96)
                lt = rt5[:, 0, :]
                link(V.tensor_tensor(w_lam[:, 0:3:2, :], w_lam[:, 0:3:2, :], w_lam[:, 1:4:2, :], ALU.mult))
                V.tensor_reduce(lt[:, 0:2], w_lam[:, 0:3:2, :], AX.X, ALU.add).then_inc(sem("a3_lam"), 1)
                dve.wait_ge(sem("a3_lam_e"), 1)
                link(V.tensor_tensor(lt[:, 4:5], lt[:, 2:3], lt[:, 3:4], ALU.subtract))
                link(V.tensor_scalar(lt[:, 4:5], lt[:, 4:5], LAMBDA_INIT, None, ALU.add))
                V.memset(v3.rearrange("p i (a b) -> p (i a) b", b=VP3)[:, :, VD3:VP3], 1.0)
                V.memset(qt3[64:128, TILES - 1, :], 0.0)
                V.memset(kt3[64:128, TILES - 1, :], 0.0)
                V.memset(o3[64:128, TILES - 1, :], 1.0).then_inc(sem("a3_zero"), 1)
                dve.wait_ge(sem("a3_zero"), 1)
                dve.wait_ge(sem("a3_qkv_sb"), TILES)
                HR = HD3 // 2
                for src, dst, n, rep in ((qt3, qt3, 32, 1), (kt3, kr3, 16, 2)):
                    G3 = TILES * n
                    flat = src.rearrange("p i (m d) -> p (i m) d", d=HD3)[:ROWS]
                    x1, x2 = flat[:, :, 0:HR], flat[:, :, HR:HD3]
                    cos = bc(const("cos3")[:ROWS].unsqueeze(1), [ROWS, G3, HR])
                    sin = bc(const("sin3")[:ROWS].unsqueeze(1), [ROWS, G3, HR])
                    t = [rt3[:ROWS, z, 0:G3 * HR].rearrange("p (m d) -> p m d", d=HR) for z in range(4)]
                    V.tensor_tensor(t[0], x1, cos, ALU.mult)
                    V.tensor_tensor(t[1], x2, sin, ALU.mult)
                    V.tensor_tensor(t[2], x2, cos, ALU.mult)
                    link(V.tensor_tensor(t[3], x1, sin, ALU.mult))
                    if rep == 1:
                        V.tensor_tensor(x1, t[0], t[1], ALU.add)
                        link(V.tensor_tensor(x2, t[2], t[3], ALU.subtract))
                    else:
                        for r in range(rep):
                            o = dst.rearrange("p i (v r w) -> p (i v) r w", r=2, w=2 * HD3)[:ROWS, :, r, :]\
                                .rearrange("p v (w d) -> p v w d", w=2)
                            tt = [z.rearrange("p (v w) d -> p v w d", w=2) for z in t]
                            V.tensor_tensor(o[:, :, :, 0:HR], tt[0], tt[1], ALU.add)
                            ins = V.tensor_tensor(o[:, :, :, HR:HD3], tt[2], tt[3], ALU.subtract)
                        ins.then_inc(sem("a3_rope"), 1)
                dve.wait_ge(sem("a3_qkT"), TILES)
                for m in range(MAPS):
                    if m % 3 == 1:
                        continue
                    dst = kx3[:, m, :] if m < 16 else kx3b[:, m - 16, :]
                    V.tensor_scalar(dst, kT3[:, m // 16, :], const("own")[:, m % 16:m % 16 + 1], None, ALU.mult)\
                        .then_inc(sem("a3_kx"), 1)
                units = 8 * TILES

                def o3_copy(k):
                    i, G = k // 2, k % 2
                    w = 16 * (VD3 + 1)
                    dve.wait_ge(sem("a3_back"), k + 1)
                    V.tensor_copy(o3[:N[i], i, w * G:w * G + w].rearrange("p (q m d) -> p m q d", q=4, m=4),
                                  PS[:N[i], 0, :].rearrange("p (m q d) -> p m q d", m=4, q=4)[:, :, :, 0:VD3 + 1])\
                        .then_inc(sem("a3_o_sb"), 1)

                for u in range(units):
                    if u >= 10 and u % 4 == 2:
                        o3_copy(u // 4 - 2)
                    n = N[u // 8]
                    dve.wait_ge(sem("u_s"), UNITS2 + u + 1)
                    if u >= 3:
                        dve.wait_ge(sem("u_p"), UNITS2 + u - 2)
                    s = sm3[:n, u % 3, :].rearrange("p (a b) -> p a b", a=4)[:, :, 0:n]
                    V.tensor_tensor(s, PS[:n, 1 + u % 3, 0:4 * ROWS].rearrange("p (a b) -> p a b", a=4)[:, :, 0:n],
                                    bc(const("causal")[:n, 0:n].unsqueeze(1), [n, 4, n]), ALU.add).then_inc(sem("u_sm"), 1)
                    dve.wait_ge(sem("u_sm"), UNITS2 + u + 1)
                    V.tensor_reduce(rt5[:n, 1 + u % 3, 0:4], s, AX.X, ALU.max).then_inc(sem("u_mx"), 1)
                for k in range(units // 4 - 2, units // 4):
                    o3_copy(k)
                dve.wait_ge(sem("a3_o_sb"), units // 4)
                M5 = TILES * H3
                W1 = VD3 + 1
                ov = o3.rearrange("p i (m d) -> p (i m) d", d=W1)[:ROWS]
                rs = rt3[:ROWS, 0, 0:2 * M5]
                link(V.reciprocal(rs, ov[:, :, VD3]))
                rs2 = rs.rearrange("p (m w) -> p m w", w=2)
                link(V.tensor_scalar(rs2[:, :, 1], rs2[:, :, 1], lt[:ROWS, 4:5], None, ALU.mult))
                link(V.tensor_tensor(ov[:, :, 0:VD3], ov[:, :, 0:VD3], bc(rs.unsqueeze(2), [ROWS, 2 * M5, VD3]), ALU.mult))
                o4 = o3.rearrange("p i (m w d) -> p (i m) w d", w=2, d=W1)[:ROWS]
                a3 = at3.rearrange("p i (m d) -> p (i m) d", d=VD3)[:ROWS]
                s3 = sq3.rearrange("p i (m d) -> p (i m) d", d=VD3)[:ROWS]
                link(V.tensor_tensor(a3, o4[:, :, 0, 0:VD3], o4[:, :, 1, 0:VD3], ALU.subtract))
                rr, big, fac = [rt3[:ROWS, z, 0:M5] for z in range(3)]
                link(V.tensor_reduce(big, a3, AX.X, ALU.max, apply_absolute_value=True))
                link(V.tensor_scalar(big, big, 2.0 ** 60, None, ALU.is_gt))
                link(V.tensor_scalar(fac, big, 2.0 ** -40 - 1.0, 1.0, ALU.mult, ALU.add))
                link(V.tensor_scalar(fac, fac, 2.0 ** -40, None, ALU.max))
                link(V.tensor_tensor(a3, a3, bc(fac.unsqueeze(2), [ROWS, M5, VD3]), ALU.mult))
                link(V.tensor_scalar(a3, a3, 2.0 ** 60, -(2.0 ** 60), ALU.min, ALU.max))
                link(V.tensor_tensor(s3, a3, a3, ALU.mult))
                V.tensor_reduce(rr, s3, AX.X, ALU.add).then_inc(sem("a3_ms"), 1)
                dve.wait_ge(sem("a3_ms"), 1)
                link(V.scalar_tensor_tensor(big, rr, 2.0 ** 48, big, ALU.is_ge, ALU.mult))
                link(V.tensor_scalar(big, big, LAMBDA_INIT - 1.0, 1.0 - LAMBDA_INIT, ALU.mult, ALU.add))
                dve.wait_ge(sem("a3_rms"), 1)
                link(V.reciprocal(rr, fac))
                link(V.tensor_tensor(rr, rr, big, ALU.mult))
                link(V.tensor_tensor(a3, a3, bc(rr.unsqueeze(2), [ROWS, M5, VD3]), ALU.mult))
                V.tensor_tensor(a3, a3, bc(w_rms[:ROWS].unsqueeze(1), [ROWS, M5, VD3]), ALU.mult).then_inc(sem("a3_at"), 1)
                add_out("a3_out", "a3_h", [2 + i % 2 for i in range(TILES)], "n3f")

            if stop >= 8:
                for i in range(TILES):
                    dve.wait_ge(sem("f3_y"), i + 1)
                    V.tensor_tensor(h[:N[i], i, :], PS[:N[i], 2 + i, 0:D], h[:N[i], i, :], ALU.add).then_inc(sem("done"), 1)
            else:
                for i in range(TILES):
                    V.memset(flag[:, 2 + i:3 + i], 0.0).then_inc(sem("done"), 1)


def arrange(x):
    c = np.ascontiguousarray
    g = {}
    g["consts"] = constants()[1]
    p = np.asarray(x["x"]).reshape(BATCH, 3, 4, 16, 4, 16).transpose(1, 3, 5, 0, 2, 4).reshape(PK, 128, BATCH, 16)
    p = np.concatenate([np.zeros((PK, 128, BATCH, 1), np.float32), p], 3)
    g["patches"] = p.reshape(PK, 128, TOK).transpose(1, 0, 2)

    def rows(w, k):
        w = np.asarray(w)
        return w.reshape(k, 128, w.shape[1]).transpose(1, 0, 2)

    g["w_tok"] = rows(np.asarray(x["L0_tok_W"]).T, PK)
    bias = np.broadcast_to(np.asarray(x["L0_tok_b"])[None], (SEQ - 1, D))
    g["pos"] = np.concatenate([np.asarray(x["cls_tok"]).reshape(1, D), np.asarray(x["L0_tok_pos_emb"]),
                               np.zeros((1, D), np.float32), bias], 0)
    g["w_qkv0"] = np.stack([rows(x[f"L0_attn_W_{k}"], KD) for k in "qkv"], 1)
    g["w_r0"] = rows(np.asarray(x["L0_ffn_Wr"]).T, KD)
    cat = np.concatenate([np.asarray(x["L0_ffn_Wqkv"]), np.asarray(x["L0_ffn_Wr"])[:, :, None]], 2)
    g["w_cat"] = cat.reshape(E0, KD, 128, QKVW).transpose(2, 1, 0, 3)
    g["w_o0"] = np.asarray(x["L0_ffn_Wo"]).transpose(1, 0, 2)
    g["w_in"] = rows(np.asarray(x["L1_attn_W_in"]).T, KD)
    g["w_out"] = rows(np.asarray(x["L1_attn_W_out"]).T, INNER)
    chan = lambda a, n: np.asarray(a).reshape(INNER, 128, n).transpose(1, 0, 2)
    g["m_small"] = np.concatenate([chan(x["L1_attn_conv_w"], 4), chan(x["L1_attn_conv_b"], 1), chan(x["L1_attn_D"], 1),
                                   chan(x["L1_attn_A_log"], STATE)], 2)
    g["w_r1"] = rows(x["L1_ffn_Wr"], KD)
    g["w_br"] = np.asarray(x["L1_ffn_br"])[None]
    g["w_b1"] = np.asarray(x["L1_ffn_b1"]).reshape(E1, F1C, 128).transpose(2, 0, 1)
    g["w_b2"] = np.asarray(x["L1_ffn_b2"])
    g["w1_1"] = np.asarray(x["L1_ffn_W1"]).reshape(E1, KD, 128, F1C * 128).transpose(0, 2, 1, 3).reshape(E1, 128, -1)
    g["w2_1"] = np.asarray(x["L1_ffn_W2"]).reshape(E1, F1C, 128, D).transpose(0, 2, 1, 3).reshape(E1, 128, -1)
    g["w_ln"] = np.stack([np.asarray(x["L2_attn_ln_scale"]).reshape(KD, 128).T,
                          np.asarray(x["L2_attn_ln_bias"]).reshape(KD, 128).T], 1)
    g["w_dq"] = rows(np.asarray(x["L2_attn_w_down_q"]).T, KD)
    g["w_dkv"] = rows(np.asarray(x["L2_attn_w_down_kv"]).T, KD)

    def pairs(w):
        w = np.asarray(w).reshape(4, 4, 32, 2, 128).transpose(4, 0, 3, 1, 2)
        return w.reshape(128, 8, 128)

    g["w_uq"] = pairs(x["L2_attn_w_up_q"])
    g["w_uk"] = pairs(x["L2_attn_w_up_k"])
    g["w_uv"] = np.asarray(x["L2_attn_w_up_v"]).reshape(4, 4, DH2, 128).transpose(3, 1, 0, 2).reshape(128, 1024)
    g["w_o2"] = rows(np.asarray(x["L2_attn_w_out"]).T.reshape(4, 4, DH2, D).transpose(1, 0, 2, 3).reshape(1024, D), 8)
    g["w_gate"] = rows(np.asarray(x["L2_ffn_gate_w"])[:E2].T, KD)
    for n, k in (("w1", KD), ("w3", KD), ("w2", F2C)):
        w = np.asarray(x[f"L2_ffn_{n}"])[:E2]
        g[n + "_2"] = w.reshape(E2, k, 128, w.shape[2]).transpose(0, 2, 1, 3).reshape(E2, 128, -1)
    g["w_q3"] = rows(x["L3_attn_Wq"], KD)
    g["w_k3"] = rows(x["L3_attn_Wk"], KD)
    g["w_v3"] = rows(x["L3_attn_Wv"], KD)
    g["w_o3"] = rows(x["L3_attn_Wo"], KD)
    lam = np.stack([np.asarray(x["L3_attn_lambda_" + k]) for k in ("q1", "k1", "q2", "k2")])
    g["w_lam"] = np.broadcast_to(lam[None], (128, 4, HD3))
    g["w_rms"] = np.broadcast_to(np.asarray(x["L3_attn_rms_w"])[None], (128, VD3))
    g["ids"] = np.asarray(x["L3_ffn_ids"])[None]
    g["w_adp"] = np.broadcast_to(np.asarray(x["L3_ffn_weights"])[None], (128, ADAPT))
    g["w_acol"] = np.asarray(x["L3_ffn_weights"])[:, None]
    w = np.asarray(x["L3_ffn_W"])
    g["w_all"] = w.transpose(0, 2, 1).reshape(w.shape[0], KD, 128, D).transpose(0, 2, 1, 3).reshape(w.shape[0], 128, -1)
    g["b_all"] = np.asarray(x["L3_ffn_b"])
    return {k: c(v) for k, v in g.items()}


def kernel(**inputs):
    import concourse.bacc as bacc
    from concourse.bass_utils import run_bass_kernel_spmd

    nc = bacc.Bacc("TRN2", target_bir_lowering=False, num_devices=1)
    arrays = arrange(inputs)
    dram = {n: nc.dram_tensor(n + "_dram", a.shape, mybir.dt.from_np(a.dtype), kind="ExternalInput").ap()
            for n, a in arrays.items()}
    out = nc.dram_tensor("out", (TOK, D), F32, kind="ExternalOutput").ap()
    build(nc, dram, out)
    r = run_bass_kernel_spmd(nc, [{n + "_dram": a for n, a in arrays.items()}], core_ids=[0])
    return r.results[0]["out"].reshape(BATCH, SEQ, D)
```
